# Optimizing a Trainium2 kernel written in Bass

```python
import numpy as np
import jax
import jax.numpy as jnp

def _softmax(x, axis=-1):
    return jax.nn.softmax(x, axis=axis)

def _gelu(x):
    return jax.nn.gelu(x, approximate=True)

def _silu(x):
    return jax.nn.silu(x)

def _sigmoid(x):
    return jax.nn.sigmoid(x)

def _layernorm(x, axis=-1, eps=1e-05):
    m = jnp.mean(x, axis=axis, keepdims=True)
    v = jnp.var(x, axis=axis, keepdims=True)
    return (x - m) / jnp.sqrt(v + eps)

def _scatter_add(tgt, idx, src, axis=0):
    return tgt.at[idx].add(src)

def _segment_sum(src, seg, n):
    return jax.ops.segment_sum(src, seg, n)
kernel_name = 'mk_early_fusion_embed_d2_tok_img768_r4_498b77'

def setup_inputs(seed: int=0):
    np.random.seed(seed)
    _w = jnp.asarray

    def _rec_inputs():
        import jax
        import jax.numpy as jnp
        _rk = jax.random.key(seed)
        x = -0.000137204 + 0.999937 * jax.random.normal(jax.random.fold_in(_rk, 1), (32, 3, 128, 128), jnp.float32)
        x_txt = jax.random.randint(jax.random.fold_in(_rk, 51), (32, 128), 0, 31999, jnp.int32)
        mask_BS_i2_0 = jnp.where(jnp.ones((32, 128), dtype=bool), 2, 0).astype(jnp.int32)
        return (x, x_txt, mask_BS_i2_0)
    x, x_txt, mask_BS_i2_0 = _rec_inputs()

    def _L0_tok_setup():
        import jax, jax.numpy as jnp
        import numpy as np
        B, C, H, W_IMG = (128, 3, 224, 224)
        N_PATCH, EMBED = (256, 192)
        GRID = 32
        key = jax.random.key(seed)
        k1, k2, k3, k4 = jax.random.split(key, 4)
        x = jax.random.normal(k1, (B, C, H, W_IMG), dtype=jnp.float32)
        curve = jax.random.randint(k2, (N_PATCH, 2), 0, GRID, dtype=jnp.int32)
        proj_w = jax.random.normal(k3, (EMBED, C), dtype=jnp.float32) * 0.02
        proj_b = jax.random.normal(k4, (EMBED,), dtype=jnp.float32) * 0.02
        return {'x': x, 'curve': curve, 'proj_w': proj_w, 'proj_b': proj_b}
    _L0_tok_all = _L0_tok_setup()
    _L0_tok_in = {k: v for k, v in _L0_tok_all.items() if k in ('curve', 'proj_w', 'proj_b')}
    del _L0_tok_all

    def _L0_txt_setup():
        import jax, jax.numpy as jnp
        import numpy as np
        VOCAB = 8000
        DIM = 192
        BATCH = 8
        SEQ = 512

        def _sinusoidal_pos(seq_len, dim):
            pos = jnp.arange(seq_len, dtype=jnp.float32)[:, None]
            ids = jnp.arange(dim, dtype=jnp.float32)[None, :]
            even_exp = jnp.floor(ids / 2.0) * 2.0 / dim
            angle = pos / jnp.power(10000.0, even_exp)
            return jnp.where(jnp.arange(dim) % 2 == 0, jnp.sin(angle), jnp.cos(angle))
        key = jax.random.key(seed)
        k1, k2, k3, k4 = jax.random.split(key, 4)
        input_tensor = jax.random.randint(k1, (BATCH, SEQ), 0, VOCAB)
        segment_label = jax.random.randint(k2, (BATCH, SEQ), 0, 3)
        token_table = jax.random.normal(k3, (VOCAB, DIM), dtype=jnp.float32) * 0.02
        segm_table = jax.random.normal(k4, (3, DIM), dtype=jnp.float32) * 0.02
        token_table = token_table.at[0].set(0.0)
        segm_table = segm_table.at[0].set(0.0)
        return {'input_tensor': input_tensor, 'segment_label': segment_label, 'token_table': token_table, 'segm_table': segm_table}
    _L0_txt_all = _L0_txt_setup()
    _L0_txt_in = {k: v for k, v in _L0_txt_all.items() if k in ('token_table', 'segm_table')}
    del _L0_txt_all

    def _L0_attn_setup():
        import jax, jax.numpy as jnp
        import numpy as np
        B, N, DIM, H = (8, 256, 192, 12)
        DH = DIM // H
        LATENT = 32
        EPS = 1e-05

        def _heads(t):
            b, n, _ = t.shape
            return t.reshape(b, n, H, DH).transpose(0, 2, 1, 3).reshape(b * H, n, DH)

        def _merge(t, b):
            _, n, dh = t.shape
            return t.reshape(b, H, n, dh).transpose(0, 2, 1, 3).reshape(b, n, H * dh)

        def _ln(v, g, bta):
            mu = v.mean(-1, keepdims=True)
            var = ((v - mu) ** 2).mean(-1, keepdims=True)
            return (v - mu) * jax.lax.rsqrt(var + EPS) * g + bta

        def _rope(t):
            n, dh = (t.shape[-2], t.shape[-1])
            inv = 1.0 / 10000.0 ** (jnp.arange(0, dh, 2, dtype=jnp.float32) / dh)
            f = jnp.arange(n, dtype=jnp.float32)[:, None] * inv[None, :]
            f = jnp.concatenate([f, f], -1)[None]
            x1, x2 = jnp.split(t, 2, -1)
            rot = jnp.concatenate([-x2, x1], -1)
            return t * jnp.cos(f) + rot * jnp.sin(f)
        key = jax.random.key(seed)
        ks = jax.random.split(key, 6)
        s = 0.02
        return {'x': jax.random.normal(ks[0], (B, N, DIM), jnp.float32), 'Wq': jax.random.normal(ks[1], (DIM, DIM), jnp.float32) * s, 'Wkv': jax.random.normal(ks[2], (DIM, DIM), jnp.float32) * s, 'Wo_ctx': jax.random.normal(ks[3], (DIM, DIM), jnp.float32) * s, 'bo_ctx': jnp.zeros((DIM,), jnp.float32), 'Wo_lat': jax.random.normal(ks[4], (DIM, DIM), jnp.float32) * s, 'bo_lat': jnp.zeros((DIM,), jnp.float32), 'ln_g': jnp.ones((DH,), jnp.float32), 'ln_b': jnp.zeros((DH,), jnp.float32)}
    _L0_attn_all = _L0_attn_setup()
    _L0_attn_in = {k: v for k, v in _L0_attn_all.items() if k in ('Wq', 'Wkv', 'Wo_ctx', 'bo_ctx', 'Wo_lat', 'bo_lat', 'ln_g', 'ln_b')}
    del _L0_attn_all

    def _L0_ffn_setup():
        import jax, jax.numpy as jnp
        import numpy as np
        E, H, I = (5, 192, 256)
        TOP_K = 2
        key = jax.random.key(seed)
        ks = jax.random.split(key, 6)
        s = 0.02
        return {'x': jax.random.normal(ks[0], (4, 512, H), dtype=jnp.float32), 'router_w': jax.random.normal(ks[1], (E, H), dtype=jnp.float32) * s, 'router_b': jnp.zeros((E,), dtype=jnp.float32), 'gate_w': jax.random.normal(ks[2], (E, H, I), dtype=jnp.float32) * s, 'up_w': jax.random.normal(ks[3], (E, H, I), dtype=jnp.float32) * s, 'down_w': jax.random.normal(ks[4], (E, I, H), dtype=jnp.float32) * s}
    _L0_ffn_all = _L0_ffn_setup()
    _L0_ffn_in = {k: v for k, v in _L0_ffn_all.items() if k in ('router_w', 'router_b', 'gate_w', 'up_w', 'down_w')}
    del _L0_ffn_all

    def _L1_attn_setup():
        import jax, jax.numpy as jnp
        import numpy as np
        import math
        D_MODEL = 192
        N_HEADS = 6
        HD = D_MODEL // N_HEADS
        RANK = D_MODEL // 4
        B, T = (128, 64)

        def _rope_tables(T, dim):
            inv = 1.0 / 10000.0 ** (jnp.arange(0, dim, 2, dtype=jnp.float32) / dim)
            t = jnp.arange(T, dtype=jnp.float32)
            freqs = jnp.outer(t, inv)
            emb = jnp.concatenate([freqs, freqs], axis=-1)
            return (jnp.cos(emb), jnp.sin(emb))

        def _rot(x):
            h = x.shape[-1] // 2
            return jnp.concatenate([-x[..., h:], x[..., :h]], axis=-1)
        key = jax.random.key(seed)
        ks = jax.random.split(key, 8)
        s_in = 1.0 / math.sqrt(D_MODEL)
        s_r = 1.0 / math.sqrt(RANK)
        inp = {'x': jax.random.normal(ks[0], (B, T, D_MODEL), dtype=jnp.float32), 'qA': jax.random.normal(ks[1], (D_MODEL, RANK), dtype=jnp.float32) * s_in, 'qB': jax.random.normal(ks[2], (RANK, D_MODEL), dtype=jnp.float32) * s_r, 'kA': jax.random.normal(ks[3], (D_MODEL, RANK), dtype=jnp.float32) * s_in, 'kB': jax.random.normal(ks[4], (RANK, D_MODEL), dtype=jnp.float32) * s_r, 'vA': jax.random.normal(ks[5], (D_MODEL, RANK), dtype=jnp.float32) * s_in, 'vB': jax.random.normal(ks[6], (RANK, D_MODEL), dtype=jnp.float32) * s_r, 'o_w': jax.random.normal(ks[7], (D_MODEL, D_MODEL), dtype=jnp.float32) * s_in}
        return inp
    _L1_attn_all = _L1_attn_setup()
    _L1_attn_in = {k: v for k, v in _L1_attn_all.items() if k in ('qA', 'qB', 'kA', 'kB', 'vA', 'vB', 'o_w')}
    del _L1_attn_all

    def _L1_ffn_setup():
        import jax, jax.numpy as jnp
        import numpy as np
        E = 8
        TOP_K = 2
        CAP_RATIO = 1.2
        key = jax.random.key(seed)
        k1, k2, k3, k4 = jax.random.split(key, 4)
        B, L, D, H = (2, 512, 192, 512)
        x = jax.random.normal(k1, (B, L, D), dtype=jnp.float32)
        Wg = jax.random.normal(k2, (D, E), dtype=jnp.float32) * 0.02
        W1 = jax.random.normal(k3, (E, D, 2 * H), dtype=jnp.float32) * 0.02
        W2 = jax.random.normal(k4, (E, H, D), dtype=jnp.float32) * 0.02
        return {'x': x, 'Wg': Wg, 'W1': W1, 'W2': W2}
    _L1_ffn_all = _L1_ffn_setup()
    _L1_ffn_in = {k: v for k, v in _L1_ffn_all.items() if k in ('Wg', 'W1', 'W2')}
    del _L1_ffn_all
    return {'x': x, 'x_txt': x_txt, 'mask_BS_i2_0': mask_BS_i2_0, 'L0_tok_curve': _L0_tok_in['curve'], 'L0_tok_proj_w': _L0_tok_in['proj_w'], 'L0_tok_proj_b': _L0_tok_in['proj_b'], 'L0_txt_token_table': _L0_txt_in['token_table'], 'L0_txt_segm_table': _L0_txt_in['segm_table'], 'L0_attn_Wq': _L0_attn_in['Wq'], 'L0_attn_Wkv': _L0_attn_in['Wkv'], 'L0_attn_Wo_ctx': _L0_attn_in['Wo_ctx'], 'L0_attn_bo_ctx': _L0_attn_in['bo_ctx'], 'L0_attn_Wo_lat': _L0_attn_in['Wo_lat'], 'L0_attn_bo_lat': _L0_attn_in['bo_lat'], 'L0_attn_ln_g': _L0_attn_in['ln_g'], 'L0_attn_ln_b': _L0_attn_in['ln_b'], 'L0_ffn_router_w': _L0_ffn_in['router_w'], 'L0_ffn_router_b': _L0_ffn_in['router_b'], 'L0_ffn_gate_w': _L0_ffn_in['gate_w'], 'L0_ffn_up_w': _L0_ffn_in['up_w'], 'L0_ffn_down_w': _L0_ffn_in['down_w'], 'L1_attn_qA': _L1_attn_in['qA'], 'L1_attn_qB': _L1_attn_in['qB'], 'L1_attn_kA': _L1_attn_in['kA'], 'L1_attn_kB': _L1_attn_in['kB'], 'L1_attn_vA': _L1_attn_in['vA'], 'L1_attn_vB': _L1_attn_in['vB'], 'L1_attn_o_w': _L1_attn_in['o_w'], 'L1_ffn_Wg': _L1_ffn_in['Wg'], 'L1_ffn_W1': _L1_ffn_in['W1'], 'L1_ffn_W2': _L1_ffn_in['W2']}

def reference(x, x_txt, mask_BS_i2_0, L0_tok_curve, L0_tok_proj_w, L0_tok_proj_b, L0_txt_token_table, L0_txt_segm_table, L0_attn_Wq, L0_attn_Wkv, L0_attn_Wo_ctx, L0_attn_bo_ctx, L0_attn_Wo_lat, L0_attn_bo_lat, L0_attn_ln_g, L0_attn_ln_b, L0_ffn_router_w, L0_ffn_router_b, L0_ffn_gate_w, L0_ffn_up_w, L0_ffn_down_w, L1_attn_qA, L1_attn_qB, L1_attn_kA, L1_attn_kB, L1_attn_vA, L1_attn_vB, L1_attn_o_w, L1_ffn_Wg, L1_ffn_W1, L1_ffn_W2):
    import jax
    import jax.numpy as jnp

    def _L0_tok_ref(x, curve, proj_w, proj_b):
        import jax, jax.numpy as jnp
        import numpy as np
        B, C, H, W_IMG = (128, 3, 224, 224)
        N_PATCH, EMBED = (256, 192)
        GRID = 32
        gathered = x[:, :, curve[:, 1], curve[:, 0]]
        return jnp.einsum('bcn,ec->bne', gathered, proj_w) + proj_b

    def _L0_txt_ref(input_tensor, segment_label, token_table, segm_table):
        import jax, jax.numpy as jnp
        import numpy as np
        VOCAB = 8000
        DIM = 192
        BATCH = 8
        SEQ = 512

        def _sinusoidal_pos(seq_len, dim):
            pos = jnp.arange(seq_len, dtype=jnp.float32)[:, None]
            ids = jnp.arange(dim, dtype=jnp.float32)[None, :]
            even_exp = jnp.floor(ids / 2.0) * 2.0 / dim
            angle = pos / jnp.power(10000.0, even_exp)
            return jnp.where(jnp.arange(dim) % 2 == 0, jnp.sin(angle), jnp.cos(angle))
        batch, seq = input_tensor.shape
        pos = _sinusoidal_pos(seq, token_table.shape[1])
        tokens_embed = token_table[input_tensor]
        segments_embed = segm_table[segment_label]
        return segments_embed + pos[None, :, :] + tokens_embed

    def _L0_attn_ref(x, Wq, Wkv, Wo_ctx, bo_ctx, Wo_lat, bo_lat, ln_g, ln_b):
        import jax, jax.numpy as jnp
        import numpy as np
        B, N, DIM, H = (8, 256, 192, 12)
        DH = DIM // H
        LATENT = 32
        EPS = 1e-05

        def _heads(t):
            b, n, _ = t.shape
            return t.reshape(b, n, H, DH).transpose(0, 2, 1, 3).reshape(b * H, n, DH)

        def _merge(t, b):
            _, n, dh = t.shape
            return t.reshape(b, H, n, dh).transpose(0, 2, 1, 3).reshape(b, n, H * dh)

        def _ln(v, g, bta):
            mu = v.mean(-1, keepdims=True)
            var = ((v - mu) ** 2).mean(-1, keepdims=True)
            return (v - mu) * jax.lax.rsqrt(var + EPS) * g + bta

        def _rope(t):
            n, dh = (t.shape[-2], t.shape[-1])
            inv = 1.0 / 10000.0 ** (jnp.arange(0, dh, 2, dtype=jnp.float32) / dh)
            f = jnp.arange(n, dtype=jnp.float32)[:, None] * inv[None, :]
            f = jnp.concatenate([f, f], -1)[None]
            x1, x2 = jnp.split(t, 2, -1)
            rot = jnp.concatenate([-x2, x1], -1)
            return t * jnp.cos(f) + rot * jnp.sin(f)
        b, n, _ = x.shape
        ctx = n - LATENT
        q = _heads(x @ Wq)
        kv = _heads(x @ Wkv)
        q = _rope(q)
        kv = _rope(kv)
        q = q * DH ** (-0.5)
        q_lat, q_ctx = (q[:, ctx:], q[:, :ctx])
        kv_ctx = kv[:, :ctx]
        lkv = _ln(kv, ln_g, ln_b)
        lkv_ctx = _ln(kv_ctx, ln_g, ln_b)
        attn_lat = jax.nn.softmax(jnp.einsum('bid,bkd->bik', q_lat, kv), axis=-1)
        attn_ctx = jax.nn.softmax(jnp.einsum('bid,bkd->bik', q_ctx, kv_ctx), axis=-1)
        out_lat = _merge(jnp.einsum('bik,bkd->bid', attn_lat, lkv), b) @ Wo_lat + bo_lat
        out_ctx = _merge(jnp.einsum('bik,bkd->bid', attn_ctx, lkv_ctx), b) @ Wo_ctx + bo_ctx
        return jnp.concatenate([out_ctx, out_lat], axis=1)

    def _L0_ffn_ref(x, router_w, router_b, gate_w, up_w, down_w):
        import jax, jax.numpy as jnp
        import numpy as np
        E, H, I = (5, 192, 256)
        TOP_K = 2
        B, S, Hd = x.shape
        xf = x.reshape(-1, Hd)
        T = xf.shape[0]
        logits = xf @ router_w.T + router_b
        scores = jax.nn.softmax(logits, axis=-1)
        vals, idx = jax.lax.top_k(scores, TOP_K)
        vals = vals / jnp.sum(vals, axis=-1, keepdims=True)
        comb = jnp.zeros((T, gate_w.shape[0]), dtype=x.dtype)
        comb = comb.at[jnp.arange(T)[:, None], idx].add(vals)
        g = jnp.einsum('th,ehi->tei', xf, gate_w)
        u = jnp.einsum('th,ehi->tei', xf, up_w)
        y = jnp.einsum('tei,eih->teh', jax.nn.silu(g) * u, down_w)
        out = jnp.einsum('teh,te->th', y, comb)
        return out.reshape(B, S, Hd)

    def _L1_attn_ref(x, qA, qB, kA, kB, vA, vB, o_w):
        import jax, jax.numpy as jnp
        import numpy as np
        import math
        D_MODEL = 192
        N_HEADS = 6
        HD = D_MODEL // N_HEADS
        RANK = D_MODEL // 4
        B, T = (128, 64)

        def _rope_tables(T, dim):
            inv = 1.0 / 10000.0 ** (jnp.arange(0, dim, 2, dtype=jnp.float32) / dim)
            t = jnp.arange(T, dtype=jnp.float32)
            freqs = jnp.outer(t, inv)
            emb = jnp.concatenate([freqs, freqs], axis=-1)
            return (jnp.cos(emb), jnp.sin(emb))

        def _rot(x):
            h = x.shape[-1] // 2
            return jnp.concatenate([-x[..., h:], x[..., :h]], axis=-1)
        Bb, Tt, _ = x.shape

        def proj(A, W):
            h = x @ A @ W
            return h.reshape(Bb, Tt, N_HEADS, HD).transpose(0, 2, 1, 3)
        q = proj(qA, qB)
        k = proj(kA, kB)
        v = proj(vA, vB)
        cos, sin = _rope_tables(Tt, HD)
        q = q * cos + _rot(q) * sin
        k = k * cos + _rot(k) * sin
        att = jnp.einsum('bhqd,bhkd->bhqk', q, k) / math.sqrt(HD)
        causal = jnp.tril(jnp.ones((Tt, Tt), dtype=bool))
        att = jnp.where(causal, att, -jnp.inf)
        att = jax.nn.softmax(att, axis=-1)
        out = jnp.einsum('bhqk,bhkd->bhqd', att, v)
        out = out.transpose(0, 2, 1, 3).reshape(Bb, Tt, D_MODEL)
        return out @ o_w

    def _L1_ffn_ref(x, Wg, W1, W2):
        import jax, jax.numpy as jnp
        import numpy as np
        E = 8
        TOP_K = 2
        CAP_RATIO = 1.2
        B, L, D = x.shape
        H = W2.shape[1]
        xf = x.reshape(-1, D)
        N = xf.shape[0]
        capacity = int(CAP_RATIO * N / E)
        logits = xf @ Wg
        scores, idx = jax.lax.top_k(logits, TOP_K)
        weights = jax.nn.softmax(scores, axis=-1)
        xpad = jnp.concatenate([xf, jnp.zeros((1, D), xf.dtype)], axis=0)
        wpad_zero = jnp.zeros((1,), weights.dtype)
        out = jnp.zeros((N, D), x.dtype)
        for k in range(TOP_K):
            ik = idx[:, k]
            onehot = ik[:, None] == jnp.arange(E)[None, :]
            pos = jnp.cumsum(onehot, axis=0) - 1
            posk = jnp.take_along_axis(pos, ik[:, None], axis=1)[:, 0]
            keep = posk < capacity
            buf = jnp.full((E, capacity), N, dtype=jnp.int32)
            buf = buf.at[ik, posk].set(jnp.arange(N, dtype=jnp.int32), mode='drop')
            xg = xpad[buf]
            h = jnp.einsum('ecd,edh->ech', xg, W1)
            act = h[..., :H] * jax.nn.silu(h[..., H:])
            ye = jnp.einsum('ech,ehd->ecd', act, W2)
            wk = jnp.where(keep, weights[:, k], 0.0)
            w_buf = jnp.concatenate([wk, wpad_zero])[buf]
            out = out.at[buf.reshape(-1)].add((w_buf[..., None] * ye).reshape(E * capacity, D), mode='drop')
        return out.reshape(B, L, D)
    h = _L0_tok_ref(x, L0_tok_curve, L0_tok_proj_w, L0_tok_proj_b)
    h = jnp.concatenate([h, _L0_txt_ref(x_txt, mask_BS_i2_0, L0_txt_token_table, L0_txt_segm_table)], axis=1)
    h = h + _L0_attn_ref(_layernorm(h, axis=-1), L0_attn_Wq, L0_attn_Wkv, L0_attn_Wo_ctx, L0_attn_bo_ctx, L0_attn_Wo_lat, L0_attn_bo_lat, L0_attn_ln_g, L0_attn_ln_b)
    h = h + _L0_ffn_ref(_layernorm(h, axis=-1), L0_ffn_router_w, L0_ffn_router_b, L0_ffn_gate_w, L0_ffn_up_w, L0_ffn_down_w)
    h = h + _L1_attn_ref(_layernorm(h, axis=-1), L1_attn_qA, L1_attn_qB, L1_attn_kA, L1_attn_kB, L1_attn_vA, L1_attn_vB, L1_attn_o_w)
    h = h + _L1_ffn_ref(_layernorm(h, axis=-1), L1_ffn_Wg, L1_ffn_W1, L1_ffn_W2)
    return h

_drawn_inputs = setup_inputs


def setup_inputs(seed=0):
    import zlib

    import numpy as np

    out = dict(_drawn_inputs(seed))
    spreads = {'L0_attn_bo_ctx': (0.0, 0.1),
     'L0_attn_bo_lat': (0.0, 0.29),
     'L0_attn_ln_g': (1.0, 0.2),
     'L0_attn_ln_b': (0.0, 0.1),
     'L0_ffn_router_b': (0.0, 0.8)}
    factors = {'L0_txt_token_table': 3.976,
     'L0_txt_segm_table': 3.443,
     'L0_attn_Wq': 2.959,
     'L1_ffn_Wg': 8.0,
     'L1_ffn_W1': 8.0,
     'L1_ffn_W2': 8.0}
    for name, (base, spread) in spreads.items():
        noise = np.random.default_rng([zlib.crc32(name.encode()), seed]).standard_normal(out[name].shape)
        drawn = base * np.exp(spread * noise) if base else spread * noise
        out[name] = jnp.asarray(drawn.astype(out[name].dtype))
    for name, factor in factors.items():
        out[name] = (out[name] * factor).astype(out[name].dtype)
    return out
```

```python
from contextlib import ExitStack

import concourse.bass as bass
from concourse import mybir

F32 = mybir.dt.float32
F32R = mybir.dt.float32r
BF16 = mybir.dt.bfloat16
I32 = mybir.dt.int32
U32 = mybir.dt.uint32
ALU = mybir.AluOpType
ACT = mybir.ActivationFunctionType
AX = mybir.AxisListType

P = 128
D = 192
KH = D // 2
B = 32
NVIS, NTXT = 256, 128
T = NVIS + NTXT
NT = T // P
LAT = 32
CTX = T - LAT
N = B * T
VOCAB, NSEG, IMG = 8000, 3, 128
H0, DH0 = 12, 16
H1, DH1, RANK = 6, 32, 48
QKW = 384
E0, I0 = 5, 256
E1, HF = 8, 512
CAP = int(1.2 * N / E1)
EROWS = -(-2 * CAP // T) * T
NCHUNK = EROWS // T
NROWS = E1 * EROWS
EPS = 1e-5
NEG = -1e30
NA, NV = 3, 3
PTH = 3
CIMG = 4

_COLS = {}
_w = 0
for _name, _n in (("ident", P), ("maskq", P), ("maskt", P), ("before", P), ("pos", D),
                  ("cos0", NT * DH0), ("sin0", NT * DH0), ("cos1", NT * DH1), ("sin1", NT * DH1),
                  ("iota", E1), ("base", 2 * E1), ("drop", 2 * NT), ("own", B)):
    _COLS[_name] = slice(_w, _w + _n)
    _w += _n
NCOLS = _w


def constants():
    import numpy as np

    c = np.zeros((P, NCOLS), np.float32)
    p = np.arange(P)
    c[:, _COLS["ident"]] = np.eye(P)
    c[:, _COLS["maskq"]] = np.where(p[None, :] <= p[:, None], 0.0, NEG)
    c[:, _COLS["maskt"]] = np.where(p[:, None] <= p[None, :], 0.0, NEG)
    c[:, _COLS["before"]] = p[:, None] < p[None, :]
    ids = np.arange(D, dtype=np.float32)
    angle = p.astype(np.float32)[:, None] / np.power(
        np.float32(10000.0), np.floor(ids / np.float32(2)) * np.float32(2) / np.float32(D)).astype(np.float32)[None]
    c[:, _COLS["pos"]] = np.where(np.arange(D) % 2 == 0, np.sin(angle.astype(np.float64)),
                                  np.cos(angle.astype(np.float64)))
    for name, dh in (("0", DH0), ("1", DH1)):
        inv = (np.float32(1.0) / np.power(np.float32(10000.0), np.arange(0, dh, 2, dtype=np.float32)
                                          / np.float32(dh))).astype(np.float32)
        f = (np.arange(T, dtype=np.float32)[:, None] * inv[None, :]).astype(np.float32).astype(np.float64)
        cos = np.concatenate([np.cos(f), np.cos(f)], 1).reshape(NT, P, dh).transpose(1, 0, 2)
        sin = np.concatenate([-np.sin(f), np.sin(f)], 1).reshape(NT, P, dh).transpose(1, 0, 2)
        c[:, _COLS["cos" + name]] = cos.reshape(P, -1)
        c[:, _COLS["sin" + name]] = sin.reshape(P, -1)
    c[:, _COLS["iota"]] = np.arange(E1)[None]
    c[:, _COLS["base"]] = (np.arange(2)[:, None] * CAP + np.arange(E1)[None] * EROWS).reshape(1, -1)
    c[:, _COLS["drop"]] = (NROWS + np.arange(NT)[None, :, None] * P + p[:, None, None]
                           + np.arange(2)[None, None, :] * N).reshape(P, -1)
    c[:3 * B, _COLS["own"]] = np.repeat(np.eye(B), 3, axis=0)
    c[3 * B, _COLS["own"]] = 1.0
    return c


def bank_plan():
    def attention(k, heads, per_block):
        a, v = [], []
        for b in range(3):
            v.append(("q_round", k, b))
            a.append(("k_t", k, b))
        v += [("max", k, hd, t) for hd in range(heads) for t in range(NT)]
        for hd in range(heads):
            if hd % per_block == 0:
                a.append(("q_t", k, hd // per_block))
            a += [("score", k, hd, t) for t in range(NT)]
        return a + [("att_t", k)], v + [("att_t", k)] + [("out", k, t) for t in range(NT)]

    a, v = [("xt", 0)], [("patch", 0), ("patch", 1), ("xt", 0)] + [("qk", 0, t) for t in range(NT)]
    a0, v0 = attention(0, H0, 4)
    a += a0 + [("xt", 1)] + [("gate", e, m) for e in range(E0) for m in range(2)]
    v += v0 + [("xt", 1), ("logits", 0)]
    for e in range(E0):
        v += [("up", e, m) for m in range(2)] + [("down", e - 1, t) for t in range(NT) if e]
    v += [("down", E0 - 1, t) for t in range(NT)]
    a1, v1 = attention(1, H1, 2)
    a += [("xt", 2), ("r_qk",)] + [("v1", t) for t in range(NT)] + a1 + [("xt", 3)]
    v += [("xt", 2), ("r_v",)] + [("qk", 1, t) for t in range(NT)] + v1 + [("xt", 3), ("logits", 1), ("rank",)]
    return {what: n for n, what in enumerate(a)}, {what: n for n, what in enumerate(v)}


A, V = bank_plan()


def early_fusion_kernel(nc, consts, img, txt, seg, curve, projw, projb, tok_table, seg_table, wqkv,
                        wo_ctx, bo_ctx, wo_lat, bo_lat, ln_g, ln_b, router_w, router_b, gate_w, up_w,
                        down_w, qa, qb, ka, kb, va, vb, ow, wg, w1, w2, out):
    xs_dram = nc.dram_tensor("xs_dram", (NROWS + 2 * N, D), F32, kind="Internal").ap()
    y_dram = nc.dram_tensor("y_dram", (NROWS, D), F32, kind="Internal").ap()
    h_dram = nc.dram_tensor("h_dram", (N, D), F32, kind="Internal").ap()

    with ExitStack() as whole:
        slots_all = whole.enter_context(nc.sbuf_tensor("slots_all", [P, B * NT * 2], I32))
        weights_all = whole.enter_context(nc.sbuf_tensor("weights_all", [P, B * NT * 2], F32))
        ident = whole.enter_context(nc.sbuf_tensor("ident", [P, P], F32))
        token_stages(nc, consts, img, txt, seg, curve, projw, projb, tok_table, seg_table, wqkv,
                     wo_ctx, bo_ctx, wo_lat, bo_lat, ln_g, ln_b, router_w, router_b, gate_w, up_w,
                     down_w, qa, qb, ka, kb, va, vb, ow, wg, xs_dram, h_dram, slots_all, weights_all, ident)
        expert_stage(nc, w1, w2, xs_dram, y_dram, ident)
        combine_stage(nc, y_dram, h_dram, out, slots_all, weights_all)


def token_stages(nc, consts, img, txt, seg, curve, projw, projb, tok_table, seg_table, wqkv,
                 wo_ctx, bo_ctx, wo_lat, bo_lat, ln_g, ln_b, router_w, router_b, gate_w, up_w,
                 down_w, qa, qb, ka, kb, va, vb, ow, wg, xs_dram, h_dram, slots_all, weights_all, ident):
    ctx = ExitStack()
    with ctx:
        def sb(name, shape, dt=F32):
            return ctx.enter_context(nc.sbuf_tensor(name, shape, dt))

        def ps(name):
            return ctx.enter_context(nc.psum_tensor(name, [P, 512], F32))

        def sem(name):
            return ctx.enter_context(nc.semaphore(name))

        cst = sb("cst", [P, NCOLS])
        identb = sb("identb", [P, P], BF16)
        maskq = sb("maskq", [P, P], BF16)
        maskt = sb("maskt", [P, P], BF16)
        before = sb("before", [P, P], BF16)
        onesb = sb("onesb", [P, P], BF16)
        pow_half = sb("pow_half", [P, 36])
        zeros = sb("zeros", [P, 8 * D])
        w_qkv = sb("w_qkv", [KH, 2, 2 * D])
        w_octx = sb("w_octx", [KH + 1, 2, D])
        w_olat = sb("w_olat", [KH + 1, 2, D])
        w_router = sb("w_router", [KH + 1, 2, E0])
        w_gate = sb("w_gate", [KH, 2, E0, I0])
        w_up = sb("w_up", [KH, 2, E0, I0])
        w_down = sb("w_down", [P, 2, E0, D])
        w_a = sb("w_a", [KH, 2, 64 + RANK])
        w_va = sb("w_va", [KH, 2, RANK])
        w_b = sb("w_b", [64 + RANK, 2 * D])
        w_vb = sb("w_vb", [RANK, D])
        w_o1 = sb("w_o1", [KH, 2, D])
        w_g1 = sb("w_g1", [KH, 2, E1])
        lng = sb("lng", [P, DH0])
        lnb = sb("lnb", [P, DH0])
        proj = sb("proj", [3 * B + 1, D])
        own_proj = sb("own_proj", [3 * B + 1, B, D])
        curve_i = sb("curve_i", [P, 2, 2], I32)
        curve_f = sb("curve_f", [P, 2, 2])
        pix_f = sb("pix_f", [P, 2])
        pix_i = sb("pix_i", [P, 2], I32)
        ids_i = sb("ids_i", [P, 2, B], I32)
        ids_f = sb("ids_f", [P, 2, B])
        patches = sb("patches", [P, 2, 3 * B])
        patches_t = sb("patches_t", [3 * B + 1, 2, P])

        idx = sb("idx", [P, 2], I32)
        tokrow = sb("tokrow", [P, D])
        segrow = sb("segrow", [P, D])
        embsum = sb("embsum", [P, D])
        h = sb("h", [P, NT, D])
        st6 = sb("st6", [P, NT, 6])
        mv = sb("mv", [P, NT, 2])
        ve = sb("ve", [P, NT])
        rstd = sb("rstd", [P, NT])
        xn = sb("xn", [P, NT, D])
        xt = sb("xt", [KH + 1, 2, T])
        rope_a = sb("rope_a", [P, NT, 2 * D])
        rope_b = sb("rope_b", [P, NT, 2 * D])
        qk0 = sb("qk0", [P, NT, 2, QKW])
        qk1 = sb("qk1", [P, NT, 2, QKW])
        q_round = sb("q_round", [P, 3, T], F32R)
        k_round = sb("k_round", [P, 3, T], F32R)
        q_t = sb("q_t", [P, 3, T])
        k_t = sb("k_t", [P, 3, T])
        probs = sb("probs", [P, PTH, NT, T])
        v0 = sb("v0", [P, NT, H0, DH0 + 1])
        v1 = sb("v1", [P, NT, H1, DH1 + 1])
        vsum = sb("vsum", [P, NT * H0])
        vcen = sb("vcen", [P, NT * H0, DH0])
        vsq = sb("vsq", [P, NT * H0, DH0])
        vvar = sb("vvar", [P, NT * H0])
        vms = sb("vms", [P, NT * H0])
        vrstd = sb("vrstd", [P, NT * H0])
        rsum = sb("rsum", [P, NT, H0])
        att = sb("att", [P, NT, D])
        att_t = sb("att_t", [KH + 1, 2, T])
        silu = sb("silu", [P, 2, T])
        hid = sb("hid", [P, 2, 2, T])
        r_qk = sb("r_qk", [64 + RANK, T])
        r_v = sb("r_v", [RANK, T])
        lg = [sb(f"lg{k}", [P, NT, 8]) for k in range(2)]
        top = sb("top", [P, NT, 8])
        topi = sb("topi", [P, NT, 8], U32)
        topf = sb("topf", [P, NT, 2])
        dl = sb("dl", [P, NT])
        ed = sb("ed", [P, NT])
        ed1 = sb("ed1", [P, NT])
        wk = sb("wk", [P, NT, 2])
        oh = sb("oh", [P, NT, 2, 8])
        ohw = sb("ohw", [P, NT, 2, 8])
        ohbase = sb("ohbase", [P, NT, 2, 8])
        ohb = sb("ohb", [P, NT, 2 * 8], BF16)
        comb = sb("comb", [P, NT, 8])
        seen = sb("seen", [P, 2 * 8])
        seenb = sb("seenb", [P, 2 * 8], BF16)
        rank = sb("rank", [P, NT, 2])
        bases = sb("bases", [P, NT, 2])
        keep = sb("keep", [P, NT, 2])
        place = sb("place", [P, NT, 2])
        kept = sb("kept", [P, NT, 2])
        off = sb("off", [P, NT, 2])
        drop = sb("drop", [P, NT, 2])
        slot_i = sb("slot_i", [P, NT * 2], I32)

        bank_a = [ps(f"bank_a{i}") for i in range(NA)]
        bank_v = [ps(f"bank_v{i}") for i in range(NV)]
        bank_o = [ps(f"bank_o{i}") for i in range(2)]

        def out_of(t, heads, width):
            w = heads * width
            return (bank_o[0][:, t * w:(t + 1) * w] if t < 2 else bank_o[1][:, 0:w]).rearrange(
                "p (h d) -> p h d", d=width)

        def heads0(ap):
            return ap.rearrange("p (h d) -> p h d", d=32)

        def heads1(ap):
            return ap.rearrange("p (h d) -> p h d", d=64)

        def c(name, inner=None):
            ap = cst[:, _COLS[name]]
            return ap if inner is None else ap.rearrange("p (a b) -> p a b", b=inner)

        zeroed = sem("zeroed")
        loaded = sem("loaded")
        pix_ready = sem("pix_ready")
        patch_in = sem("patch_in")
        set_v = sem("set_v")
        set_p = sem("set_p")
        patch_tr = sem("patch_tr")
        zero_ready = sem("zero_ready")

        n_zero = NROWS // (P * 8)
        halves = lambda ap: ap.rearrange("(k p) n -> p k n", p=KH)
        row = lambda ap, n: bass.AP(ap.tensor, ap.offset, [[0, n], [1, ap.shape[-1]]])
        loads = [
            (cst[:], consts), (curve_i[:], curve.rearrange("(t p) c -> p t c", p=P)),
            (ids_i[:, 0, :], txt), (ids_i[:, 1, :], seg),
            (proj[3 * B:3 * B + 1, :], row(projb, 1)),
            (w_qkv[:], halves(wqkv)), (w_octx[0:KH], halves(wo_ctx)), (w_olat[0:KH], halves(wo_lat)),
            (w_octx[KH:KH + 1, 0, :], row(bo_ctx, 1)), (w_olat[KH:KH + 1, 0, :], row(bo_lat, 1)),
            (w_router[0:KH], halves(router_w)), (w_router[KH:KH + 1, 0, :], row(router_b, 1)),
            (w_va[:], halves(va)), (w_a[:, :, 0:RANK], halves(qa)), (w_a[:, :, 64:64 + RANK], halves(ka)),
            (w_b[0:RANK, 0:D], qb), (w_b[64:64 + RANK, D:2 * D], kb), (w_vb[:], vb),
            (w_o1[:], halves(ow)), (w_g1[:], halves(wg)),
            (lng[:], row(ln_g, P)), (lnb[:], row(ln_b, P)),
        ] + [(w_gate[:, :, e, :], halves(gate_w[e])) for e in range(E0)] \
          + [(w_up[:, :, e, :], halves(up_w[e])) for e in range(E0)] \
          + [(w_down[:, :, e, :], down_w[e].rearrange("(k p) n -> p k n", p=P)) for e in range(E0)] \
          + [(proj[3 * b:3 * b + 3, :], projw) for b in range(B)]

        with nc.Block() as block:
            @block.sync
            def _(sp):
                sp.wait_ge(set_p, 2)
                for dst, src in loads:
                    sp.dma_start(dst, src).then_inc(loaded, 16)

            @block.scalar
            def _(act):
                act.wait_ge(zero_ready, 1)
                for n in range(n_zero):
                    act.dma_start(xs_dram[n * 8 * P:(n + 1) * 8 * P, :].rearrange("(p r) d -> p (r d)", r=8),
                                  zeros[:]).then_inc(zeroed, 16)

            @block.gpsimd
            def _(pool):
                pool.memset(w_a[:], 0.0).then_inc(set_p, 1)
                pool.memset(w_b[:], 0.0).then_inc(set_p, 1)
                pool.memset(xt[:], 1.0).then_inc(set_p, 1)
                pool.memset(att_t[:], 1.0).then_inc(set_p, 1)
                pool.memset(patches_t[:], 1.0).then_inc(set_p, 1)
                pool.memset(pow_half[:], -0.5).then_inc(set_p, 1)
                pool.wait_ge(pix_ready, 1)
                for t in range(2):
                    pool.indirect_dma_start(patches[:, t, :], None, img,
                                            bass.IndirectOffsetOnAxis(ap=pix_i[:, t:t + 1], axis=0)
                                            ).then_inc(patch_in, 16)
                pool.wait_ge(patch_in, 32)

            @block.vector
            def _(dve):
                n = 0

                def chain(ins):
                    nonlocal n
                    n += 1
                    ins.then_inc(set_v, 1)

                nc.vector.memset(zeros[:], 0.0).then_inc(zero_ready, 1)
                chain(dve.memset(onesb[:], 1.0))
                chain(dve.memset(qk0[:], 0.0))
                chain(dve.memset(qk1[:], 0.0))
                chain(dve.memset(v0[:], 1.0))
                chain(dve.memset(v1[:], 1.0))
                chain(dve.memset(lg[0][:], NEG))
                chain(dve.memset(seen[:], 0.0))
                dve.wait_ge(set_v, n)
                for t in range(NT):
                    chain(dve.memset(heads0(qk0[:, t, 1, :])[:, :, DH0:DH0 + 1], 1.0))
                    chain(dve.memset(heads1(qk1[:, t, 1, :])[:, :, DH1:DH1 + 1], 1.0))
                dve.wait_ge(loaded, 16 * len(loads))
                chain(dve.tensor_copy(ident[:], c("ident")))
                chain(dve.tensor_copy(identb[:], c("ident")))
                chain(dve.tensor_copy(maskq[:], c("maskq")))
                chain(dve.tensor_copy(maskt[:], c("maskt")))
                chain(dve.tensor_copy(before[:], c("before")))
                chain(dve.tensor_copy(drop[:], c("drop", 2)))
                chain(dve.tensor_tensor(
                    own_proj[:], proj[:].unsqueeze(1).to_broadcast([3 * B + 1, B, D]),
                    cst[0:3 * B + 1, _COLS["own"]].unsqueeze(2).to_broadcast([3 * B + 1, B, D]), ALU.mult))
                chain(dve.tensor_scalar(curve_f[:], curve_i[:], 0.0, float(IMG - 1), ALU.max, ALU.min))
                chain(dve.tensor_scalar(ids_f[:, 0, :], ids_i[:, 0, :], 0.0, float(VOCAB - 1), ALU.max, ALU.min))
                chain(dve.tensor_scalar(ids_f[:, 1, :], ids_i[:, 1, :], 0.0, float(NSEG - 1), ALU.max, ALU.min))
                dve.wait_ge(set_v, n)
                chain(dve.tensor_copy(ids_i[:], ids_f[:]))
                chain(dve.scalar_tensor_tensor(pix_f[:], curve_f[:, :, 1], float(IMG), curve_f[:, :, 0],
                                               ALU.mult, ALU.add))
                dve.wait_ge(set_v, n)
                dve.tensor_copy(pix_i[:], pix_f[:]).then_inc(pix_ready, 1)
                dve.wait_ge(patch_tr, 2)
                dve.wait_ge(set_p, 5)
                for t in range(2):
                    chain(dve.tensor_copy(patches_t[0:3 * B, t, :], bank_v[t][0:3 * B, 0:P]))

            @block.tensor
            def _(pe):
                pe.wait_ge(patch_in, 32)
                for t in range(2):
                    pe.transpose(bank_v[t][0:3 * B, 0:P], patches[:, t, :], ident[:]).then_inc(patch_tr, 1)

        rows_in = sem("rows_in")
        scattered = sem("scattered")
        emb_ready = sem("emb_ready")
        a_full, a_free = sem("a_full"), sem("a_free")
        v_full, v_free = sem("v_full"), sem("v_free")
        dve_step, pool_step = sem("dve_step"), sem("pool_step")
        var_ready, rstd_ready, xn_ready = sem("var_ready"), sem("rstd_ready"), sem("xn_ready")
        rope_ready = sem("rope_ready")
        k_round_ready = sem("k_round_ready")
        vcen_ready, vsq_ready = sem("vcen_ready"), sem("vsq_ready")
        vvar_ready, vrstd_ready, v0_ready = sem("vvar_ready"), sem("vrstd_ready"), sem("v0_ready")
        heads_done = sem("heads_done")
        att_ready = sem("att_ready")
        dl_ready, ed_ready = sem("dl_ready"), sem("ed_ready")
        oh_ready = sem("oh_ready")
        slot_ready = sem("slot_ready")
        h_stored = sem("h_stored")
        per_image = range(emb_ready.num, h_stored.num + 1)

        with nc.Fori(0, B) as image:
            with nc.Block(no_gpsimd_drain=True) as block:

                @block.sync
                def _(sp):
                    sp.wait_ge(v_free, V["out", 1, NT - 1] + 1)
                    sp.dma_start(h_dram.rearrange("(i t p) d -> p i t d", t=NT, p=P)[:, bass.ds(image, 1)],
                                 h[:].unsqueeze(1)).then_inc(h_stored, 16)
                    sp.wait_ge(h_stored, 16)

                @block.gpsimd
                def _(pool):
                    pool.tensor_copy(idx[:].unsqueeze(2), ids_i[:, :, bass.ds(image, 1)]).then_inc(pool_step, 1)
                    pool.wait_ge(pool_step, 1)
                    pool.indirect_dma_start(tokrow[:], None, tok_table,
                                            bass.IndirectOffsetOnAxis(ap=idx[:, 0:1], axis=0)).then_inc(rows_in, 16)
                    pool.indirect_dma_start(segrow[:], None, seg_table,
                                            bass.IndirectOffsetOnAxis(ap=idx[:, 1:2], axis=0)).then_inc(rows_in, 16)
                    pool.wait_ge(rows_in, (image + 1) * 32)
                    pool.tensor_tensor(embsum[:], segrow[:], c("pos"), ALU.add).then_inc(pool_step, 1)
                    pool.wait_ge(pool_step, 2)
                    pool.tensor_tensor(h[:, 2, :], embsum[:], tokrow[:], ALU.add).then_inc(emb_ready, 1)

                    def inverse_root(k):
                        pool.wait_ge(var_ready, k + 1)
                        pool.tensor_tensor(rstd[:], ve[:], pow_half[:, 0:NT], ALU.pow).then_inc(rstd_ready, 1)

                    def rope_sum(k, dst):
                        for t in range(NT):
                            pool.wait_ge(v_free, V["qk", k, t] + 1)
                            pool.tensor_tensor(
                                dst(t), rope_a[:, t, :].rearrange("p (g d) -> p g d", d=(DH0, DH1)[k]),
                                rope_b[:, t, :].rearrange("p (g d) -> p g d", d=(DH0, DH1)[k]),
                                ALU.add).then_inc(rope_ready, 1)

                    inverse_root(0)
                    rope_sum(0, lambda t: qk0[:, t].rearrange("p a (h d) -> p (a h) d", d=32)[:, :, 0:DH0])
                    pool.wait_ge(vcen_ready, NT)
                    pool.tensor_tensor(vsq[:], vcen[:], vcen[:], ALU.mult).then_inc(vsq_ready, 1)
                    pool.wait_ge(vvar_ready, 1)
                    pool.tensor_tensor(vrstd[:], vvar[:], pow_half[:], ALU.pow).then_inc(vrstd_ready, 1)
                    inverse_root(1)
                    inverse_root(2)
                    rope_sum(1, lambda t: qk1[:, t].rearrange("p a (h d) -> p (a h) d", d=64)[:, :, 0:DH1])
                    inverse_root(3)
                    pool.wait_ge(zeroed, 16 * n_zero)
                    pool.wait_ge(xn_ready, 4 * NT)
                    pool.wait_ge(slot_ready, 1)
                    for t in range(NT):
                        for k in range(2):
                            pool.indirect_dma_start(
                                xs_dram, bass.IndirectOffsetOnAxis(ap=slot_i[:, 2 * t + k:2 * t + k + 1], axis=0),
                                xn[:, t, :], None).then_inc(scattered, 16)
                    pool.wait_ge(scattered, (image + 1) * (16 * 2 * NT))

                @block.scalar
                def _(act):
                    def empty(*what):
                        act.wait_ge(a_full, A[what] + 1)
                        return bank_a[A[what] % NA]

                    def keys_transposed(k):
                        for b in range(3):
                            bank = empty("k_t", k, b)
                            act.activation(k_round[:, b, :], bank[:, 0:T], ACT.Copy).then_inc(k_round_ready, 1)
                            act.activation(k_t[:, b, :], bank[:, 0:T], ACT.Copy).then_inc(a_free, 1)

                    def exponentials(k, heads, per_block, scale, before):
                        for hd in range(heads):
                            if hd % per_block == 0:
                                b = hd // per_block
                                act.activation(q_t[:, b, :], empty("q_t", k, b)[:, 0:T], ACT.Copy
                                               ).then_inc(a_free, 1)
                            if before + hd >= PTH:
                                act.wait_ge(heads_done, before + hd - PTH + 1)
                            for kt in range(NT):
                                lo = kt * P if k == 1 else 0
                                act.activation(probs[:, (before + hd) % PTH, kt, lo:T],
                                               empty("score", k, hd, kt)[:, lo:T], ACT.Exp,
                                               scale=scale).then_inc(a_free, 1)

                    def choice_weights(k):
                        act.wait_ge(dl_ready, k + 1)
                        act.activation(ed[:], dl[:], ACT.Exp).then_inc(ed_ready, 1)

                    def half_transposed(dst, *what):
                        act.activation(dst[0:KH, 0, :], empty(*what)[0:KH, 0:T], ACT.Copy).then_inc(a_free, 1)

                    half_transposed(xt, "xt", 0)
                    keys_transposed(0)
                    exponentials(0, H0, 4, DH0 ** -0.5, 0)
                    half_transposed(att_t, "att_t", 0)
                    half_transposed(xt, "xt", 1)
                    choice_weights(0)
                    for e in range(E0):
                        for m in range(2):
                            if e:
                                act.wait_ge(v_free, V["up", e - 1, m] + 1)
                            act.activation(silu[:, m, :], empty("gate", e, m)[:, 0:T], ACT.Silu).then_inc(a_free, 1)
                    half_transposed(xt, "xt", 2)
                    act.activation(r_qk[:], empty("r_qk")[0:64 + RANK, 0:T], ACT.Copy).then_inc(a_free, 1)
                    for t in range(NT):
                        act.activation(v1[:, t, :, 0:DH1],
                                       empty("v1", t)[:, 0:D].rearrange("p (h d) -> p h d", d=DH1),
                                       ACT.Copy).then_inc(a_free, 1)
                    keys_transposed(1)
                    exponentials(1, H1, 2, DH1 ** -0.5, H0)
                    half_transposed(att_t, "att_t", 1)
                    half_transposed(xt, "xt", 3)
                    choice_weights(1)

                @block.tensor
                def _(pe):
                    def fill_a(*what):
                        if A[what] >= NA:
                            pe.wait_ge(a_free, A[what] - NA + 1)
                        return bank_a[A[what] % NA]

                    def fill_v(*what):
                        if V[what] >= NV:
                            pe.wait_ge(v_free, V[what] - NV + 1)
                        return bank_v[V[what] % NV]

                    def emptied_a(*what):
                        pe.wait_ge(a_free, A[what] + 1)

                    def emptied_v(*what):
                        pe.wait_ge(v_free, V[what] + 1)

                    def two_halves(name, k, src, ready):
                        for half, (bank, full) in enumerate(((fill_a(name, k), a_full), (None, v_full))):
                            if half:
                                bank = fill_v(name, k)
                            for t in range(NT):
                                pe.wait_ge(ready[0], ready[1] + t + 1)
                                mm = pe.transpose(bank[0:KH, t * P:(t + 1) * P],
                                                  src[:, t, half * KH:(half + 1) * KH], ident[:])
                            mm.then_inc(full, 1)

                    def halves_ready(name, k):
                        emptied_a(name, k)
                        emptied_v(name, k)

                    def project(dst, x, tokens, w, cols, bias):
                        pe.matmul(dst, x[0:KH + bias, 0, tokens], w[0:KH + bias, 0, cols], start=True, stop=False)
                        return pe.matmul(dst, x[0:KH, 1, tokens], w[0:KH, 1, cols], start=False, stop=True)

                    tile = [slice(t * P, (t + 1) * P) for t in range(NT)]

                    def attention(k, heads, per_block, dh, qk, v, before):
                        step = P // per_block
                        pe.wait_ge(rope_ready, NT * (k + 1))
                        for b in range(3):
                            bank = fill_v("q_round", k, b)
                            for t in range(NT):
                                mm = pe.transpose(bank[:, tile[t]], qk[:, t, 0, b * P:(b + 1) * P], ident[:])
                            mm.then_inc(v_full, 1)
                            bank = fill_a("k_t", k, b)
                            for t in range(NT):
                                mm = pe.transpose(bank[:, tile[t]], qk[:, t, 1, b * P:(b + 1) * P], ident[:])
                            mm.then_inc(a_full, 1)

                        def maxima(hd):
                            b, r = hd // per_block, step * (hd % per_block)
                            if hd % per_block == 0:
                                emptied_v("q_round", k, b)
                                pe.wait_ge(k_round_ready, 3 * k + b + 1)
                            for t in range(NT):
                                bank = fill_v("max", k, hd, t)
                                keys = (t + 1) * P if k == 1 else T
                                mm = pe.matmul(bank[:, 0:keys], q_round[r:r + dh, b, tile[t]],
                                               k_round[r:r + dh, b, 0:keys], start=True, stop=(k == 0))
                                if k == 1:
                                    mm = pe.matmul(bank[:, tile[t]], identb[:], maskq[:], start=False, stop=True)
                                mm.then_inc(v_full, 1)

                        def scores(hd):
                            b, r = hd // per_block, step * (hd % per_block)
                            if hd % per_block == 0:
                                emptied_v("max", k, hd + per_block - 1, NT - 1)
                                bank = fill_a("q_t", k, b)
                                for t in range(NT):
                                    mm = pe.transpose(bank[:, tile[t]], qk[:, t, 0, b * P:(b + 1) * P], ident[:])
                                mm.then_inc(a_full, 1)
                                emptied_a("q_t", k, b)
                            for t in range(NT):
                                bank = fill_a("score", k, hd, t)
                                lo = t * P if k == 1 else 0
                                mm = pe.matmul(bank[:, lo:T], k_t[r:r + dh + 1, b, tile[t]],
                                               q_t[r:r + dh + 1, b, lo:T], start=True, stop=(k == 0))
                                if k == 1:
                                    mm = pe.matmul(bank[:, tile[t]], identb[:], maskt[:], start=False, stop=True)
                                mm.then_inc(a_full, 1)

                        def apply(hd):
                            emptied_a("score", k, hd, NT - 1)
                            if k == 0 and hd == 0:
                                pe.wait_ge(v0_ready, 1)
                            pr = probs[:, (before + hd) % PTH]
                            for t in range(NT):
                                o = out_of(t, heads, dh + 1)[:, hd, :]
                                if k == 1:
                                    for kt in range(t + 1):
                                        mm = pe.matmul(o, pr[:, kt, tile[t]], v[:, kt, hd, :],
                                                       start=(kt == 0), stop=(kt == t))
                                elif t < NT - 1:
                                    for kt in range(NT):
                                        n = P if kt < NT - 1 else P - LAT
                                        mm = pe.matmul(o, pr[0:n, kt, tile[t]], v[0:n, kt, hd, :],
                                                       start=(kt == 0), stop=(kt == NT - 1))
                                else:
                                    for kt in range(NT):
                                        n = P if kt < NT - 1 else P - LAT
                                        pe.matmul(o[0:P - LAT], pr[0:n, kt, t * P:CTX], v[0:n, kt, hd, :],
                                                  start=(kt == 0), stop=(kt == NT - 1))
                                    for kt in range(NT):
                                        mm = pe.matmul(o[P - LAT:P], pr[:, kt, CTX:T], v[:, kt, hd, :],
                                                       start=(kt == 0), stop=(kt == NT - 1))
                            mm.then_inc(heads_done, 1)

                        for hd in range(per_block):
                            maxima(hd)
                        for hd in range(heads):
                            scores(hd)
                            if hd + per_block < heads:
                                maxima(hd + per_block)
                            if hd:
                                apply(hd - 1)
                        apply(heads - 1)
                        two_halves("att_t", k, att, (att_ready, NT * k))
                        halves_ready("att_t", k)

                    for t in range(2):
                        pe.matmul(fill_v("patch", t)[:, 0:D], patches_t[:, t, :],
                                  own_proj[:, bass.ds(image, 1), :].rearrange("p a d -> p (a d)"),
                                  start=True, stop=True).then_inc(v_full, 1)
                    two_halves("xt", 0, xn, (xn_ready, 0))
                    halves_ready("xt", 0)
                    for t in range(NT):
                        project(fill_v("qk", 0, t)[:, 0:2 * D], xt, tile[t], w_qkv, slice(0, 2 * D), 0
                                ).then_inc(v_full, 1)
                    attention(0, H0, 4, DH0, qk0, v0, 0)
                    for t in range(NT):
                        bank = fill_v("out", 0, t)
                        if t < NT - 1:
                            mm = project(bank[:, 0:D], att_t, tile[t], w_octx, slice(0, D), 1)
                        else:
                            project(bank[0:P - LAT, 0:D], att_t, slice(t * P, CTX), w_octx, slice(0, D), 1)
                            mm = project(bank[P - LAT:P, 0:D], att_t, slice(CTX, T), w_olat, slice(0, D), 1)
                        mm.then_inc(v_full, 1)

                    two_halves("xt", 1, xn, (xn_ready, NT))
                    halves_ready("xt", 1)
                    bank = fill_v("logits", 0)
                    for t in range(NT):
                        mm = project(bank[:, 8 * t:8 * t + E0], xt, tile[t], w_router, slice(0, E0), 1)
                    mm.then_inc(v_full, 1)

                    def down(e):
                        emptied_v("up", e, 1)
                        for t in range(NT):
                            bank = fill_v("down", e, t)
                            for m in range(2):
                                mm = pe.matmul(bank[:, 0:D], hid[:, e % 2, m, tile[t]], w_down[:, m, e, :],
                                               start=(m == 0), stop=(m == 1))
                            mm.then_inc(v_full, 1)

                    for e in range(E0):
                        for m in range(2):
                            for w, bank, full in ((w_gate, fill_a("gate", e, m), a_full), (w_up, None, v_full)):
                                if bank is None:
                                    bank = fill_v("up", e, m)
                                for half in range(2):
                                    mm = pe.matmul(bank[:, 0:T], w[:, half, e, m * P:(m + 1) * P],
                                                   xt[0:KH, half, :], start=(half == 0), stop=(half == 1))
                                mm.then_inc(full, 1)
                        if e:
                            down(e - 1)
                    down(E0 - 1)

                    two_halves("xt", 2, xn, (xn_ready, 2 * NT))
                    halves_ready("xt", 2)
                    for w, bank, rows, full in ((w_a, fill_a("r_qk"), 64 + RANK, a_full),
                                                (w_va, fill_v("r_v"), RANK, v_full)):
                        for half in range(2):
                            mm = pe.matmul(bank[0:rows, 0:T], w[:, half, :], xt[0:KH, half, :],
                                           start=(half == 0), stop=(half == 1))
                        mm.then_inc(full, 1)
                    emptied_a("r_qk")
                    emptied_v("r_v")
                    for t in range(NT):
                        bank = fill_v("qk", 1, t)
                        pe.matmul(bank[:, 0:2 * D], r_qk[:, tile[t]], w_b[:], start=True, stop=True
                                  ).then_inc(v_full, 1)
                        pe.matmul(fill_a("v1", t)[:, 0:D], r_v[:, tile[t]], w_vb[:], start=True, stop=True
                                  ).then_inc(a_full, 1)
                    attention(1, H1, 2, DH1, qk1, v1, H0)
                    for t in range(NT):
                        project(fill_v("out", 1, t)[:, 0:D], att_t, tile[t], w_o1, slice(0, D), 0
                                ).then_inc(v_full, 1)

                    two_halves("xt", 3, xn, (xn_ready, 3 * NT))
                    halves_ready("xt", 3)
                    bank = fill_v("logits", 1)
                    for t in range(NT):
                        mm = project(bank[:, 8 * t:8 * t + E1], xt, tile[t], w_g1, slice(0, E1), 0)
                    mm.then_inc(v_full, 1)
                    pe.wait_ge(oh_ready, 1)
                    bank = fill_v("rank")
                    for t in range(NT):
                        o = bank[:, 16 * t:16 * t + 16]
                        pe.matmul(o, before[:], ohb[:, t, :], start=True, stop=False)
                        for u in range(t):
                            pe.matmul(o, onesb[:], ohb[:, u, :], start=False, stop=False)
                        mm = pe.matmul(o, onesb[:], seenb[:], start=False, stop=True)
                    mm.then_inc(v_full, 1)

                @block.vector
                def _(dve):
                    steps = 0

                    def step(ins):
                        nonlocal steps
                        steps += 1
                        ins.then_inc(dve_step, 1)

                    def done():
                        dve.wait_ge(dve_step, steps)

                    def full(*what):
                        dve.wait_ge(v_full, V[what] + 1)
                        return bank_v[V[what] % NV]

                    def written(*what):
                        dve.wait_ge(v_free, V[what] + 1)

                    def normalise(k):
                        for t in range(NT):
                            step(dve.bn_stats(st6[:, t, :], h[:, t, :]))
                        done()
                        for t in range(NT):
                            step(dve.bn_aggr(mv[:, t, :], st6[:, t, :]))
                        done()
                        dve.tensor_scalar(ve[:], mv[:, :, 1], EPS, None, ALU.add).then_inc(var_ready, 1)
                        dve.wait_ge(rstd_ready, k + 1)
                        for t in range(NT):
                            dve.tensor_scalar(xn[:, t, :], h[:, t, :], mv[:, t, 0:1], rstd[:, t:t + 1],
                                              ALU.subtract, ALU.mult).then_inc(xn_ready, 1)
                        dve.tensor_copy(xt[0:KH, 1, :], full("xt", k)[0:KH, 0:T]).then_inc(v_free, 1)

                    def rope_products(k):
                        dh = (DH0, DH1)[k]
                        g, half = 2 * D // dh, dh // 2
                        for t in range(NT):
                            x = full("qk", k, t)[:, 0:2 * D].rearrange("p (g d) -> p g d", d=dh)
                            cos = c(f"cos{k}", dh)[:, t, :].unsqueeze(1)
                            sin = c(f"sin{k}", dh)[:, t, :].unsqueeze(1)
                            a = rope_a[:, t, :].rearrange("p (g d) -> p g d", d=dh)
                            b = rope_b[:, t, :].rearrange("p (g d) -> p g d", d=dh)
                            step(dve.tensor_tensor(a, x, cos.to_broadcast([P, g, dh]), ALU.mult))
                            step(dve.tensor_tensor(b[:, :, 0:half], x[:, :, half:dh],
                                                   sin[:, :, 0:half].to_broadcast([P, g, half]), ALU.mult))
                            done()
                            dve.tensor_tensor(b[:, :, half:dh], x[:, :, 0:half],
                                              sin[:, :, half:dh].to_broadcast([P, g, half]), ALU.mult
                                              ).then_inc(v_free, 1)

                    def queries_rounded(k):
                        for b in range(3):
                            dve.tensor_copy(q_round[:, b, :], full("q_round", k, b)[:, 0:T]).then_inc(v_free, 1)

                    def maxima(k, heads, dh, width, qk):
                        for hd in range(heads):
                            for t in range(NT):
                                bank = full("max", k, hd, t)
                                to = qk[:, t, 0, hd * width + dh:hd * width + dh + 1]
                                if k == 0 and t == NT - 1:
                                    step(dve.tensor_reduce(to[P - LAT:P], bank[P - LAT:P, 0:T], AX.X, ALU.max,
                                                           negate=True))
                                    done()
                                    dve.tensor_reduce(to[0:P - LAT], bank[0:P - LAT, 0:CTX], AX.X, ALU.max,
                                                      negate=True).then_inc(v_free, 1)
                                else:
                                    keys = (t + 1) * P if k == 1 else CTX
                                    dve.tensor_reduce(to, bank[:, 0:keys], AX.X, ALU.max, negate=True
                                                      ).then_inc(v_free, 1)

                    def attention_out(k, heads, dh, before):
                        dve.wait_ge(heads_done, before + heads)
                        for t in range(NT):
                            o = out_of(t, heads, dh + 1)
                            step(dve.reciprocal(rsum[:, t, 0:heads], o[:, :, dh]))
                        done()
                        for t in range(NT):
                            o = out_of(t, heads, dh + 1)
                            dve.tensor_tensor(att[:, t, :].rearrange("p (h d) -> p h d", d=dh), o[:, :, 0:dh],
                                              rsum[:, t, 0:heads].unsqueeze(2).to_broadcast([P, heads, dh]),
                                              ALU.mult).then_inc(att_ready, 1)
                        dve.tensor_copy(att_t[0:KH, 1, :], full("att_t", k)[0:KH, 0:T]).then_inc(v_free, 1)
                        for t in range(NT):
                            dve.tensor_tensor(h[:, t, :], full("out", k, t)[:, 0:D], h[:, t, :], ALU.add
                                              ).then_inc(v_free, 1)
                        written("out", k, NT - 1)

                    def choose(k, experts):
                        dve.tensor_copy(lg[k][:, :, 0:experts],
                                        full("logits", k)[:, 0:8 * NT].rearrange("p (t e) -> p t e", e=8)
                                        [:, :, 0:experts]).then_inc(v_free, 1)
                        written("logits", k)
                        for t in range(NT):
                            step(dve.max(top[:, t, :], lg[k][:, t, :]))
                        done()
                        dve.tensor_tensor(dl[:], top[:, :, 1], top[:, :, 0], ALU.subtract).then_inc(dl_ready, 1)
                        for t in range(NT):
                            step(dve.max_index(topi[:, t, :], top[:, t, :], lg[k][:, t, :]))
                        done()
                        step(dve.tensor_copy(topf[:], topi[:, :, 0:2]))
                        done()
                        step(dve.tensor_tensor(
                            oh[:].rearrange("p t k e -> p (t k) e"),
                            c("iota").unsqueeze(1).to_broadcast([P, 2 * NT, 8]),
                            topf[:].rearrange("p t k -> p (t k)").unsqueeze(2).to_broadcast([P, 2 * NT, 8]),
                            ALU.is_equal))
                        dve.wait_ge(ed_ready, k + 1)
                        step(dve.tensor_scalar(ed1[:], ed[:], 1.0, None, ALU.add))
                        done()
                        step(dve.reciprocal(wk[:, :, 0], ed1[:]))
                        done()
                        step(dve.tensor_tensor(wk[:, :, 1], ed[:], wk[:, :, 0], ALU.mult))
                        done()

                    for t in range(2):
                        dve.tensor_copy(h[:, t, :], full("patch", t)[:, 0:D]).then_inc(v_free, 1)
                    written("patch", 1)
                    dve.wait_ge(emb_ready, 1)
                    normalise(0)
                    rope_products(0)
                    queries_rounded(0)
                    keys = qk0[:, :, 1, :].rearrange("p t (h d) -> p t h d", d=32)[:, :, :, 0:DH0]
                    tiled = lambda ap: ap.rearrange("p (t h) -> p t h", h=H0)
                    step(dve.tensor_reduce(tiled(vsum[:]), keys, AX.X, ALU.add))
                    done()
                    for t in range(NT):
                        dve.scalar_tensor_tensor(
                            vcen[:, t * H0:(t + 1) * H0, :],
                            vsum[:, t * H0:(t + 1) * H0].unsqueeze(2).to_broadcast([P, H0, DH0]), -1.0 / DH0,
                            keys[:, t], ALU.mult, ALU.add).then_inc(vcen_ready, 1)
                    dve.wait_ge(vsq_ready, 1)
                    step(dve.tensor_reduce(vms[:], vsq[:], AX.X, ALU.add))
                    done()
                    dve.tensor_scalar(vvar[:], vms[:], 1.0 / DH0, EPS, ALU.mult, ALU.add).then_inc(vvar_ready, 1)
                    dve.wait_ge(vrstd_ready, 1)
                    vv = v0[:].rearrange("p t h d -> p (t h) d")[:, :, 0:DH0]
                    step(dve.tensor_tensor(vv, vcen[:], vrstd[:].unsqueeze(2).to_broadcast([P, NT * H0, DH0]),
                                           ALU.mult))
                    done()
                    step(dve.tensor_tensor(vv, vv, lng[:].unsqueeze(1).to_broadcast([P, NT * H0, DH0]), ALU.mult))
                    done()
                    dve.tensor_tensor(vv, vv, lnb[:].unsqueeze(1).to_broadcast([P, NT * H0, DH0]), ALU.add
                                      ).then_inc(v0_ready, 1)
                    maxima(0, H0, DH0, 32, qk0)
                    attention_out(0, H0, DH0, 0)

                    normalise(1)
                    choose(0, E0)
                    step(dve.tensor_tensor(ohw[:], oh[:], wk[:].unsqueeze(3).to_broadcast([P, NT, 2, 8]), ALU.mult))
                    done()
                    step(dve.tensor_tensor(comb[:], ohw[:, :, 0, :], ohw[:, :, 1, :], ALU.add))
                    done()

                    def down(e):
                        for t in range(NT):
                            if e:
                                written("down", e - 1, t)
                            dve.scalar_tensor_tensor(h[:, t, :], full("down", e, t)[:, 0:D], comb[:, t, e:e + 1],
                                                     h[:, t, :], ALU.mult, ALU.add).then_inc(v_free, 1)

                    for e in range(E0):
                        for m in range(2):
                            bank = full("up", e, m)
                            dve.wait_ge(a_free, A["gate", e, m] + 1)
                            dve.tensor_tensor(hid[:, e % 2, m, :], bank[:, 0:T], silu[:, m, :], ALU.mult
                                              ).then_inc(v_free, 1)
                        if e:
                            down(e - 1)
                    down(E0 - 1)
                    written("down", E0 - 1, NT - 1)

                    normalise(2)
                    dve.tensor_copy(r_v[:], full("r_v")[0:RANK, 0:T]).then_inc(v_free, 1)
                    rope_products(1)
                    queries_rounded(1)
                    maxima(1, H1, DH1, 64, qk1)
                    attention_out(1, H1, DH1, H0)

                    normalise(3)
                    choose(1, E1)
                    step(dve.tensor_copy(seenb[:], seen[:]))
                    done()
                    dve.tensor_copy(ohb[:], oh[:].rearrange("p t k e -> p t (k e)")).then_inc(oh_ready, 1)
                    for t in range(NT):
                        done()
                        step(dve.tensor_tensor(seen[:], seen[:], oh[:, t].rearrange("p k e -> p (k e)"), ALU.add))
                    step(dve.tensor_tensor(
                        ohbase[:].rearrange("p t k e -> p t (k e)"), oh[:].rearrange("p t k e -> p t (k e)"),
                        c("base").unsqueeze(1).to_broadcast([P, NT, 16]), ALU.mult))
                    done()
                    step(dve.tensor_reduce(bases[:], ohbase[:], AX.X, ALU.add))
                    bank = full("rank")
                    dve.tensor_tensor(ohw[:].rearrange("p t k e -> p (t k e)"), bank[:, 0:16 * NT],
                                      oh[:].rearrange("p t k e -> p (t k e)"), ALU.mult).then_inc(v_free, 1)
                    written("rank")
                    step(dve.tensor_reduce(rank[:], ohw[:], AX.X, ALU.add))
                    done()
                    step(dve.tensor_scalar(keep[:], rank[:], float(CAP), None, ALU.is_lt))
                    step(dve.tensor_tensor(place[:], rank[:], bases[:], ALU.add))
                    done()
                    step(dve.tensor_tensor(off[:], place[:], drop[:], ALU.subtract))
                    step(dve.tensor_tensor(kept[:], place[:], keep[:], ALU.mult))
                    step(dve.tensor_tensor(weights_all[:, bass.ds(image * (2 * NT), 2 * NT)],
                                           wk[:].rearrange("p t k -> p (t k)"),
                                           keep[:].rearrange("p t k -> p (t k)"), ALU.mult))
                    done()
                    step(dve.tensor_copy(slots_all[:, bass.ds(image * (2 * NT), 2 * NT)],
                                         kept[:].rearrange("p t k -> p (t k)")))
                    step(dve.tensor_tensor(place[:], off[:], keep[:], ALU.mult))
                    done()
                    dve.tensor_tensor(slot_i[:].rearrange("p (t k) -> p t k", k=2), place[:], drop[:], ALU.add
                                      ).then_inc(slot_ready, 1)
                    dve.wait_ge(slot_ready, 1)
                    step(dve.tensor_scalar(drop[:], drop[:], float(T), None, ALU.add))
                    done()
            nc.all_engine_barrier(sems_to_clear=per_image)


def expert_stage(nc, w1, w2, xs_dram, y_dram, ident):
    NX = 3
    with ExitStack() as ctx:
        def sb(name, shape, dt=F32):
            return ctx.enter_context(nc.sbuf_tensor(name, shape, dt))

        def sem(name):
            return ctx.enter_context(nc.semaphore(name))

        w_in = sb("w_in", [KH, 2, 2 * HF])
        w_out = sb("w_out", [P, HF // P, D])
        rows = sb("rows", [P, NX, NT, D])
        rows_t = sb("rows_t", [KH, 2, 2, T])
        gated = sb("gated", [P, 2, T])
        hid = sb("e_hid", [P, 2, HF // P, T])
        res = sb("res", [P, 2, NT, D])
        bank_a = [ctx.enter_context(nc.psum_tensor(f"e_bank_a{i}", [P, 512], F32)) for i in range(4)]
        bank_v = [ctx.enter_context(nc.psum_tensor(f"e_bank_v{i}", [P, 512], F32)) for i in range(4)]

        w_loaded = sem("w_loaded")
        rows_in = [sem(f"rows_in{i}") for i in range(NX)]
        ea_full, ea_free, ev_full, ev_free = sem("ea_full"), sem("ea_free"), sem("ev_full"), sem("ev_free")
        stored = [sem(f"stored{i}") for i in range(2)]
        per_expert = range(w_loaded.num, ev_free.num + 1)
        of_buffer = [len(range(i, NCHUNK, 2)) for i in range(2)]

        NM = HF // P
        a, v = [("x", 0)], [("x", 0)]
        for ch in range(NCHUNK):
            a += [("b", ch, m) for m in range(NM)]
            v += [("a", ch, m) for m in range(NM)]
            if ch + 1 < NCHUNK:
                a.append(("x", ch + 1))
                v.append(("x", ch + 1))
            a += [("y", ch, t) for t in range(NT)]
        ea = {what: n for n, what in enumerate(a)}
        ev = {what: n for n, what in enumerate(v)}

        with nc.Fori(0, E1) as expert:
            with nc.Block(no_gpsimd_drain=True) as block:

                @block.sync
                def _(sp):
                    xs = xs_dram[0:NROWS, :].rearrange("(e c t p) d -> p e c t d", e=E1, c=NCHUNK, p=P)
                    sp.dma_start(w_in[:].unsqueeze(1),
                                 w1.rearrange("e (k p) n -> p e k n", p=KH)[:, bass.ds(expert, 1)]
                                 ).then_inc(w_loaded, 16)
                    for ch in range(NCHUNK):
                        if ch >= NX:
                            sp.wait_ge(ev_full, ev["x", ch - NX] + 1)
                        for t in range(NT):
                            sp.dma_start(rows[:, ch % NX, t, :].unsqueeze(1), xs[:, bass.ds(expert, 1), ch, t]
                                         ).then_inc(rows_in[ch % NX], 16)
                        if ch == 0:
                            sp.dma_start(w_out[:].unsqueeze(1),
                                         w2.rearrange("e (k p) n -> p e k n", p=P)[:, bass.ds(expert, 1)]
                                         ).then_inc(w_loaded, 16)

                @block.gpsimd
                def _(pool):
                    ys = y_dram.rearrange("(e c t p) d -> p e c t d", e=E1, c=NCHUNK, p=P)
                    for ch in range(NCHUNK):
                        pool.wait_ge(ea_free, ea["y", ch, NT - 1] + 1)
                        pool.dma_start(ys[:, bass.ds(expert, 1), ch], res[:, ch % 2].unsqueeze(1)
                                       ).then_inc(stored[ch % 2], 16)
                    for i in range(2):
                        pool.wait_ge(stored[i], (expert + 1) * (16 * of_buffer[i]))

                @block.tensor
                def _(pe):
                    def fill_a(*what):
                        if ea[what] >= 4:
                            pe.wait_ge(ea_free, ea[what] - 4 + 1)
                        return bank_a[ea[what] % 4]

                    def fill_v(*what):
                        if ev[what] >= 4:
                            pe.wait_ge(ev_free, ev[what] - 4 + 1)
                        return bank_v[ev[what] % 4]

                    def down(ch):
                        pe.wait_ge(ev_free, ev["a", ch, NM - 1] + 1)
                        for t in range(NT):
                            bank = fill_a("y", ch, t)
                            for m in range(NM):
                                mm = pe.matmul(bank[:, 0:D], hid[:, ch % 2, m, t * P:(t + 1) * P], w_out[:, m, :],
                                               start=(m == 0), stop=(m == NM - 1))
                            mm.then_inc(ea_full, 1)

                    def transpose_rows(ch):
                        pe.wait_ge(rows_in[ch % NX], 16 * NT * (ch // NX + 1))
                        bank = fill_a("x", ch)
                        for t in range(NT):
                            mm = pe.transpose(bank[0:KH, t * P:(t + 1) * P], rows[:, ch % NX, t, 0:KH], ident[:])
                        mm.then_inc(ea_full, 1)
                        bank = fill_v("x", ch)
                        for t in range(NT):
                            mm = pe.transpose(bank[0:KH, t * P:(t + 1) * P], rows[:, ch % NX, t, KH:D], ident[:])
                        mm.then_inc(ev_full, 1)

                    transpose_rows(0)
                    pe.wait_ge(w_loaded, 32)
                    for ch in range(NCHUNK):
                        pe.wait_ge(ea_free, ea["x", ch] + 1)
                        pe.wait_ge(ev_free, ev["x", ch] + 1)
                        for m in range(NM):
                            for at, bank, full in ((HF + m * P, fill_a("b", ch, m), ea_full), (m * P, None, ev_full)):
                                if bank is None:
                                    bank = fill_v("a", ch, m)
                                for half in range(2):
                                    mm = pe.matmul(bank[:, 0:T], w_in[:, half, at:at + P], rows_t[:, ch % 2, half, :],
                                                   start=(half == 0), stop=(half == 1))
                                mm.then_inc(full, 1)
                        if ch + 1 < NCHUNK:
                            transpose_rows(ch + 1)
                        down(ch)

                @block.scalar
                def _(act):
                    def full(*what):
                        act.wait_ge(ea_full, ea[what] + 1)
                        return bank_a[ea[what] % 4]

                    def results(ch):
                        if ch >= 2:
                            act.wait_ge(stored[ch % 2], expert * (16 * of_buffer[ch % 2]) + 16 * (ch // 2))
                        for t in range(NT):
                            act.activation(res[:, ch % 2, t, :], full("y", ch, t)[:, 0:D], ACT.Copy
                                           ).then_inc(ea_free, 1)

                    def half_transposed(ch):
                        act.activation(rows_t[:, ch % 2, 0, :], full("x", ch)[0:KH, 0:T], ACT.Copy
                                       ).then_inc(ea_free, 1)

                    half_transposed(0)
                    for ch in range(NCHUNK):
                        for m in range(NM):
                            if m >= 2:
                                act.wait_ge(ev_free, ev["a", ch, m - 2] + 1)
                            elif ch:
                                act.wait_ge(ev_free, ev["a", ch - 1, m + NM - 2] + 1)
                            act.activation(gated[:, m % 2, :], full("b", ch, m)[:, 0:T], ACT.Silu
                                           ).then_inc(ea_free, 1)
                        if ch + 1 < NCHUNK:
                            half_transposed(ch + 1)
                        results(ch)

                @block.vector
                def _(dve):
                    def full(*what):
                        dve.wait_ge(ev_full, ev[what] + 1)
                        return bank_v[ev[what] % 4]

                    def half_transposed(ch):
                        dve.tensor_copy(rows_t[:, ch % 2, 1, :], full("x", ch)[0:KH, 0:T]).then_inc(ev_free, 1)

                    half_transposed(0)
                    for ch in range(NCHUNK):
                        for m in range(NM):
                            bank = full("a", ch, m)
                            dve.wait_ge(ea_free, ea["b", ch, m] + 1)
                            dve.tensor_tensor(hid[:, ch % 2, m, :], bank[:, 0:T], gated[:, m % 2, :], ALU.mult
                                              ).then_inc(ev_free, 1)
                        if ch + 1 < NCHUNK:
                            half_transposed(ch + 1)
            nc.all_engine_barrier(sems_to_clear=per_expert)


def combine_stage(nc, y_dram, h_dram, out, slots_all, weights_all):
    TI = CIMG * NT
    with ExitStack() as ctx:
        def sb(name, shape, dt=F32):
            return ctx.enter_context(nc.sbuf_tensor(name, shape, dt))

        def sem(name):
            return ctx.enter_context(nc.semaphore(name))

        idx = sb("c_idx", [P, 2 * TI], I32)
        wts = sb("c_wts", [P, 2 * TI])
        hrow = sb("hrow", [P, TI, D])
        y = sb("y", [P, TI, 2, D])
        part = sb("part", [P, TI, D])
        y_in = [sem(f"y_in{t}") for t in range(TI)]
        idx_copied, wts_copied, h_in = sem("idx_copied"), sem("wts_copied"), sem("h_in")
        first_added, both_added, out_stored = sem("first_added"), sem("both_added"), sem("out_stored")
        per_step = range(idx_copied.num, out_stored.num + 1)
        tiles = lambda ap: ap.rearrange("(s t p) d -> p s t d", t=TI, p=P)

        with nc.Fori(0, B // CIMG) as group:
            with nc.Block(no_gpsimd_drain=True) as block:

                @block.gpsimd
                def _(pool):
                    pool.tensor_copy(idx[:], slots_all[:, bass.ds(group * (2 * TI), 2 * TI)]).then_inc(idx_copied, 1)
                    pool.wait_ge(idx_copied, 1)
                    for t in range(TI):
                        for k in range(2):
                            pool.indirect_dma_start(
                                y[:, t, k, :], None, y_dram,
                                bass.IndirectOffsetOnAxis(ap=idx[:, 2 * t + k:2 * t + k + 1], axis=0)
                            ).then_inc(y_in[t], 16)

                @block.sync
                def _(sp):
                    sp.dma_start(hrow[:].unsqueeze(1), tiles(h_dram)[:, bass.ds(group, 1)]).then_inc(h_in, 16)
                    sp.wait_ge(both_added, TI)
                    sp.dma_start(tiles(out)[:, bass.ds(group, 1)], hrow[:].unsqueeze(1)).then_inc(out_stored, 16)
                    sp.wait_ge(out_stored, 16)

                @block.vector
                def _(dve):
                    dve.tensor_copy(wts[:], weights_all[:, bass.ds(group * (2 * TI), 2 * TI)]
                                    ).then_inc(wts_copied, 1)
                    dve.wait_ge(wts_copied, 1)
                    dve.wait_ge(h_in, 16)
                    for t in range(TI):
                        dve.wait_ge(y_in[t], (group + 1) * 32)
                        dve.scalar_tensor_tensor(part[:, t, :], y[:, t, 0, :], wts[:, 2 * t:2 * t + 1], hrow[:, t, :],
                                                 ALU.mult, ALU.add).then_inc(first_added, 1)
                        dve.wait_ge(first_added, t + 1)
                        dve.scalar_tensor_tensor(hrow[:, t, :], y[:, t, 1, :], wts[:, 2 * t + 1:2 * t + 2],
                                                 part[:, t, :], ALU.mult, ALU.add).then_inc(both_added, 1)
            nc.all_engine_barrier(sems_to_clear=per_step)


def kernel(x, x_txt, mask_BS_i2_0, L0_tok_curve, L0_tok_proj_w, L0_tok_proj_b, L0_txt_token_table,
           L0_txt_segm_table, L0_attn_Wq, L0_attn_Wkv, L0_attn_Wo_ctx, L0_attn_bo_ctx, L0_attn_Wo_lat,
           L0_attn_bo_lat, L0_attn_ln_g, L0_attn_ln_b, L0_ffn_router_w, L0_ffn_router_b, L0_ffn_gate_w,
           L0_ffn_up_w, L0_ffn_down_w, L1_attn_qA, L1_attn_qB, L1_attn_kA, L1_attn_kB, L1_attn_vA,
           L1_attn_vB, L1_attn_o_w, L1_ffn_Wg, L1_ffn_W1, L1_ffn_W2):
    import numpy as np
    import concourse.bacc as bacc
    from concourse.bass_utils import run_bass_kernel_spmd

    a = np.asarray
    arrays = {
        "consts": constants(),
        "img": a(x).transpose(2, 3, 0, 1).reshape(IMG * IMG, 3 * B),
        "txt": a(x_txt).T, "seg": a(mask_BS_i2_0).T, "curve": a(L0_tok_curve),
        "projw": a(L0_tok_proj_w).T, "projb": a(L0_tok_proj_b),
        "tok_table": a(L0_txt_token_table), "seg_table": a(L0_txt_segm_table),
        "wqkv": np.concatenate([a(L0_attn_Wq), a(L0_attn_Wkv)], axis=1),
        "wo_ctx": a(L0_attn_Wo_ctx), "bo_ctx": a(L0_attn_bo_ctx),
        "wo_lat": a(L0_attn_Wo_lat), "bo_lat": a(L0_attn_bo_lat),
        "ln_g": a(L0_attn_ln_g), "ln_b": a(L0_attn_ln_b),
        "router_w": a(L0_ffn_router_w).T, "router_b": a(L0_ffn_router_b),
        "gate_w": a(L0_ffn_gate_w), "up_w": a(L0_ffn_up_w), "down_w": a(L0_ffn_down_w),
        "qa": a(L1_attn_qA), "qb": a(L1_attn_qB), "ka": a(L1_attn_kA), "kb": a(L1_attn_kB),
        "va": a(L1_attn_vA), "vb": a(L1_attn_vB), "ow": a(L1_attn_o_w),
        "wg": a(L1_ffn_Wg), "w1": a(L1_ffn_W1), "w2": a(L1_ffn_W2),
    }
    arrays = {name: np.ascontiguousarray(value) for name, value in arrays.items()}
    nc = bacc.Bacc("TRN2", target_bir_lowering=False, num_devices=1)
    args = [nc.dram_tensor(f"in_{name}", value.shape, mybir.dt.from_np(value.dtype), kind="ExternalInput").ap()
            for name, value in arrays.items()]
    out = nc.dram_tensor("out_tokens", (N, D), F32, kind="ExternalOutput").ap()
    early_fusion_kernel(nc, *args, out)
    got = run_bass_kernel_spmd(nc, [{f"in_{name}": value for name, value in arrays.items()}], core_ids=[0])
    return np.asarray(got.results[0]["out_tokens"]).reshape(B, T, D)
```

```python
from contextlib import ExitStack

import concourse.bass as bass
from concourse import mybir

F32 = mybir.dt.float32
F32R = mybir.dt.float32r
BF16 = mybir.dt.bfloat16
I32 = mybir.dt.int32
U32 = mybir.dt.uint32
ALU = mybir.AluOpType
ACT = mybir.ActivationFunctionType
AX = mybir.AxisListType

P = 128
D = 192
KH = D // 2
B = 32
NVIS, NTXT = 256, 128
T = NVIS + NTXT
NT = T // P
LAT = 32
CTX = T - LAT
N = B * T
VOCAB, NSEG, IMG = 8000, 3, 128
H0, DH0 = 12, 16
H1, DH1, RANK = 6, 32, 48
QKW = 384
E0, I0 = 5, 256
E1, HF = 8, 512
CAP = int(1.2 * N / E1)
EROWS = -(-2 * CAP // T) * T
NCHUNK = EROWS // T
NROWS = E1 * EROWS
EPS = 1e-5
NEG = -1e30
NA, NV = 3, 3
PTH = 3
CIMG = 4
HEADS, DHS = (H0, H1), (DH0, DH1)
PER_BLOCK = (4, 2)
AHEAD = (6, 4)
PHASES = ((1, 1, 1), (0, 15, 13), (10, 10, 18), (0, None, None))
STREAM_OF_NORM = (0, 0, 1, 2)

_COLS = {}
_w = 0
for _name, _n in (("ident", P), ("maskq", P), ("maskt", P), ("before", P), ("pos", D),
                  ("cos0", NT * DH0), ("sin0", NT * DH0), ("cos1", NT * DH1), ("sin1", NT * DH1),
                  ("iota", E1), ("base", 2 * E1), ("drop", 2 * NT), ("own", B)):
    _COLS[_name] = slice(_w, _w + _n)
    _w += _n
NCOLS = _w


def constants():
    import numpy as np

    c = np.zeros((P, NCOLS), np.float32)
    p = np.arange(P)
    c[:, _COLS["ident"]] = np.eye(P)
    c[:, _COLS["maskq"]] = np.where(p[None, :] <= p[:, None], 0.0, NEG)
    c[:, _COLS["maskt"]] = np.where(p[:, None] <= p[None, :], 0.0, NEG)
    c[:, _COLS["before"]] = p[:, None] < p[None, :]
    ids = np.arange(D, dtype=np.float32)
    angle = p.astype(np.float32)[:, None] / np.power(
        np.float32(10000.0), np.floor(ids / np.float32(2)) * np.float32(2) / np.float32(D)).astype(np.float32)[None]
    c[:, _COLS["pos"]] = np.where(np.arange(D) % 2 == 0, np.sin(angle.astype(np.float64)),
                                  np.cos(angle.astype(np.float64)))
    for name, dh in (("0", DH0), ("1", DH1)):
        inv = (np.float32(1.0) / np.power(np.float32(10000.0), np.arange(0, dh, 2, dtype=np.float32)
                                          / np.float32(dh))).astype(np.float32)
        f = (np.arange(T, dtype=np.float32)[:, None] * inv[None, :]).astype(np.float32).astype(np.float64)
        cos = np.concatenate([np.cos(f), np.cos(f)], 1).reshape(NT, P, dh).transpose(1, 0, 2)
        sin = np.concatenate([-np.sin(f), np.sin(f)], 1).reshape(NT, P, dh).transpose(1, 0, 2)
        c[:, _COLS["cos" + name]] = cos.reshape(P, -1)
        c[:, _COLS["sin" + name]] = sin.reshape(P, -1)
    c[:, _COLS["iota"]] = np.arange(E1)[None]
    c[:, _COLS["base"]] = (np.arange(2)[:, None] * CAP + np.arange(E1)[None] * EROWS).reshape(1, -1)
    c[:, _COLS["drop"]] = (NROWS + np.arange(NT)[None, :, None] * P + p[:, None, None]
                           + np.arange(2)[None, None, :] * N).reshape(P, -1)
    c[:3 * B, _COLS["own"]] = np.repeat(np.eye(B), 3, axis=0)
    c[3 * B, _COLS["own"]] = 1.0
    return c


def units():
    x = ([("rows",), ("patches",), ("stats", 0), ("xn", 0), ("xt", 0)] + [("qk", 0, t) for t in range(NT)]
         + [("blocks", 0, b) for b in range(3)] + [("values", n) for n in range(3)]
         + [("maxima", 0, hd) for hd in range(AHEAD[0])] + [("head", 0, hd) for hd in range(H0)]
         + [("last", 0)] + [("sums", 0, t) for t in range(NT)] + [("att_t", 0), ("out", 0), ("stats", 1), ("xn", 1), ("xt", 1), ("logits", 0),
            ("exp", 0), ("weights", 0)])
    y = [("carry", 1)]
    for e in range(E0):
        y += [("ffn", e, m) for m in range(2)] + [("down", e - 1)] * (e > 0)
    y += [("down", E0 - 1), ("stats", 2), ("xn", 2), ("xt", 2), ("low_rank",)]
    y += [("qk", 1, t) for t in range(NT)] + [("blocks", 1, b) for b in range(3)]
    y += [("maxima", 1, hd) for hd in range(AHEAD[1])] + [("head", 1, hd) for hd in range(H1)]
    y += [("last", 1)] + [("sums", 1, t) for t in range(NT)]
    z = [("carry", 2), ("att_t", 1), ("out", 1), ("stats", 3), ("xn", 3), ("xt", 3), ("logits", 1), ("exp", 1),
         ("weights", 1), ("rank",), ("places",)]
    return {"x": x, "y": y, "z": z}


def schedule(streams):
    todo = {s: list(u) for s, u in units().items()}
    order = []
    for counts in PHASES:
        spread = []
        for s, n in zip("zyx", counts):
            n = len(todo[s]) if n is None else n
            spread += [((i + 0.5) / n, s, todo[s][i]) for i in range(n)]
            todo[s] = todo[s][n:]
        order += [unit for _, s, unit in sorted(spread, key=lambda e: e[0]) if s in streams]
    return order


def bank_plan(order):
    a, v = [], []
    for what, *at in order:
        if what == "patches":
            v += [("patch", t) for t in range(2)]
        elif what in ("xt", "att_t"):
            a.append((what, *at))
            v.append((what, *at))
        elif what == "qk":
            v.append(("qk", *at))
            if at[0] == 1:
                a.append(("v1", at[1]))
        elif what == "blocks":
            v.append(("q_round", *at))
            a.append(("k_t", *at))
        elif what == "maxima":
            v += [("max", *at, t) for t in range(NT)]
        elif what == "head":
            k, hd = at
            if hd % PER_BLOCK[k] == 0:
                a.append(("q_t", k, hd // PER_BLOCK[k]))
            a += [("score", k, hd, t) for t in range(NT)]
            if hd + AHEAD[k] < HEADS[k]:
                v += [("max", k, hd + AHEAD[k], t) for t in range(NT)]
        elif what == "sums":
            v.append(("sums", *at))
        elif what == "out":
            v += [("out", at[0], t) for t in range(NT)]
        elif what == "logits":
            v.append(("logits", at[0]))
        elif what == "ffn":
            a.append(("gate", *at))
            v.append(("up", *at))
        elif what == "down":
            v += [("down", at[0], t) for t in range(NT)]
        elif what == "low_rank":
            a.append(("r_qk",))
            v.append(("r_v",))
        elif what == "rank":
            v.append(("rank",))
    return {what: n for n, what in enumerate(a)}, {what: n for n, what in enumerate(v)}


def early_fusion_kernel(nc, consts, img, txt, seg, curve, projw, projb, tok_table, seg_table, wqkv,
                        wo_ctx, bo_ctx, wo_lat, bo_lat, ln_g, ln_b, router_w, router_b, gate_w, up_w,
                        down_w, qa, qb, ka, kb, va, vb, ow, wg, w1, w2, out):
    xs_dram = nc.dram_tensor("xs_dram", (NROWS + 2 * N, D), F32, kind="Internal").ap()
    y_dram = nc.dram_tensor("y_dram", (NROWS, D), F32, kind="Internal").ap()
    h_dram = nc.dram_tensor("h_dram", (N, D), F32, kind="Internal").ap()

    with ExitStack() as whole:
        slots_all = whole.enter_context(nc.sbuf_tensor("slots_all", [P, B * NT * 2], I32))
        weights_all = whole.enter_context(nc.sbuf_tensor("weights_all", [P, B * NT * 2], F32))
        ident = whole.enter_context(nc.sbuf_tensor("ident", [P, P], F32))
        token_stages(nc, consts, img, txt, seg, curve, projw, projb, tok_table, seg_table, wqkv,
                     wo_ctx, bo_ctx, wo_lat, bo_lat, ln_g, ln_b, router_w, router_b, gate_w, up_w,
                     down_w, qa, qb, ka, kb, va, vb, ow, wg, xs_dram, h_dram, slots_all, weights_all, ident)
        expert_stage(nc, w1, w2, xs_dram, y_dram, ident)
        combine_stage(nc, y_dram, h_dram, out, slots_all, weights_all)


def token_stages(nc, consts, img, txt, seg, curve, projw, projb, tok_table, seg_table, wqkv,
                 wo_ctx, bo_ctx, wo_lat, bo_lat, ln_g, ln_b, router_w, router_b, gate_w, up_w,
                 down_w, qa, qb, ka, kb, va, vb, ow, wg, xs_dram, h_dram, slots_all, weights_all, ident):
    ctx = ExitStack()
    with ctx:
        def sb(name, shape, dt=F32):
            return ctx.enter_context(nc.sbuf_tensor(name, shape, dt))

        def ps(name):
            return ctx.enter_context(nc.psum_tensor(name, [P, 512], F32))

        def sem(name):
            return ctx.enter_context(nc.semaphore(name))

        cst = sb("cst", [P, NCOLS])
        identb = sb("identb", [P, P], BF16)
        maskq = sb("maskq", [P, P], BF16)
        maskt = sb("maskt", [P, P], BF16)
        before = sb("before", [P, P], BF16)
        onesb = sb("onesb", [P, P], BF16)
        pow_half = sb("pow_half", [P, 36])
        zeros = sb("zeros", [P, 1, D])
        w_qkv = sb("w_qkv", [KH, 2, 2 * D])
        w_octx = sb("w_octx", [KH + 1, 2, D])
        w_olat = sb("w_olat", [KH + 1, 2, D])
        w_router = sb("w_router", [KH + 1, 2, E0])
        w_gate = sb("w_gate", [KH, 2, E0, I0])
        w_up = sb("w_up", [KH, 2, E0, I0])
        w_down = sb("w_down", [P, 2, E0, D])
        w_a = sb("w_a", [KH, 2, 64 + RANK])
        w_va = sb("w_va", [KH, 2, RANK])
        w_b = sb("w_b", [64 + RANK, 2 * D])
        w_vb = sb("w_vb", [RANK, D])
        w_o1 = sb("w_o1", [KH, 2, D])
        w_g1 = sb("w_g1", [KH, 2, E1])
        lng = sb("lng", [P, DH0])
        lnb = sb("lnb", [P, DH0])
        proj = sb("proj", [3 * B + 1, D])
        own_proj = sb("own_proj", [3 * B + 1, D])
        curve_i = sb("curve_i", [P, 2, 2], I32)
        curve_f = sb("curve_f", [P, 2, 2])
        pix_f = sb("pix_f", [P, 2])
        pix_i = sb("pix_i", [P, 2], I32)
        ids_i = sb("ids_i", [P, 2, B], I32)
        ids_f = sb("ids_f", [P, 2, B])
        patches = sb("patches", [P, 2, 3 * B])
        patches_t = sb("patches_t", [3 * B + 1, 2, P])

        idx = sb("idx", [P, 2], I32)
        tokrow = sb("tokrow", [P, D])
        segrow = sb("segrow", [P, D])
        embsum = sb("embsum", [P, D])
        h = [sb(f"h_{s}", [P, NT, D]) for s in "xyz"]
        st6 = [sb(f"st6{k}", [P, NT, 6]) for k in range(4)]
        mv = [sb(f"mv{k}", [P, NT, 2]) for k in range(4)]
        ve = [sb(f"ve{k}", [P, NT]) for k in range(4)]
        rstd = [sb(f"rstd{k}", [P, NT]) for k in range(4)]
        xn_of = [sb(f"xn_{s}", [P, NT, D]) for s in "xyz"]
        xn = [xn_of[s] for s in STREAM_OF_NORM]
        xt_of = [sb(f"xt{i}", [KH + 1, 2, T]) for i in range(2)]
        xt = [xt_of[i] for i in (0, 1, 1, 0)]
        rope_a = sb("rope_a", [P, NT, 2 * D])
        rope_b = sb("rope_b", [P, NT, 2 * D])
        qk0 = sb("qk0", [P, NT, 2, QKW])
        qk1 = sb("qk1", [P, NT, 2, QKW])
        q_round = [sb(f"q_round{k}", [P, 3, T], F32R) for k in range(2)]
        k_round = [sb(f"k_round{k}", [P, 3, T], F32R) for k in range(2)]
        q_t = [sb(f"q_t{k}", [P, 3, T]) for k in range(2)]
        k_t = [sb(f"k_t{k}", [P, 3, T]) for k in range(2)]
        probs = sb("probs", [P, PTH, NT, T])
        v0 = sb("v0", [P, NT, H0, 32])
        v1 = sb("v1", [P, NT, H1, 64])
        sums_t = [sb(f"sums_t{k}", [P, 3, T]) for k in range(2)]
        vsum = sb("vsum", [P, NT * H0])
        vcen = sb("vcen", [P, NT * H0, DH0])
        vsq = sb("vsq", [P, NT * H0, DH0])
        vvar = sb("vvar", [P, NT * H0])
        vms = sb("vms", [P, NT * H0])
        vrstd = sb("vrstd", [P, NT * H0])
        rsum = [sb(f"rsum{k}", [P, NT, H0]) for k in range(2)]
        att = [sb(f"att{k}", [P, NT, D]) for k in range(2)]
        att_t = sb("att_t", [KH + 1, 2, T])
        silu = sb("silu", [P, 2, T])
        hid = sb("hid", [P, 2, 2, T])
        r_qk = sb("r_qk", [64 + RANK, T])
        r_v = sb("r_v", [RANK, T])
        lg = [sb(f"lg{k}", [P, NT, 8]) for k in range(2)]
        top = [sb(f"top{k}", [P, NT, 8]) for k in range(2)]
        topi = [sb(f"topi{k}", [P, NT, 8], U32) for k in range(2)]
        topf = [sb(f"topf{k}", [P, NT, 2]) for k in range(2)]
        dl = [sb(f"dl{k}", [P, NT]) for k in range(2)]
        ed = [sb(f"ed{k}", [P, NT]) for k in range(2)]
        ed1 = [sb(f"ed1{k}", [P, NT]) for k in range(2)]
        wk = [sb(f"wk{k}", [P, NT, 2]) for k in range(2)]
        oh = [sb(f"oh{k}", [P, NT, 2, 8]) for k in range(2)]
        ohw = [sb(f"ohw{k}", [P, NT, 2, 8]) for k in range(2)]
        ohbase = sb("ohbase", [P, NT, 2, 8])
        ohb = sb("ohb", [P, NT, 2 * 8], BF16)
        comb = sb("comb", [P, NT, 8])
        seen = sb("seen", [P, 2 * 8])
        seenb = sb("seenb", [P, 2 * 8], BF16)
        rank = sb("rank", [P, NT, 2])
        bases = sb("bases", [P, NT, 2])
        keep = sb("keep", [P, NT, 2])
        place = sb("place", [P, NT, 2])
        kept = sb("kept", [P, NT, 2])
        off = sb("off", [P, NT, 2])
        drop = sb("drop", [P, NT, 2])
        slot_i = sb("slot_i", [P, NT * 2], I32)

        bank_a = [ps(f"bank_a{i}") for i in range(NA)]
        bank_v = [ps(f"bank_v{i}") for i in range(NV)]
        bank_o = [ps(f"bank_o{i}") for i in range(2)]

        def heads0(ap):
            return ap.rearrange("p (h d) -> p h d", d=32)

        def heads1(ap):
            return ap.rearrange("p (h d) -> p h d", d=64)

        def c(name, inner=None):
            ap = cst[:, _COLS[name]]
            return ap if inner is None else ap.rearrange("p (a b) -> p a b", b=inner)

        zeroed = sem("zeroed")
        loaded = sem("loaded")
        pix_ready = sem("pix_ready")
        patch_in = sem("patch_in")
        set_v = sem("set_v")
        set_p = sem("set_p")
        patch_tr = sem("patch_tr")
        zero_ready = sem("zero_ready")

        n_zero = NROWS // (P * 8)
        halves = lambda ap: ap.rearrange("(k p) n -> p k n", p=KH)
        row = lambda ap, n: bass.AP(ap.tensor, ap.offset, [[0, n], [1, ap.shape[-1]]])
        loads = [
            (cst[:], consts), (curve_i[:], curve.rearrange("(t p) c -> p t c", p=P)),
            (ids_i[:, 0, :], txt), (ids_i[:, 1, :], seg),
            (proj[3 * B:3 * B + 1, :], row(projb, 1)),
            (w_qkv[:], halves(wqkv)), (w_octx[0:KH], halves(wo_ctx)), (w_olat[0:KH], halves(wo_lat)),
            (w_octx[KH:KH + 1, 0, :], row(bo_ctx, 1)), (w_olat[KH:KH + 1, 0, :], row(bo_lat, 1)),
            (w_router[0:KH], halves(router_w)), (w_router[KH:KH + 1, 0, :], row(router_b, 1)),
            (w_va[:], halves(va)), (w_a[:, :, 0:RANK], halves(qa)), (w_a[:, :, 64:64 + RANK], halves(ka)),
            (w_b[0:RANK, 0:D], qb), (w_b[64:64 + RANK, D:2 * D], kb), (w_vb[:], vb),
            (w_o1[:], halves(ow)), (w_g1[:], halves(wg)),
            (lng[:], row(ln_g, P)), (lnb[:], row(ln_b, P)),
        ] + [(w_gate[:, :, e, :], halves(gate_w[e])) for e in range(E0)] \
          + [(w_up[:, :, e, :], halves(up_w[e])) for e in range(E0)] \
          + [(w_down[:, :, e, :], down_w[e].rearrange("(k p) n -> p k n", p=P)) for e in range(E0)] \
          + [(proj[3 * b:3 * b + 3, :], projw) for b in range(B)]

        with nc.Block() as block:
            @block.sync
            def _(sp):
                sp.wait_ge(set_p, 2)
                for dst, src in loads:
                    sp.dma_start(dst, src).then_inc(loaded, 16)

            @block.scalar
            def _(act):
                act.wait_ge(zero_ready, 1)
                for n in range(n_zero):
                    act.dma_start(xs_dram[n * 8 * P:(n + 1) * 8 * P, :].rearrange("(p r) d -> p r d", r=8),
                                  zeros[:].to_broadcast([P, 8, D])).then_inc(zeroed, 16)

            @block.gpsimd
            def _(pool):
                pool.memset(w_a[:], 0.0).then_inc(set_p, 1)
                pool.memset(w_b[:], 0.0).then_inc(set_p, 1)
                for i in range(2):
                    pool.memset(xt_of[i][:], 1.0).then_inc(set_p, 1)
                pool.memset(att_t[:], 1.0).then_inc(set_p, 1)
                pool.memset(patches_t[:], 1.0).then_inc(set_p, 1)
                pool.memset(pow_half[:], -0.5).then_inc(set_p, 1)
                pool.wait_ge(pix_ready, 1)
                for t in range(2):
                    pool.indirect_dma_start(patches[:, t, :], None, img,
                                            bass.IndirectOffsetOnAxis(ap=pix_i[:, t:t + 1], axis=0)
                                            ).then_inc(patch_in, 16)
                pool.wait_ge(patch_in, 32)

            @block.vector
            def _(dve):
                n = 0

                def chain(ins):
                    nonlocal n
                    n += 1
                    ins.then_inc(set_v, 1)

                nc.vector.memset(zeros[:], 0.0).then_inc(zero_ready, 1)
                chain(dve.memset(onesb[:], 1.0))
                chain(dve.memset(qk0[:], 0.0))
                chain(dve.memset(qk1[:], 0.0))
                chain(dve.memset(v0[:], 1.0))
                chain(dve.memset(v1[:], 1.0))
                chain(dve.memset(lg[0][:], NEG))
                chain(dve.memset(seen[:], 0.0))
                dve.wait_ge(set_v, n)
                for t in range(NT):
                    chain(dve.memset(heads0(qk0[:, t, 1, :])[:, :, DH0:DH0 + 1], 1.0))
                    chain(dve.memset(heads1(qk1[:, t, 1, :])[:, :, DH1:DH1 + 1], 1.0))
                dve.wait_ge(loaded, 16 * len(loads))
                chain(dve.tensor_copy(ident[:], c("ident")))
                chain(dve.tensor_copy(identb[:], c("ident")))
                chain(dve.tensor_copy(maskq[:], c("maskq")))
                chain(dve.tensor_copy(maskt[:], c("maskt")))
                chain(dve.tensor_copy(before[:], c("before")))
                chain(dve.tensor_copy(drop[:], c("drop", 2)))
                chain(dve.tensor_scalar(curve_f[:], curve_i[:], 0.0, float(IMG - 1), ALU.max, ALU.min))
                chain(dve.tensor_scalar(ids_f[:, 0, :], ids_i[:, 0, :], 0.0, float(VOCAB - 1), ALU.max, ALU.min))
                chain(dve.tensor_scalar(ids_f[:, 1, :], ids_i[:, 1, :], 0.0, float(NSEG - 1), ALU.max, ALU.min))
                dve.wait_ge(set_v, n)
                chain(dve.tensor_copy(ids_i[:], ids_f[:]))
                chain(dve.scalar_tensor_tensor(pix_f[:], curve_f[:, :, 1], float(IMG), curve_f[:, :, 0],
                                               ALU.mult, ALU.add))
                dve.wait_ge(set_v, n)
                dve.tensor_copy(pix_i[:], pix_f[:]).then_inc(pix_ready, 1)
                dve.wait_ge(patch_tr, 2)
                dve.wait_ge(set_p, 6)
                for t in range(2):
                    chain(dve.tensor_copy(patches_t[0:3 * B, t, :], bank_v[t][0:3 * B, 0:P]))

            @block.tensor
            def _(pe):
                pe.wait_ge(patch_in, 32)
                for t in range(2):
                    pe.transpose(bank_v[t][0:3 * B, 0:P], patches[:, t, :], ident[:]).then_inc(patch_tr, 1)

        rows_in = sem("rows_in")
        scattered = sem("scattered")
        emb_ready = sem("emb_ready")
        own_ready = sem("own_ready")
        carried = [sem(f"carried{s}") for s in range(3)]
        a_full, a_free = sem("a_full"), sem("a_free")
        v_full, v_free = sem("v_full"), sem("v_free")
        dve_step, pool_step = sem("dve_step"), sem("pool_step")
        var_ready = [sem(f"var_ready{k}") for k in range(4)]
        rstd_ready = [sem(f"rstd_ready{k}") for k in range(4)]
        xn_ready = [sem(f"xn_ready{k}") for k in range(4)]
        rope_ready = [sem(f"rope_ready{k}") for k in range(2)]
        k_round_ready = [sem(f"k_round_ready{k}") for k in range(2)]
        vcen_ready, vsq_ready = sem("vcen_ready"), sem("vsq_ready")
        vvar_ready, vrstd_ready, v0_ready = sem("vvar_ready"), sem("vrstd_ready"), sem("v0_ready")
        heads_done = [sem(f"heads_done{k}") for k in range(2)]
        o_free = sem("o_free")
        dl_ready = [sem(f"dl_ready{k}") for k in range(2)]
        ed_ready = [sem(f"ed_ready{k}") for k in range(2)]
        oh_ready = sem("oh_ready")
        slot_ready = sem("slot_ready")
        h_stored = sem("h_stored")
        per_body = range(emb_ready.num, h_stored.num + 1)

        def body(streams, image_x, image_y, image_z):
            order = schedule(streams)
            A, V = bank_plan(order)
            head_order = [(k, hd) for what, *at in order if what == "head" for k, hd in [at]]
            probs_of = {head: n for n, head in enumerate(head_order)}
            o_of = {group: n for n, group in enumerate(
                (k, hd // PER_BLOCK[k]) for k, hd in head_order if hd % PER_BLOCK[k] == 0)}

            def one(i, n=1):
                return slice(i * n, (i + 1) * n) if isinstance(i, int) else bass.ds(i * n, n)

            with nc.Block(no_gpsimd_drain=True) as block:

                @block.sync
                def _(sp):
                    if "z" in streams:
                        sp.wait_ge(v_free, V["out", 1, NT - 1] + 1)
                        sp.dma_start(h_dram.rearrange("(i t p) d -> p i t d", t=NT, p=P)[:, one(image_z)],
                                     h[2][:].unsqueeze(1)).then_inc(h_stored, 16)
                        sp.wait_ge(h_stored, 16)

                @block.gpsimd
                def _(pool):
                    steps = 0

                    def step(ins):
                        nonlocal steps
                        steps += 1
                        ins.then_inc(pool_step, 1)
                        pool.wait_ge(pool_step, steps)

                    for what, *at in order:
                        if what == "carry":
                            s, = at
                            if s == 1 and "z" in streams:
                                pool.wait_ge(carried[2], 1)
                            pool.tensor_copy(h[s][:], h[s - 1][:]).then_inc(carried[s], 1)
                        elif what == "rows":
                            step(pool.tensor_copy(idx[:].unsqueeze(2), ids_i[:, :, one(image_x)]))
                            pool.indirect_dma_start(tokrow[:], None, tok_table,
                                                    bass.IndirectOffsetOnAxis(ap=idx[:, 0:1], axis=0)
                                                    ).then_inc(rows_in, 16)
                            pool.indirect_dma_start(segrow[:], None, seg_table,
                                                    bass.IndirectOffsetOnAxis(ap=idx[:, 1:2], axis=0)
                                                    ).then_inc(rows_in, 16)
                            pool.tensor_tensor(own_proj[:], proj[:], cst[0:3 * B + 1, _COLS["own"]][:, one(image_x)]
                                               .to_broadcast([3 * B + 1, D]), ALU.mult).then_inc(own_ready, 1)
                        elif what == "patches":
                            pool.wait_ge(rows_in, (image_x + 1) * 32)
                            step(pool.tensor_tensor(embsum[:], segrow[:], c("pos"), ALU.add))
                            if "y" in streams:
                                pool.wait_ge(carried[1], 1)
                            pool.tensor_tensor(h[0][:, 2, :], embsum[:], tokrow[:], ALU.add).then_inc(emb_ready, 1)
                        elif what == "stats":
                            k, = at
                            pool.wait_ge(var_ready[k], 1)
                            pool.tensor_tensor(rstd[k][:], ve[k][:], pow_half[:, 0:NT], ALU.pow
                                               ).then_inc(rstd_ready[k], 1)
                        elif what == "qk":
                            k, t = at
                            padded = (qk0, qk1)[k][:, t].rearrange("p a (h d) -> p (a h) d", d=(32, 64)[k])
                            pool.wait_ge(v_free, V["qk", k, t] + 1)
                            pool.tensor_tensor(padded[:, :, 0:DHS[k]],
                                               rope_a[:, t, :].rearrange("p (g d) -> p g d", d=DHS[k]),
                                               rope_b[:, t, :].rearrange("p (g d) -> p g d", d=DHS[k]),
                                               ALU.add).then_inc(rope_ready[k], 1)
                        elif what == "values":
                            if at[0] == 0:
                                pool.wait_ge(vcen_ready, NT)
                                pool.tensor_tensor(vsq[:], vcen[:], vcen[:], ALU.mult).then_inc(vsq_ready, 1)
                            elif at[0] == 1:
                                pool.wait_ge(vvar_ready, 1)
                                pool.tensor_tensor(vrstd[:], vvar[:], pow_half[:], ALU.pow
                                                   ).then_inc(vrstd_ready, 1)
                        elif what == "places":
                            pool.wait_ge(zeroed, 16 * n_zero)
                            pool.wait_ge(xn_ready[3], NT)
                            pool.wait_ge(slot_ready, 1)
                            for t in range(NT):
                                for k in range(2):
                                    pool.indirect_dma_start(
                                        xs_dram,
                                        bass.IndirectOffsetOnAxis(ap=slot_i[:, 2 * t + k:2 * t + k + 1], axis=0),
                                        xn[3][:, t, :], None).then_inc(scattered, 16)
                    if "z" in streams:
                        pool.wait_ge(scattered, (image_z + 1) * (16 * 2 * NT))

                @block.scalar
                def _(act):
                    def empty(*what):
                        act.wait_ge(a_full, A[what] + 1)
                        return bank_a[A[what] % NA]

                    def group_summed(k, hd):
                        g = hd // PER_BLOCK[k]
                        act.wait_ge(heads_done[k], hd + 1)
                        act.activation(sums_t[k][:, g, :], bank_o[o_of[k, g] % 2][:, 0:T], ACT.Copy
                                       ).then_inc(o_free, 1)

                    for what, *at in order:
                        if what in ("xt", "att_t"):
                            k, = at
                            dst = xt[k] if what == "xt" else att_t
                            act.activation(dst[0:KH, 0, :], empty(what, k)[0:KH, 0:T], ACT.Copy
                                           ).then_inc(a_free, 1)
                        elif what == "low_rank":
                            act.activation(r_qk[:], empty("r_qk")[0:64 + RANK, 0:T], ACT.Copy).then_inc(a_free, 1)
                        elif what == "qk" and at[0] == 1:
                            act.activation(v1[:, at[1], :, 0:DH1],
                                           empty("v1", at[1])[:, 0:D].rearrange("p (h d) -> p h d", d=DH1),
                                           ACT.Copy).then_inc(a_free, 1)
                        elif what == "blocks":
                            k, b = at
                            bank = empty("k_t", k, b)
                            act.activation(k_round[k][:, b, :], bank[:, 0:T], ACT.Copy
                                           ).then_inc(k_round_ready[k], 1)
                            act.activation(k_t[k][:, b, :], bank[:, 0:T], ACT.Copy).then_inc(a_free, 1)
                        elif what == "head":
                            k, hd = at
                            if hd % PER_BLOCK[k] == 0:
                                b = hd // PER_BLOCK[k]
                                act.activation(q_t[k][:, b, :], empty("q_t", k, b)[:, 0:T], ACT.Copy
                                               ).then_inc(a_free, 1)
                            n = probs_of[k, hd]
                            if n >= PTH:
                                k_old, hd_old = head_order[n - PTH]
                                act.wait_ge(heads_done[k_old], hd_old + 1)
                            for kt in range(NT):
                                lo = kt * P if k == 1 else 0
                                act.activation(probs[:, n % PTH, kt, lo:T],
                                               empty("score", k, hd, kt)[:, lo:T], ACT.Exp,
                                               scale=DHS[k] ** -0.5).then_inc(a_free, 1)
                            if hd and hd % PER_BLOCK[k] == 0:
                                group_summed(k, hd - 1)
                        elif what == "last":
                            group_summed(at[0], HEADS[at[0]] - 1)
                        elif what == "exp":
                            k, = at
                            act.wait_ge(dl_ready[k], 1)
                            act.activation(ed[k][:], dl[k][:], ACT.Exp).then_inc(ed_ready[k], 1)
                        elif what == "ffn":
                            e, m = at
                            if e:
                                act.wait_ge(v_free, V["up", e - 1, m] + 1)
                            act.activation(silu[:, m, :], empty("gate", e, m)[:, 0:T], ACT.Silu).then_inc(a_free, 1)

                @block.tensor
                def _(pe):
                    def fill_a(*what):
                        if A[what] >= NA:
                            pe.wait_ge(a_free, A[what] - NA + 1)
                        return bank_a[A[what] % NA]

                    def fill_v(*what):
                        if V[what] >= NV:
                            pe.wait_ge(v_free, V[what] - NV + 1)
                        return bank_v[V[what] % NV]

                    def emptied_a(*what):
                        pe.wait_ge(a_free, A[what] + 1)

                    def emptied_v(*what):
                        pe.wait_ge(v_free, V[what] + 1)

                    def two_halves(name, k, src, ready):
                        for half, (bank, full) in enumerate(((fill_a(name, k), a_full), (None, v_full))):
                            if half:
                                bank = fill_v(name, k)
                            for t in range(NT):
                                if ready is not None:
                                    pe.wait_ge(ready, t + 1)
                                mm = pe.transpose(bank[0:KH, t * P:(t + 1) * P],
                                                  src[:, t, half * KH:(half + 1) * KH], ident[:])
                            mm.then_inc(full, 1)

                    def halves_ready(name, k):
                        emptied_a(name, k)
                        emptied_v(name, k)

                    def project(dst, x, tokens, w, cols, bias):
                        pe.matmul(dst, x[0:KH + bias, 0, tokens], w[0:KH + bias, 0, cols], start=True, stop=False)
                        return pe.matmul(dst, x[0:KH, 1, tokens], w[0:KH, 1, cols], start=False, stop=True)

                    tile = [slice(t * P, (t + 1) * P) for t in range(NT)]

                    def maxima(k, hd):
                        b, r, dh = hd // PER_BLOCK[k], P // PER_BLOCK[k] * (hd % PER_BLOCK[k]), DHS[k]
                        if hd % PER_BLOCK[k] == 0:
                            emptied_v("q_round", k, b)
                            pe.wait_ge(k_round_ready[k], b + 1)
                        for t in range(NT):
                            bank = fill_v("max", k, hd, t)
                            keys = (t + 1) * P if k == 1 else T
                            mm = pe.matmul(bank[:, 0:keys], q_round[k][r:r + dh, b, tile[t]],
                                           k_round[k][r:r + dh, b, 0:keys], start=True, stop=(k == 0))
                            if k == 1:
                                mm = pe.matmul(bank[:, tile[t]], identb[:], maskq[:], start=False, stop=True)
                            mm.then_inc(v_full, 1)

                    def scores(k, hd):
                        b, r, dh = hd // PER_BLOCK[k], P // PER_BLOCK[k] * (hd % PER_BLOCK[k]), DHS[k]
                        if hd % PER_BLOCK[k] == 0:
                            emptied_v("max", k, hd + PER_BLOCK[k] - 1, NT - 1)
                            bank = fill_a("q_t", k, b)
                            for t in range(NT):
                                mm = pe.transpose(bank[:, tile[t]], (qk0, qk1)[k][:, t, 0, b * P:(b + 1) * P],
                                                  ident[:])
                            mm.then_inc(a_full, 1)
                            emptied_a("q_t", k, b)
                        for t in range(NT):
                            bank = fill_a("score", k, hd, t)
                            lo = t * P if k == 1 else 0
                            mm = pe.matmul(bank[:, lo:T], k_t[k][r:r + dh + 1, b, tile[t]],
                                           q_t[k][r:r + dh + 1, b, lo:T], start=True, stop=(k == 0))
                            if k == 1:
                                mm = pe.matmul(bank[:, tile[t]], identb[:], maskt[:], start=False, stop=True)
                            mm.then_inc(a_full, 1)

                    def apply(k, hd):
                        emptied_a("score", k, hd, NT - 1)
                        if hd == 0 and k == 0:
                            pe.wait_ge(v0_ready, 1)
                        pr, v, rows = probs[:, probs_of[k, hd] % PTH], (v0, v1)[k], P // PER_BLOCK[k]
                        n = o_of[k, hd // PER_BLOCK[k]]
                        if hd % PER_BLOCK[k] == 0 and n >= 2:
                            pe.wait_ge(o_free, n - 1)
                        r = rows * (hd % PER_BLOCK[k])
                        o = bank_o[n % 2][r:r + rows]
                        last = NT - 1
                        if k == 1:
                            for kt in range(NT):
                                mm = pe.matmul(o[:, kt * P:T], v[:, kt, hd, :], pr[:, kt, kt * P:T],
                                               start=(kt == 0), stop=(kt == last))
                        else:
                            for kt in range(last):
                                pe.matmul(o[:, 0:T], v[:, kt, hd, :], pr[:, kt, :], start=(kt == 0), stop=False)
                            pe.matmul(o[:, 0:CTX], v[0:P - LAT, last, hd, :], pr[0:P - LAT, last, 0:CTX],
                                      start=False, stop=False)
                            mm = pe.matmul(o[:, CTX:T], v[:, last, hd, :], pr[:, last, CTX:T],
                                           start=False, stop=True)
                        mm.then_inc(heads_done[k], 1)

                    for what, *at in order:
                        if what == "patches":
                            pe.wait_ge(own_ready, 1)
                            for t in range(2):
                                pe.matmul(fill_v("patch", t)[:, 0:D], patches_t[:, t, :], own_proj[:],
                                          start=True, stop=True).then_inc(v_full, 1)
                        elif what == "xt":
                            two_halves("xt", at[0], xn[at[0]], xn_ready[at[0]])
                        elif what == "qk":
                            k, t = at
                            if k == 0:
                                halves_ready("xt", 0)
                                project(fill_v("qk", 0, t)[:, 0:2 * D], xt[0], tile[t], w_qkv, slice(0, 2 * D), 0
                                        ).then_inc(v_full, 1)
                            else:
                                emptied_a("r_qk")
                                emptied_v("r_v")
                                pe.matmul(fill_v("qk", 1, t)[:, 0:2 * D], r_qk[:, tile[t]], w_b[:], start=True,
                                          stop=True).then_inc(v_full, 1)
                                pe.matmul(fill_a("v1", t)[:, 0:D], r_v[:, tile[t]], w_vb[:], start=True, stop=True
                                          ).then_inc(a_full, 1)
                        elif what == "blocks":
                            k, b = at
                            pe.wait_ge(rope_ready[k], NT)
                            bank = fill_v("q_round", k, b)
                            for t in range(NT):
                                mm = pe.transpose(bank[:, tile[t]], (qk0, qk1)[k][:, t, 0, b * P:(b + 1) * P],
                                                  ident[:])
                            mm.then_inc(v_full, 1)
                            bank = fill_a("k_t", k, b)
                            for t in range(NT):
                                mm = pe.transpose(bank[:, tile[t]], (qk0, qk1)[k][:, t, 1, b * P:(b + 1) * P],
                                                  ident[:])
                            mm.then_inc(a_full, 1)
                        elif what == "maxima":
                            maxima(*at)
                        elif what == "head":
                            k, hd = at
                            scores(k, hd)
                            if hd + AHEAD[k] < HEADS[k]:
                                maxima(k, hd + AHEAD[k])
                            if hd:
                                apply(k, hd - 1)
                        elif what == "last":
                            apply(at[0], HEADS[at[0]] - 1)
                        elif what == "sums":
                            k, t = at
                            pe.wait_ge(o_free, o_of[k, HEADS[k] // PER_BLOCK[k] - 1] + 1)
                            bank = fill_v("sums", k, t)
                            for g in range(3):
                                mm = pe.transpose(bank[:, g * P:(g + 1) * P], sums_t[k][:, g, tile[t]], ident[:])
                            mm.then_inc(v_full, 1)
                        elif what == "att_t":
                            if at[0] == 0:
                                emptied_v("sums", 0, NT - 1)
                            two_halves("att_t", at[0], att[at[0]], None)
                        elif what == "out":
                            k, = at
                            halves_ready("att_t", k)
                            for t in range(NT):
                                bank = fill_v("out", k, t)
                                if k == 1:
                                    mm = project(bank[:, 0:D], att_t, tile[t], w_o1, slice(0, D), 0)
                                elif t < NT - 1:
                                    mm = project(bank[:, 0:D], att_t, tile[t], w_octx, slice(0, D), 1)
                                else:
                                    project(bank[0:P - LAT, 0:D], att_t, slice(t * P, CTX), w_octx, slice(0, D), 1)
                                    mm = project(bank[P - LAT:P, 0:D], att_t, slice(CTX, T), w_olat, slice(0, D), 1)
                                mm.then_inc(v_full, 1)
                        elif what == "logits":
                            k, = at
                            halves_ready("xt", (1, 3)[k])
                            bank = fill_v("logits", k)
                            w, n = ((w_router, E0), (w_g1, E1))[k]
                            for t in range(NT):
                                mm = project(bank[:, 8 * t:8 * t + n], xt[(1, 3)[k]], tile[t], w, slice(0, n), 1 - k)
                            mm.then_inc(v_full, 1)
                        elif what == "ffn":
                            e, m = at
                            for w, bank, full in ((w_gate, fill_a("gate", e, m), a_full), (w_up, None, v_full)):
                                if bank is None:
                                    bank = fill_v("up", e, m)
                                for half in range(2):
                                    mm = pe.matmul(bank[:, 0:T], w[:, half, e, m * P:(m + 1) * P],
                                                   xt[1][0:KH, half, :], start=(half == 0), stop=(half == 1))
                                mm.then_inc(full, 1)
                        elif what == "down":
                            e, = at
                            emptied_v("up", e, 1)
                            for t in range(NT):
                                bank = fill_v("down", e, t)
                                for m in range(2):
                                    mm = pe.matmul(bank[:, 0:D], hid[:, e % 2, m, tile[t]], w_down[:, m, e, :],
                                                   start=(m == 0), stop=(m == 1))
                                mm.then_inc(v_full, 1)
                        elif what == "low_rank":
                            halves_ready("xt", 2)
                            for w, bank, rows, full in ((w_a, fill_a("r_qk"), 64 + RANK, a_full),
                                                        (w_va, fill_v("r_v"), RANK, v_full)):
                                for half in range(2):
                                    mm = pe.matmul(bank[0:rows, 0:T], w[:, half, :], xt[2][0:KH, half, :],
                                                   start=(half == 0), stop=(half == 1))
                                mm.then_inc(full, 1)
                        elif what == "rank":
                            pe.wait_ge(oh_ready, 1)
                            bank = fill_v("rank")
                            for t in range(NT):
                                o = bank[:, 16 * t:16 * t + 16]
                                pe.matmul(o, before[:], ohb[:, t, :], start=True, stop=False)
                                for u in range(t):
                                    pe.matmul(o, onesb[:], ohb[:, u, :], start=False, stop=False)
                                mm = pe.matmul(o, onesb[:], seenb[:], start=False, stop=True)
                            mm.then_inc(v_full, 1)

                @block.vector
                def _(dve):
                    steps = 0

                    def step(ins):
                        nonlocal steps
                        steps += 1
                        ins.then_inc(dve_step, 1)

                    def done():
                        dve.wait_ge(dve_step, steps)

                    def full(*what):
                        dve.wait_ge(v_full, V[what] + 1)
                        return bank_v[V[what] % NV]

                    def written(*what):
                        dve.wait_ge(v_free, V[what] + 1)

                    def statistics(k):
                        src = h[STREAM_OF_NORM[k]]
                        for t in range(NT):
                            step(dve.bn_stats(st6[k][:, t, :], src[:, t, :]))
                        done()
                        for t in range(NT):
                            step(dve.bn_aggr(mv[k][:, t, :], st6[k][:, t, :]))
                        done()
                        dve.tensor_scalar(ve[k][:], mv[k][:, :, 1], EPS, None, ALU.add).then_inc(var_ready[k], 1)

                    def rope_products(k, t):
                        dh = DHS[k]
                        g, half = 2 * D // dh, dh // 2
                        x = full("qk", k, t)[:, 0:2 * D].rearrange("p (g d) -> p g d", d=dh)
                        cos = c(f"cos{k}", dh)[:, t, :].unsqueeze(1)
                        sin = c(f"sin{k}", dh)[:, t, :].unsqueeze(1)
                        a = rope_a[:, t, :].rearrange("p (g d) -> p g d", d=dh)
                        b = rope_b[:, t, :].rearrange("p (g d) -> p g d", d=dh)
                        if k == 1 and "x" in streams:
                            dve.wait_ge(rope_ready[0], t + 1)
                        step(dve.tensor_tensor(a, x, cos.to_broadcast([P, g, dh]), ALU.mult))
                        step(dve.tensor_tensor(b[:, :, 0:half], x[:, :, half:dh],
                                               sin[:, :, 0:half].to_broadcast([P, g, half]), ALU.mult))
                        done()
                        dve.tensor_tensor(b[:, :, half:dh], x[:, :, 0:half],
                                          sin[:, :, half:dh].to_broadcast([P, g, half]), ALU.mult
                                          ).then_inc(v_free, 1)

                    def values(n):
                        keys = qk0[:, :, 1, :].rearrange("p t (h d) -> p t h d", d=32)[:, :, :, 0:DH0]
                        tiled = vsum[:].rearrange("p (t h) -> p t h", h=H0)
                        vv = v0[:].rearrange("p t h d -> p (t h) d")[:, :, 0:DH0]
                        if n == 0:
                            dve.wait_ge(rope_ready[0], NT)
                            step(dve.tensor_reduce(tiled, keys, AX.X, ALU.add))
                            done()
                            for t in range(NT):
                                dve.scalar_tensor_tensor(
                                    vcen[:, t * H0:(t + 1) * H0, :],
                                    vsum[:, t * H0:(t + 1) * H0].unsqueeze(2).to_broadcast([P, H0, DH0]), -1.0 / DH0,
                                    keys[:, t], ALU.mult, ALU.add).then_inc(vcen_ready, 1)
                        elif n == 1:
                            dve.wait_ge(vsq_ready, 1)
                            step(dve.tensor_reduce(vms[:], vsq[:], AX.X, ALU.add))
                            done()
                            dve.tensor_scalar(vvar[:], vms[:], 1.0 / DH0, EPS, ALU.mult, ALU.add
                                              ).then_inc(vvar_ready, 1)
                        else:
                            dve.wait_ge(vrstd_ready, 1)
                            step(dve.tensor_tensor(
                                vv, vcen[:], vrstd[:].unsqueeze(2).to_broadcast([P, NT * H0, DH0]), ALU.mult))
                            done()
                            step(dve.tensor_tensor(
                                vv, vv, lng[:].unsqueeze(1).to_broadcast([P, NT * H0, DH0]), ALU.mult))
                            done()
                            dve.tensor_tensor(vv, vv, lnb[:].unsqueeze(1).to_broadcast([P, NT * H0, DH0]), ALU.add
                                              ).then_inc(v0_ready, 1)

                    def maxima(k, hd):
                        width, dh = P // PER_BLOCK[k], DHS[k]
                        for t in range(NT):
                            bank = full("max", k, hd, t)
                            to = (qk0, qk1)[k][:, t, 0, hd * width + dh:hd * width + dh + 1]
                            if k == 0 and t == NT - 1:
                                step(dve.tensor_reduce(to[P - LAT:P], bank[P - LAT:P, 0:T], AX.X, ALU.max,
                                                       negate=True))
                                done()
                                dve.tensor_reduce(to[0:P - LAT], bank[0:P - LAT, 0:CTX], AX.X, ALU.max,
                                                  negate=True).then_inc(v_free, 1)
                            else:
                                keys = (t + 1) * P if k == 1 else CTX
                                dve.tensor_reduce(to, bank[:, 0:keys], AX.X, ALU.max, negate=True
                                                  ).then_inc(v_free, 1)

                    def attention_out(k, t):
                        heads, dh = HEADS[k], DHS[k]
                        sums = full("sums", k, t)[:, 0:3 * P].rearrange("p (h d) -> p h d", h=heads)
                        step(dve.reciprocal(rsum[k][:, t, 0:heads], sums[:, :, dh]))
                        done()
                        dve.tensor_tensor(att[k][:, t, :].rearrange("p (h d) -> p h d", d=dh), sums[:, :, 0:dh],
                                          rsum[k][:, t, 0:heads].unsqueeze(2).to_broadcast([P, heads, dh]),
                                          ALU.mult).then_inc(v_free, 1)

                    def largest(k, experts):
                        dve.tensor_copy(lg[k][:, :, 0:experts],
                                        full("logits", k)[:, 0:8 * NT].rearrange("p (t e) -> p t e", e=8)
                                        [:, :, 0:experts]).then_inc(v_free, 1)
                        written("logits", k)
                        for t in range(NT):
                            step(dve.max(top[k][:, t, :], lg[k][:, t, :]))
                        done()
                        dve.tensor_tensor(dl[k][:], top[k][:, :, 1], top[k][:, :, 0], ALU.subtract
                                          ).then_inc(dl_ready[k], 1)
                        for t in range(NT):
                            step(dve.max_index(topi[k][:, t, :], top[k][:, t, :], lg[k][:, t, :]))
                        done()
                        step(dve.tensor_copy(topf[k][:], topi[k][:, :, 0:2]))
                        done()
                        step(dve.tensor_tensor(
                            oh[k][:].rearrange("p t k e -> p (t k) e"),
                            c("iota").unsqueeze(1).to_broadcast([P, 2 * NT, 8]),
                            topf[k][:].rearrange("p t k -> p (t k)").unsqueeze(2).to_broadcast([P, 2 * NT, 8]),
                            ALU.is_equal))

                    def softmax_of_two(k):
                        dve.wait_ge(ed_ready[k], 1)
                        step(dve.tensor_scalar(ed1[k][:], ed[k][:], 1.0, None, ALU.add))
                        done()
                        step(dve.reciprocal(wk[k][:, :, 0], ed1[k][:]))
                        done()
                        step(dve.tensor_tensor(wk[k][:, :, 1], ed[k][:], wk[k][:, :, 0], ALU.mult))
                        done()

                    def count_choices():
                        step(dve.tensor_copy(seenb[:], seen[:]))
                        done()
                        dve.tensor_copy(ohb[:], oh[1][:].rearrange("p t k e -> p t (k e)")).then_inc(oh_ready, 1)
                        for t in range(NT):
                            done()
                            step(dve.tensor_tensor(seen[:], seen[:], oh[1][:, t].rearrange("p k e -> p (k e)"),
                                                   ALU.add))
                        step(dve.tensor_tensor(
                            ohbase[:].rearrange("p t k e -> p t (k e)"), oh[1][:].rearrange("p t k e -> p t (k e)"),
                            c("base").unsqueeze(1).to_broadcast([P, NT, 16]), ALU.mult))
                        done()
                        step(dve.tensor_reduce(bases[:], ohbase[:], AX.X, ALU.add))

                    def places():
                        written("rank")
                        step(dve.tensor_reduce(rank[:], ohw[1][:], AX.X, ALU.add))
                        done()
                        step(dve.tensor_scalar(keep[:], rank[:], float(CAP), None, ALU.is_lt))
                        step(dve.tensor_tensor(place[:], rank[:], bases[:], ALU.add))
                        done()
                        step(dve.tensor_tensor(off[:], place[:], drop[:], ALU.subtract))
                        step(dve.tensor_tensor(kept[:], place[:], keep[:], ALU.mult))
                        step(dve.tensor_tensor(weights_all[:, one(image_z, 2 * NT)],
                                               wk[1][:].rearrange("p t k -> p (t k)"),
                                               keep[:].rearrange("p t k -> p (t k)"), ALU.mult))
                        done()
                        step(dve.tensor_copy(slots_all[:, one(image_z, 2 * NT)],
                                             kept[:].rearrange("p t k -> p (t k)")))
                        step(dve.tensor_tensor(place[:], off[:], keep[:], ALU.mult))
                        done()
                        dve.tensor_tensor(slot_i[:].rearrange("p (t k) -> p t k", k=2), place[:], drop[:], ALU.add
                                          ).then_inc(slot_ready, 1)
                        dve.wait_ge(slot_ready, 1)
                        step(dve.tensor_scalar(drop[:], drop[:], float(T), None, ALU.add))

                    for what, *at in order:
                        if what == "patches":
                            if "y" in streams:
                                dve.wait_ge(carried[1], 1)
                            for t in range(2):
                                dve.tensor_copy(h[0][:, t, :], full("patch", t)[:, 0:D]).then_inc(v_free, 1)
                        elif what == "stats":
                            if at[0] == 0:
                                written("patch", 1)
                                dve.wait_ge(emb_ready, 1)
                            elif at[0] == 2:
                                written("down", E0 - 1, NT - 1)
                            else:
                                written("out", at[0] // 2, NT - 1)
                            statistics(*at)
                        elif what == "xn":
                            k, = at
                            dve.wait_ge(rstd_ready[k], 1)
                            for t in range(NT):
                                dve.tensor_scalar(xn[k][:, t, :], h[STREAM_OF_NORM[k]][:, t, :], mv[k][:, t, 0:1],
                                                  rstd[k][:, t:t + 1], ALU.subtract, ALU.mult
                                                  ).then_inc(xn_ready[k], 1)
                        elif what in ("xt", "att_t"):
                            k, = at
                            dst = xt[k] if what == "xt" else att_t
                            dve.tensor_copy(dst[0:KH, 1, :], full(what, k)[0:KH, 0:T]).then_inc(v_free, 1)
                        elif what == "qk":
                            rope_products(*at)
                        elif what == "blocks":
                            k, b = at
                            dve.tensor_copy(q_round[k][:, b, :], full("q_round", k, b)[:, 0:T]).then_inc(v_free, 1)
                        elif what == "values":
                            values(*at)
                        elif what == "maxima":
                            maxima(*at)
                        elif what == "head":
                            k, hd = at
                            if hd + AHEAD[k] < HEADS[k]:
                                maxima(k, hd + AHEAD[k])
                        elif what == "sums":
                            attention_out(*at)
                        elif what == "out":
                            k, = at
                            s = (0, 2)[k]
                            if k == 1:
                                dve.wait_ge(carried[2], 1)
                            for t in range(NT):
                                dve.tensor_tensor(h[s][:, t, :], full("out", k, t)[:, 0:D], h[s][:, t, :], ALU.add
                                                  ).then_inc(v_free, 1)
                        elif what == "logits":
                            largest(at[0], (E0, E1)[at[0]])
                        elif what == "weights":
                            softmax_of_two(*at)
                            if at[0] == 0:
                                step(dve.tensor_tensor(ohw[0][:], oh[0][:],
                                                       wk[0][:].unsqueeze(3).to_broadcast([P, NT, 2, 8]), ALU.mult))
                                done()
                                step(dve.tensor_tensor(comb[:], ohw[0][:, :, 0, :], ohw[0][:, :, 1, :], ALU.add))
                            else:
                                count_choices()
                        elif what == "ffn":
                            e, m = at
                            bank = full("up", e, m)
                            dve.wait_ge(a_free, A["gate", e, m] + 1)
                            dve.tensor_tensor(hid[:, e % 2, m, :], bank[:, 0:T], silu[:, m, :], ALU.mult
                                              ).then_inc(v_free, 1)
                        elif what == "low_rank":
                            dve.tensor_copy(r_v[:], full("r_v")[0:RANK, 0:T]).then_inc(v_free, 1)
                        elif what == "down":
                            e, = at
                            if e == 0:
                                dve.wait_ge(carried[1], 1)
                            for t in range(NT):
                                if e:
                                    written("down", e - 1, t)
                                dve.scalar_tensor_tensor(h[1][:, t, :], full("down", e, t)[:, 0:D],
                                                         comb[:, t, e:e + 1], h[1][:, t, :], ALU.mult, ALU.add
                                                         ).then_inc(v_free, 1)
                        elif what == "rank":
                            bank = full("rank")
                            dve.tensor_tensor(ohw[1][:].rearrange("p t k e -> p (t k e)"), bank[:, 0:16 * NT],
                                              oh[1][:].rearrange("p t k e -> p (t k e)"), ALU.mult
                                              ).then_inc(v_free, 1)
                        elif what == "places":
                            places()
                    done()
            nc.all_engine_barrier(sems_to_clear=per_body)

        body("x", 0, None, None)
        body("xy", 1, 0, None)
        with nc.Fori(0, B - 2) as image:
            body("xyz", image + 2, image + 1, image)
        body("yz", None, B - 1, B - 2)
        body("z", None, None, B - 1)


def expert_stage(nc, w1, w2, xs_dram, y_dram, ident):
    NX = 3
    with ExitStack() as ctx:
        def sb(name, shape, dt=F32):
            return ctx.enter_context(nc.sbuf_tensor(name, shape, dt))

        def sem(name):
            return ctx.enter_context(nc.semaphore(name))

        w_in = sb("w_in", [KH, 2, 2 * HF])
        w_out = sb("w_out", [P, HF // P, D])
        rows = sb("rows", [P, NX, NT, D])
        rows_t = sb("rows_t", [KH, 2, 2, T])
        gated = sb("gated", [P, 2, T])
        hid = sb("e_hid", [P, 2, HF // P, T])
        res = sb("res", [P, 2, NT, D])
        bank_a = [ctx.enter_context(nc.psum_tensor(f"e_bank_a{i}", [P, 512], F32)) for i in range(4)]
        bank_v = [ctx.enter_context(nc.psum_tensor(f"e_bank_v{i}", [P, 512], F32)) for i in range(4)]

        w_loaded = sem("w_loaded")
        rows_in = [sem(f"rows_in{i}") for i in range(NX)]
        ea_full, ea_free, ev_full, ev_free = sem("ea_full"), sem("ea_free"), sem("ev_full"), sem("ev_free")
        stored = [sem(f"stored{i}") for i in range(2)]
        per_expert = range(w_loaded.num, ev_free.num + 1)
        of_buffer = [len(range(i, NCHUNK, 2)) for i in range(2)]

        NM = HF // P
        a, v = [("x", 0)], [("x", 0)]
        for ch in range(NCHUNK):
            a += [("b", ch, m) for m in range(NM)]
            v += [("a", ch, m) for m in range(NM)]
            if ch + 1 < NCHUNK:
                a.append(("x", ch + 1))
                v.append(("x", ch + 1))
            a += [("y", ch, t) for t in range(NT)]
        ea = {what: n for n, what in enumerate(a)}
        ev = {what: n for n, what in enumerate(v)}

        with nc.Fori(0, E1) as expert:
            with nc.Block(no_gpsimd_drain=True) as block:

                @block.sync
                def _(sp):
                    xs = xs_dram[0:NROWS, :].rearrange("(e c t p) d -> p e c t d", e=E1, c=NCHUNK, p=P)
                    sp.dma_start(w_in[:].unsqueeze(1),
                                 w1.rearrange("e (k p) n -> p e k n", p=KH)[:, bass.ds(expert, 1)]
                                 ).then_inc(w_loaded, 16)
                    for ch in range(NCHUNK):
                        if ch >= NX:
                            sp.wait_ge(ev_full, ev["x", ch - NX] + 1)
                        for t in range(NT):
                            sp.dma_start(rows[:, ch % NX, t, :].unsqueeze(1), xs[:, bass.ds(expert, 1), ch, t]
                                         ).then_inc(rows_in[ch % NX], 16)
                        if ch == 0:
                            sp.dma_start(w_out[:].unsqueeze(1),
                                         w2.rearrange("e (k p) n -> p e k n", p=P)[:, bass.ds(expert, 1)]
                                         ).then_inc(w_loaded, 16)

                @block.gpsimd
                def _(pool):
                    ys = y_dram.rearrange("(e c t p) d -> p e c t d", e=E1, c=NCHUNK, p=P)
                    for ch in range(NCHUNK):
                        pool.wait_ge(ea_free, ea["y", ch, NT - 1] + 1)
                        pool.dma_start(ys[:, bass.ds(expert, 1), ch], res[:, ch % 2].unsqueeze(1)
                                       ).then_inc(stored[ch % 2], 16)
                    for i in range(2):
                        pool.wait_ge(stored[i], (expert + 1) * (16 * of_buffer[i]))

                @block.tensor
                def _(pe):
                    def fill_a(*what):
                        if ea[what] >= 4:
                            pe.wait_ge(ea_free, ea[what] - 4 + 1)
                        return bank_a[ea[what] % 4]

                    def fill_v(*what):
                        if ev[what] >= 4:
                            pe.wait_ge(ev_free, ev[what] - 4 + 1)
                        return bank_v[ev[what] % 4]

                    def down(ch):
                        pe.wait_ge(ev_free, ev["a", ch, NM - 1] + 1)
                        for t in range(NT):
                            bank = fill_a("y", ch, t)
                            for m in range(NM):
                                mm = pe.matmul(bank[:, 0:D], hid[:, ch % 2, m, t * P:(t + 1) * P], w_out[:, m, :],
                                               start=(m == 0), stop=(m == NM - 1))
                            mm.then_inc(ea_full, 1)

                    def transpose_rows(ch):
                        pe.wait_ge(rows_in[ch % NX], 16 * NT * (ch // NX + 1))
                        bank = fill_a("x", ch)
                        for t in range(NT):
                            mm = pe.transpose(bank[0:KH, t * P:(t + 1) * P], rows[:, ch % NX, t, 0:KH], ident[:])
                        mm.then_inc(ea_full, 1)
                        bank = fill_v("x", ch)
                        for t in range(NT):
                            mm = pe.transpose(bank[0:KH, t * P:(t + 1) * P], rows[:, ch % NX, t, KH:D], ident[:])
                        mm.then_inc(ev_full, 1)

                    transpose_rows(0)
                    pe.wait_ge(w_loaded, 32)
                    for ch in range(NCHUNK):
                        pe.wait_ge(ea_free, ea["x", ch] + 1)
                        pe.wait_ge(ev_free, ev["x", ch] + 1)
                        for m in range(NM):
                            for at, bank, full in ((HF + m * P, fill_a("b", ch, m), ea_full), (m * P, None, ev_full)):
                                if bank is None:
                                    bank = fill_v("a", ch, m)
                                for half in range(2):
                                    mm = pe.matmul(bank[:, 0:T], w_in[:, half, at:at + P], rows_t[:, ch % 2, half, :],
                                                   start=(half == 0), stop=(half == 1))
                                mm.then_inc(full, 1)
                        if ch + 1 < NCHUNK:
                            transpose_rows(ch + 1)
                        down(ch)

                @block.scalar
                def _(act):
                    def full(*what):
                        act.wait_ge(ea_full, ea[what] + 1)
                        return bank_a[ea[what] % 4]

                    def results(ch):
                        if ch >= 2:
                            act.wait_ge(stored[ch % 2], expert * (16 * of_buffer[ch % 2]) + 16 * (ch // 2))
                        for t in range(NT):
                            act.activation(res[:, ch % 2, t, :], full("y", ch, t)[:, 0:D], ACT.Copy
                                           ).then_inc(ea_free, 1)

                    def half_transposed(ch):
                        act.activation(rows_t[:, ch % 2, 0, :], full("x", ch)[0:KH, 0:T], ACT.Copy
                                       ).then_inc(ea_free, 1)

                    half_transposed(0)
                    for ch in range(NCHUNK):
                        for m in range(NM):
                            if m >= 2:
                                act.wait_ge(ev_free, ev["a", ch, m - 2] + 1)
                            elif ch:
                                act.wait_ge(ev_free, ev["a", ch - 1, m + NM - 2] + 1)
                            act.activation(gated[:, m % 2, :], full("b", ch, m)[:, 0:T], ACT.Silu
                                           ).then_inc(ea_free, 1)
                        if ch + 1 < NCHUNK:
                            half_transposed(ch + 1)
                        results(ch)

                @block.vector
                def _(dve):
                    def full(*what):
                        dve.wait_ge(ev_full, ev[what] + 1)
                        return bank_v[ev[what] % 4]

                    def half_transposed(ch):
                        dve.tensor_copy(rows_t[:, ch % 2, 1, :], full("x", ch)[0:KH, 0:T]).then_inc(ev_free, 1)

                    half_transposed(0)
                    for ch in range(NCHUNK):
                        for m in range(NM):
                            bank = full("a", ch, m)
                            dve.wait_ge(ea_free, ea["b", ch, m] + 1)
                            dve.tensor_tensor(hid[:, ch % 2, m, :], bank[:, 0:T], gated[:, m % 2, :], ALU.mult
                                              ).then_inc(ev_free, 1)
                        if ch + 1 < NCHUNK:
                            half_transposed(ch + 1)
            nc.all_engine_barrier(sems_to_clear=per_expert)


def combine_stage(nc, y_dram, h_dram, out, slots_all, weights_all):
    TI = CIMG * NT
    with ExitStack() as ctx:
        def sb(name, shape, dt=F32):
            return ctx.enter_context(nc.sbuf_tensor(name, shape, dt))

        def sem(name):
            return ctx.enter_context(nc.semaphore(name))

        idx = sb("c_idx", [P, 2 * TI], I32)
        wts = sb("c_wts", [P, 2 * TI])
        hrow = sb("hrow", [P, TI, D])
        y = sb("y", [P, TI, 2, D])
        part = sb("part", [P, TI, D])
        y_in = [sem(f"y_in{t}") for t in range(TI)]
        idx_copied, wts_copied, h_in = sem("idx_copied"), sem("wts_copied"), sem("h_in")
        first_added, both_added, out_stored = sem("first_added"), sem("both_added"), sem("out_stored")
        per_step = range(idx_copied.num, out_stored.num + 1)
        tiles = lambda ap: ap.rearrange("(s t p) d -> p s t d", t=TI, p=P)

        with nc.Fori(0, B // CIMG) as group:
            with nc.Block(no_gpsimd_drain=True) as block:

                @block.gpsimd
                def _(pool):
                    pool.tensor_copy(idx[:], slots_all[:, bass.ds(group * (2 * TI), 2 * TI)]).then_inc(idx_copied, 1)
                    pool.wait_ge(idx_copied, 1)
                    for t in range(TI):
                        for k in range(2):
                            pool.indirect_dma_start(
                                y[:, t, k, :], None, y_dram,
                                bass.IndirectOffsetOnAxis(ap=idx[:, 2 * t + k:2 * t + k + 1], axis=0)
                            ).then_inc(y_in[t], 16)

                @block.sync
                def _(sp):
                    sp.dma_start(hrow[:].unsqueeze(1), tiles(h_dram)[:, bass.ds(group, 1)]).then_inc(h_in, 16)
                    sp.wait_ge(both_added, TI)
                    sp.dma_start(tiles(out)[:, bass.ds(group, 1)], hrow[:].unsqueeze(1)).then_inc(out_stored, 16)
                    sp.wait_ge(out_stored, 16)

                @block.vector
                def _(dve):
                    dve.tensor_copy(wts[:], weights_all[:, bass.ds(group * (2 * TI), 2 * TI)]
                                    ).then_inc(wts_copied, 1)
                    dve.wait_ge(wts_copied, 1)
                    dve.wait_ge(h_in, 16)
                    for t in range(TI):
                        dve.wait_ge(y_in[t], (group + 1) * 32)
                        dve.scalar_tensor_tensor(part[:, t, :], y[:, t, 0, :], wts[:, 2 * t:2 * t + 1], hrow[:, t, :],
                                                 ALU.mult, ALU.add).then_inc(first_added, 1)
                        dve.wait_ge(first_added, t + 1)
                        dve.scalar_tensor_tensor(hrow[:, t, :], y[:, t, 1, :], wts[:, 2 * t + 1:2 * t + 2],
                                                 part[:, t, :], ALU.mult, ALU.add).then_inc(both_added, 1)
            nc.all_engine_barrier(sems_to_clear=per_step)


def kernel(x, x_txt, mask_BS_i2_0, L0_tok_curve, L0_tok_proj_w, L0_tok_proj_b, L0_txt_token_table,
           L0_txt_segm_table, L0_attn_Wq, L0_attn_Wkv, L0_attn_Wo_ctx, L0_attn_bo_ctx, L0_attn_Wo_lat,
           L0_attn_bo_lat, L0_attn_ln_g, L0_attn_ln_b, L0_ffn_router_w, L0_ffn_router_b, L0_ffn_gate_w,
           L0_ffn_up_w, L0_ffn_down_w, L1_attn_qA, L1_attn_qB, L1_attn_kA, L1_attn_kB, L1_attn_vA,
           L1_attn_vB, L1_attn_o_w, L1_ffn_Wg, L1_ffn_W1, L1_ffn_W2):
    import numpy as np
    import concourse.bacc as bacc
    from concourse.bass_utils import run_bass_kernel_spmd

    a = np.asarray
    arrays = {
        "consts": constants(),
        "img": a(x).transpose(2, 3, 0, 1).reshape(IMG * IMG, 3 * B),
        "txt": a(x_txt).T, "seg": a(mask_BS_i2_0).T, "curve": a(L0_tok_curve),
        "projw": a(L0_tok_proj_w).T, "projb": a(L0_tok_proj_b),
        "tok_table": a(L0_txt_token_table), "seg_table": a(L0_txt_segm_table),
        "wqkv": np.concatenate([a(L0_attn_Wq), a(L0_attn_Wkv)], axis=1),
        "wo_ctx": a(L0_attn_Wo_ctx), "bo_ctx": a(L0_attn_bo_ctx),
        "wo_lat": a(L0_attn_Wo_lat), "bo_lat": a(L0_attn_bo_lat),
        "ln_g": a(L0_attn_ln_g), "ln_b": a(L0_attn_ln_b),
        "router_w": a(L0_ffn_router_w).T, "router_b": a(L0_ffn_router_b),
        "gate_w": a(L0_ffn_gate_w), "up_w": a(L0_ffn_up_w), "down_w": a(L0_ffn_down_w),
        "qa": a(L1_attn_qA), "qb": a(L1_attn_qB), "ka": a(L1_attn_kA), "kb": a(L1_attn_kB),
        "va": a(L1_attn_vA), "vb": a(L1_attn_vB), "ow": a(L1_attn_o_w),
        "wg": a(L1_ffn_Wg), "w1": a(L1_ffn_W1), "w2": a(L1_ffn_W2),
    }
    arrays = {name: np.ascontiguousarray(value) for name, value in arrays.items()}
    nc = bacc.Bacc("TRN2", target_bir_lowering=False, num_devices=1)
    args = [nc.dram_tensor(f"in_{name}", value.shape, mybir.dt.from_np(value.dtype), kind="ExternalInput").ap()
            for name, value in arrays.items()]
    out = nc.dram_tensor("out_tokens", (N, D), F32, kind="ExternalOutput").ap()
    early_fusion_kernel(nc, *args, out)
    got = run_bass_kernel_spmd(nc, [{f"in_{name}": value for name, value in arrays.items()}], core_ids=[0])
    return np.asarray(got.results[0]["out_tokens"]).reshape(B, T, D)
```

```python
from contextlib import ExitStack

import concourse.bass as bass
from concourse import mybir

F32 = mybir.dt.float32
F32R = mybir.dt.float32r
BF16 = mybir.dt.bfloat16
I32 = mybir.dt.int32
U32 = mybir.dt.uint32
ALU = mybir.AluOpType
ACT = mybir.ActivationFunctionType
AX = mybir.AxisListType

P = 128
D = 192
KH = D // 2
B = 32
NVIS, NTXT = 256, 128
T = NVIS + NTXT
NT = T // P
LAT = 32
CTX = T - LAT
N = B * T
VOCAB, NSEG, IMG = 8000, 3, 128
H0, DH0 = 12, 16
H1, DH1, RANK = 6, 32, 48
E0, I0 = 5, 256
E1, HF = 8, 512
CAP = int(1.2 * N / E1)
EROWS = -(-2 * CAP // T) * T
NCHUNK = EROWS // T
NROWS = E1 * EROWS
EPS = 1e-5
NEG = -1e30
NA, NV = 3, 3
PTH = 2
CIMG = min(8, B)
HEADS, DHS = (H0, H1), (DH0, DH1)
D2 = D - P
PER_BLOCK = (4, 2)
HEAD_ROWS = (64, 128)
AHEAD = (6, 4)
ORDER = ("xzyyyyxyxyyyxyxyxxxxyxyxyxxyyyxyxxxxxyxyzyxyxyxzxxzz"
         "yyyxyxyxzyxxyzyxzzyyxzyxzxyxyxyxxyxyxyxyyxxyxyyyyx")
STREAM_OF_NORM = (0, 0, 1, 2)

_COLS = {}
_w = 0
for _name, _n in (("ident", P), ("maskq", P), ("maskt", P), ("maskl", LAT), ("before", P), ("pos", D),
                  ("cos0", NT * DH0), ("sin0", NT * DH0), ("cos1", NT * DH1), ("sin1", NT * DH1),
                  ("iota", E1), ("base", 2 * E1), ("drop", 2 * NT), ("own", B)):
    _COLS[_name] = slice(_w, _w + _n)
    _w += _n
NCOLS = _w


def constants():
    import numpy as np

    c = np.zeros((P, NCOLS), np.float32)
    p = np.arange(P)
    c[:, _COLS["ident"]] = np.eye(P)
    c[:, _COLS["maskq"]] = np.where(p[None, :] <= p[:, None], 0.0, NEG)
    c[:, _COLS["maskt"]] = np.where(p[:, None] <= p[None, :], 0.0, NEG)
    c[:P - LAT, _COLS["maskl"]] = NEG
    c[:, _COLS["before"]] = p[:, None] < p[None, :]
    ids = np.arange(D, dtype=np.float32)
    angle = p.astype(np.float32)[:, None] / np.power(
        np.float32(10000.0), np.floor(ids / np.float32(2)) * np.float32(2) / np.float32(D)).astype(np.float32)[None]
    c[:, _COLS["pos"]] = np.where(np.arange(D) % 2 == 0, np.sin(angle.astype(np.float64)),
                                  np.cos(angle.astype(np.float64)))
    for name, dh in (("0", DH0), ("1", DH1)):
        inv = (np.float32(1.0) / np.power(np.float32(10000.0), np.arange(0, dh, 2, dtype=np.float32)
                                          / np.float32(dh))).astype(np.float32)
        f = (np.arange(T, dtype=np.float32)[:, None] * inv[None, :]).astype(np.float32).astype(np.float64)
        cos = np.concatenate([np.cos(f), np.cos(f)], 1).reshape(NT, P, dh).transpose(1, 0, 2)
        sin = np.concatenate([-np.sin(f), np.sin(f)], 1).reshape(NT, P, dh).transpose(1, 0, 2)
        c[:, _COLS["cos" + name]] = cos.reshape(P, -1)
        c[:, _COLS["sin" + name]] = sin.reshape(P, -1)
    c[:, _COLS["iota"]] = np.arange(E1)[None]
    c[:, _COLS["base"]] = (np.arange(2)[:, None] * CAP + np.arange(E1)[None] * EROWS).reshape(1, -1)
    c[:, _COLS["drop"]] = (NROWS + np.arange(NT)[None, :, None] * P + p[:, None, None]
                           + np.arange(2)[None, None, :] * N).reshape(P, -1)
    c[:3 * B, _COLS["own"]] = np.tile(np.eye(B), (3, 1))
    c[3 * B, _COLS["own"]] = 1.0
    return c


def units():
    def heads_in_rows(k):
        values = [[("values", n)] * (k == 0) for n in range(3)]
        return [("qk", k, 0), ("qk", k, 1), ("parts", k, 0), ("qk", k, 2), ("parts", k, 1), ("blocks", k, 0),
                ("parts", k, 2), *values[0], ("blocks", k, 1), *values[1], ("blocks", k, 2),
                *(("maxima", k, hd) for hd in range(AHEAD[k])), *values[2]]

    x = [("rows",), ("patches",), ("stats", 0), ("xn", 0), ("xt", 0), *heads_in_rows(0)]
    x += [("head", 0, hd) for hd in range(H0)]
    x += [("last", 0)] + [("sums", 0, t) for t in range(NT)]
    x += [("att_t", 0), ("out", 0), ("stats", 1), ("xn", 1), ("split",), ("xt", 1)]
    y = [("carry", 1), ("logits", 0), ("ffn", 0, 0), ("tanh", 0), ("ffn", 0, 1), ("weights", 0)]
    for e in range(1, E0):
        y += [("ffn", e, m) for m in range(2)] + [("down", e - 1)]
    y += [("down", E0 - 1), ("stats", 2), ("xn", 2), ("xt", 2), ("low_rank",)]
    y += heads_in_rows(1)
    y += [("head", 1, hd) for hd in range(H1)]
    y += [("last", 1)] + [("sums", 1, t) for t in range(NT)]
    z = [("carry", 2), ("att_t", 1), ("out", 1), ("stats", 3), ("xn", 3), ("xt", 3), ("logits", 1), ("tanh", 1),
         ("weights", 1), ("rank",), ("places",)]
    return {"x": x, "y": y, "z": z}


def schedule(streams):
    todo = {s: iter(u) for s, u in units().items()}
    order = [(s, next(todo[s])) for s in ORDER]
    assert not any(list(u) for u in todo.values())
    return [unit for s, unit in order if s in streams]


def bank_plan(order):
    a, v = [], []
    for what, *at in order:
        if what == "patches":
            v += [("patch", t) for t in range(2)]
        elif (what, *at) == ("xt", 1):
            a += [("xt", 1, 0), ("xt", 1, 2)]
            v.append(("xt", 1, 1))
        elif what in ("xt", "att_t"):
            a.append((what, *at))
            v.append((what, *at))
        elif what == "qk":
            v.append(("qk", *at))
            if at[0] == 1:
                a.append(("v1", at[1]))
        elif what == "blocks":
            a += [("blocks", *at, 0), ("blocks", *at, 2)]
            v.append(("blocks", *at, 1))
        elif what == "maxima":
            v += [("max", *at, t) for t in range(NT)]
            if at[1] == AHEAD[at[0]] - 1:
                a.append(("m_t", at[0], 0))
        elif what == "head":
            k, hd = at
            a += [("score", k, hd, t) for t in range(NT)]
            if (hd + 1) % PER_BLOCK[k] == 0 and hd + 1 < HEADS[k]:
                a.append(("m_t", k, (hd + 1) // PER_BLOCK[k]))
            if hd + AHEAD[k] < HEADS[k]:
                v += [("max", k, hd + AHEAD[k], t) for t in range(NT)]
        elif what == "sums":
            v.append(("sums", *at))
        elif what == "out":
            v += [("out", at[0], t) for t in range(NT)]
        elif what == "logits":
            v.append(("logits", at[0]))
        elif what == "ffn":
            a.append(("gate", *at))
            v.append(("up", *at))
        elif what == "down":
            v += [("down", at[0], t) for t in range(NT)]
        elif what == "low_rank":
            a.append(("r_qk",))
            v.append(("r_v",))
        elif what == "rank":
            v.append(("rank",))
    return {what: n for n, what in enumerate(a)}, {what: n for n, what in enumerate(v)}


def early_fusion_kernel(nc, consts, img, txt, seg, curve, projw, projb, tok_table, seg_table, wqkv,
                        wo_ctx, bo_ctx, wo_lat, bo_lat, ln_g, ln_b, router_w, router_b, gate_w, up_w,
                        down_w, qa, qb, ka, kb, va, vb, ow, wg, w1, w2, out):
    xs_dram = nc.dram_tensor("xs_dram", (NROWS + 2 * N, D), F32, kind="Internal").ap()
    y_dram = nc.dram_tensor("y_dram", (NROWS, D), F32, kind="Internal").ap()
    h_dram = nc.dram_tensor("h_dram", (N, D), F32, kind="Internal").ap()

    with ExitStack() as whole:
        slots_all = whole.enter_context(nc.sbuf_tensor("slots_all", [P, B * NT * 2], I32))
        weights_all = whole.enter_context(nc.sbuf_tensor("weights_all", [P, B * NT * 2], F32))
        ident = whole.enter_context(nc.sbuf_tensor("ident", [P, P], F32))
        token_stages(nc, consts, img, txt, seg, curve, projw, projb, tok_table, seg_table, wqkv,
                     wo_ctx, bo_ctx, wo_lat, bo_lat, ln_g, ln_b, router_w, router_b, gate_w, up_w,
                     down_w, qa, qb, ka, kb, va, vb, ow, wg, xs_dram, h_dram, slots_all, weights_all, ident)
        expert_stage(nc, w1, w2, xs_dram, y_dram, ident)
        combine_stage(nc, y_dram, h_dram, out, slots_all, weights_all)


def token_stages(nc, consts, img, txt, seg, curve, projw, projb, tok_table, seg_table, wqkv,
                 wo_ctx, bo_ctx, wo_lat, bo_lat, ln_g, ln_b, router_w, router_b, gate_w, up_w,
                 down_w, qa, qb, ka, kb, va, vb, ow, wg, xs_dram, h_dram, slots_all, weights_all, ident):
    ctx = ExitStack()
    with ctx:
        def sb(name, shape, dt=F32):
            return ctx.enter_context(nc.sbuf_tensor(name, shape, dt))

        def ps(name):
            return ctx.enter_context(nc.psum_tensor(name, [P, 512], F32))

        def sem(name):
            return ctx.enter_context(nc.semaphore(name))

        cst = sb("cst", [P, NCOLS])
        identb = sb("identb", [P, P], BF16)
        maskq = sb("maskq", [P, P], BF16)
        maskt = sb("maskt", [P, P], BF16)
        maskl = sb("maskl", [P, LAT], BF16)
        before = sb("before", [P, P], BF16)
        onesb = sb("onesb", [P, P], BF16)
        pow_half = sb("pow_half", [P, 36])
        zeros = sb("zeros", [P, 1, D])
        w_qkv = sb("w_qkv", [KH, 2, 2 * D])
        w_octx = sb("w_octx", [KH + 1, 2, D])
        w_olat = sb("w_olat", [KH + 1, 2, D])
        w_ffn = sb("w_ffn", [P, 3, 2 * E0 * I0 + 8], F32R)
        router_bias = sb("router_bias", [P, E0])
        w_down = sb("w_down", [P, 2, E0, D])
        w_a = sb("w_a", [KH, 2, 64 + RANK])
        w_va = sb("w_va", [KH, 2, RANK])
        w_b = sb("w_b", [64 + RANK, 2 * D])
        w_vb = sb("w_vb", [RANK, D])
        w_o1 = sb("w_o1", [KH, 2, D])
        w_g1 = sb("w_g1", [KH, 2, E1])
        lng = sb("lng", [P, DH0])
        lnb = sb("lnb", [P, DH0])
        proj = sb("proj", [3 * B + 1, D])
        own_proj = sb("own_proj", [3 * B + 1, D])
        curve_i = sb("curve_i", [P, 2, 2], I32)
        curve_f = sb("curve_f", [P, 2, 2])
        pix_f = sb("pix_f", [P, 2])
        pix_i = sb("pix_i", [P, 2], I32)
        ids_i = sb("ids_i", [P, 2, B], I32)
        ids_f = sb("ids_f", [P, 2, B])
        patches = sb("patches", [P, 2, 3 * B])
        patches_t = sb("patches_t", [3 * B + 1, 2, P])

        idx = sb("idx", [P, 2], I32)
        tokrow = sb("tokrow", [P, D])
        segrow = sb("segrow", [P, D])
        embsum = sb("embsum", [P, D])
        h = [sb(f"h_{s}", [P, NT, D]) for s in "xyz"]
        st6 = [sb(f"st6{k}", [P, NT, 6]) for k in range(4)]
        mv = [sb(f"mv{k}", [P, NT, 2]) for k in range(4)]
        ve = [sb(f"ve{k}", [P, NT]) for k in range(4)]
        rstd = [sb(f"rstd{k}", [P, NT]) for k in range(4)]
        xn_of = [sb(f"xn_{s}", [P, NT, D]) for s in "xyz"]
        xn = [xn_of[s] for s in STREAM_OF_NORM]
        xt_of = [sb(f"xt{i}", [KH + 1, 2, T]) for i in range(2)]
        xt = [xt_of[0], None, xt_of[1], xt_of[0]]
        ffn_x = sb("ffn_x", [P, 4, T], F32R)
        rope_a = sb("rope_a", [P, NT, 2 * D])
        rope_b = sb("rope_b", [P, NT, 2 * D])
        parts = [sb(f"parts{i}", [P, 2, 6 * P], F32R) for i in range(2)]
        heads_t = [sb(f"heads_t{k}", [P, 12, T], F32R) for k in range(2)]
        neg_max = [sb(f"neg_max{k}", [P, NT, HEADS[k]]) for k in range(2)]
        max_t = [sb(f"max_t{k}", [P, 2, T], F32R) for k in range(2)]
        pick = sb("pick", [P, 4, P], F32R)
        identr = sb("identr", [P, P], F32R)
        probs = sb("probs", [P, PTH, NT, T])
        v0 = sb("v0", [P, NT, H0, 32])
        v1 = sb("v1", [P, NT, H1, 64])
        sums_t = [sb(f"sums_t{k}", [P, 3, T]) for k in range(2)]
        vsum = sb("vsum", [P, NT * H0])
        vcen, vsq = (sums_t[0][:].rearrange("p a n -> p (a n)")[:, i * NT * D:(i + 1) * NT * D]
                     .rearrange("p (a d) -> p a d", d=DH0) for i in range(2))
        vvar = sb("vvar", [P, NT * H0])
        vms = sb("vms", [P, NT * H0])
        vrstd = sb("vrstd", [P, NT * H0])
        rsum = [sb(f"rsum{k}", [P, NT, H0]) for k in range(2)]
        att = [sb(f"att{k}", [P, NT, D]) for k in range(2)]
        att_t = sb("att_t", [KH + 1, 2, T])
        silu = sums_t[1]
        r_qk = sums_t[1][0:64 + RANK, 0, :]
        r_v = sums_t[1][0:RANK, 1, :]
        hid = sb("hid", [P, 2, 2, T])
        lg = [sb(f"lg{k}", [P, NT, 8]) for k in range(2)]
        top = [sb(f"top{k}", [P, NT, 8]) for k in range(2)]
        topi = [sb(f"topi{k}", [P, NT, 8], U32) for k in range(2)]
        topf = [sb(f"topf{k}", [P, NT, 2]) for k in range(2)]
        dl = [sb(f"dl{k}", [P, NT]) for k in range(2)]
        th = [sb(f"th{k}", [P, NT]) for k in range(2)]
        wk = [sb(f"wk{k}", [P, NT, 2]) for k in range(2)]
        oh = [sb(f"oh{k}", [P, NT, 2, 8]) for k in range(2)]
        ohw = [sb(f"ohw{k}", [P, NT, 2, 8]) for k in range(2)]
        ohbase = sb("ohbase", [P, NT, 2, 8])
        ohb = sb("ohb", [P, NT, 2 * 8], BF16)
        comb = sb("comb", [P, NT, 8])
        seen = sb("seen", [P, 2 * 8])
        seenb = sb("seenb", [P, 2 * 8], BF16)
        rank = sb("rank", [P, NT, 2])
        bases = sb("bases", [P, NT, 2])
        keep = sb("keep", [P, NT, 2])
        place = sb("place", [P, NT, 2])
        kept = sb("kept", [P, NT, 2])
        off = sb("off", [P, NT, 2])
        drop = sb("drop", [P, NT, 2])
        slot_i = sb("slot_i", [P, NT * 2], I32)

        bank_a = [ps(f"bank_a{i}") for i in range(NA)]
        bank_v = [ps(f"bank_v{i}") for i in range(NV)]
        bank_o = [ps(f"bank_o{i}") for i in range(2)]

        def c(name, inner=None):
            ap = cst[:, _COLS[name]]
            return ap if inner is None else ap.rearrange("p (a b) -> p a b", b=inner)

        zeroed = sem("zeroed")
        loaded = sem("loaded")
        pix_ready = sem("pix_ready")
        patch_in = sem("patch_in")
        set_v = sem("set_v")
        set_p = sem("set_p")
        patch_tr = sem("patch_tr")
        ups_loaded = sem("ups_loaded")
        ffn_split = sem("ffn_split")
        zero_ready = sem("zero_ready")

        n_zero = NROWS // (P * 8)
        halves = lambda ap: ap.rearrange("(k p) n -> p k n", p=KH)
        row = lambda ap, n: bass.AP(ap.tensor, ap.offset, [[0, n], [1, ap.shape[-1]]])
        n_gate, router_cols = E0 * I0, slice(E0 * I0, E0 * I0 + 8)
        raw = [probs[:].rearrange("p a t n -> p (a t n)")[:, 0:n_gate + 8],
               hid[:].rearrange("p a m n -> p (a m n)")[:, 0:n_gate + 8]]
        ffn_cols = (slice(0, n_gate + 8), slice(n_gate + 8, 2 * n_gate + 8))
        ffn_rows = ((raw[0], slice(0, P), slice(0, P)), (raw[1], slice(0, D2), slice(P, D)),
                    (raw[1], slice(D2, P), slice(P, D)))
        loads = [
            (cst[:], consts), (curve_i[:], curve.rearrange("(t p) c -> p t c", p=P)),
            (ids_i[:, 0, :], txt), (ids_i[:, 1, :], seg),
            (proj[3 * B:3 * B + 1, :], row(projb, 1)),
            (w_qkv[:], halves(wqkv)), (w_octx[0:KH], halves(wo_ctx)), (w_olat[0:KH], halves(wo_lat)),
            (w_octx[KH:KH + 1, 0, :], row(bo_ctx, 1)), (w_olat[KH:KH + 1, 0, :], row(bo_lat, 1)),
            (router_bias[:], row(router_b, P)),
            (w_va[:], halves(va)), (w_a[:, :, 0:RANK], halves(qa)), (w_a[:, :, 64:64 + RANK], halves(ka)),
            (w_b[0:RANK, 0:D], qb), (w_b[64:64 + RANK, D:2 * D], kb), (w_vb[:], vb),
            (w_o1[:], halves(ow)), (w_g1[:], halves(wg)),
            (lng[:], row(ln_g, P)), (lnb[:], row(ln_b, P)),
        ] + [(dst[rows, 0:n_gate].rearrange("p (e i) -> p e i", e=E0), gate_w[:, src, :].rearrange("e p i -> p e i"))
             for dst, rows, src in ffn_rows] \
          + [(dst[rows, router_cols.start:router_cols.start + E0], router_w[src]) for dst, rows, src in ffn_rows] \
          + [(w_down[:, k, :, :], down_w[:, k * P:(k + 1) * P, :].rearrange("e p n -> p e n")) for k in range(2)] \
          + [(proj[i * B:(i + 1) * B, :], row(projw[i:i + 1, :], B)) for i in range(3)]

        with nc.Block() as block:
            @block.sync
            def _(sp):
                sp.wait_ge(set_p, 4)
                for dst, src in loads:
                    sp.dma_start(dst, src).then_inc(loaded, 16)
                sp.wait_ge(ffn_split, 4)
                for dst, rows, src in ffn_rows:
                    sp.dma_start(dst[rows, 0:n_gate].rearrange("p (e i) -> p e i", e=E0),
                                 up_w[:, src, :].rearrange("e p i -> p e i")).then_inc(ups_loaded, 16)

            @block.scalar
            def _(act):
                act.wait_ge(zero_ready, 1)
                for n in range(n_zero):
                    act.dma_start(xs_dram[n * 8 * P:(n + 1) * 8 * P, :].rearrange("(p r) d -> p r d", r=8),
                                  zeros[:].to_broadcast([P, 8, D])).then_inc(zeroed, 16)

            @block.gpsimd
            def _(pool):
                pool.memset(w_a[:], 0.0).then_inc(set_p, 1)
                pool.memset(w_b[:], 0.0).then_inc(set_p, 1)
                for i in range(2):
                    pool.memset(raw[i][:, router_cols], 0.0).then_inc(set_p, 1)
                for i in range(2):
                    pool.memset(xt_of[i][:], 1.0).then_inc(set_p, 1)
                pool.memset(att_t[:], 1.0).then_inc(set_p, 1)
                pool.memset(patches_t[:], 1.0).then_inc(set_p, 1)
                pool.memset(pow_half[:], -0.5).then_inc(set_p, 1)
                pool.wait_ge(pix_ready, 1)
                for t in range(2):
                    pool.indirect_dma_start(patches[:, t, :], None, img,
                                            bass.IndirectOffsetOnAxis(ap=pix_i[:, t:t + 1], axis=0)
                                            ).then_inc(patch_in, 16)
                pool.wait_ge(patch_in, 32)

            @block.vector
            def _(dve):
                n = 0

                def chain(ins):
                    nonlocal n
                    n += 1
                    ins.then_inc(set_v, 1)

                def split_weights(n):
                    cols, width = ffn_cols[n], ffn_cols[n].stop - ffn_cols[n].start
                    dve.tensor_copy(w_ffn[:, 0, cols], raw[0][:, 0:width]).then_inc(ffn_split, 1)
                    dve.tensor_copy(w_ffn[:, 2, cols], raw[1][:, 0:width]).then_inc(ffn_split, 1)
                    dve.wait_ge(ffn_split, 4 * n + 2)
                    dve.tensor_tensor(w_ffn[:, 1, cols], raw[0][:, 0:width], w_ffn[:, 0, cols].bitcast(F32),
                                      ALU.subtract).then_inc(ffn_split, 1)
                    dve.tensor_tensor(w_ffn[D2:P, 2, cols], raw[1][D2:P, 0:width],
                                      w_ffn[D2:P, 2, cols].bitcast(F32), ALU.subtract).then_inc(ffn_split, 1)

                nc.vector.memset(zeros[:], 0.0).then_inc(zero_ready, 1)
                dve.wait_ge(zero_ready, 1)
                chain(dve.memset(onesb[:], 1.0))
                chain(dve.tensor_copy(pick[:], zeros[:, :, 0:P].to_broadcast([P, 4, P])))
                for i in range(2):
                    chain(dve.tensor_copy(parts[i][:].rearrange("p s (a n) -> p (s a) n", n=P),
                                          zeros[:, :, 0:P].to_broadcast([P, 12, P])))
                    chain(dve.tensor_copy(max_t[i][:].rearrange("p a (b n) -> p (a b) n", n=P),
                                          zeros[:, :, 0:P].to_broadcast([P, 2 * NT, P])))
                chain(dve.memset(v0[:], 1.0))
                chain(dve.memset(v1[:], 1.0))
                chain(dve.memset(lg[0][:], NEG))
                chain(dve.memset(seen[:], 0.0))
                dve.wait_ge(set_v, n)
                dve.wait_ge(loaded, 16 * len(loads))
                chain(dve.tensor_copy(ident[:], c("ident")))
                chain(dve.tensor_copy(identb[:], c("ident")))
                chain(dve.tensor_copy(identr[:], c("ident")))
                split_weights(0)
                chain(dve.tensor_copy(pick[0:4], c("ident")[0:4, 0:4].unsqueeze(2).to_broadcast([4, 4, P])))
                chain(dve.tensor_copy(maskq[:], c("maskq")))
                chain(dve.tensor_copy(maskt[:], c("maskt")))
                chain(dve.tensor_copy(maskl[:], c("maskl")))
                chain(dve.tensor_copy(before[:], c("before")))
                chain(dve.tensor_copy(drop[:], c("drop", 2)))
                chain(dve.tensor_scalar(curve_f[:], curve_i[:], 0.0, float(IMG - 1), ALU.max, ALU.min))
                chain(dve.tensor_scalar(ids_f[:, 0, :], ids_i[:, 0, :], 0.0, float(VOCAB - 1), ALU.max, ALU.min))
                chain(dve.tensor_scalar(ids_f[:, 1, :], ids_i[:, 1, :], 0.0, float(NSEG - 1), ALU.max, ALU.min))
                dve.wait_ge(set_v, n)
                chain(dve.tensor_copy(ids_i[:], ids_f[:]))
                chain(dve.scalar_tensor_tensor(pix_f[:], curve_f[:, :, 1], float(IMG), curve_f[:, :, 0],
                                               ALU.mult, ALU.add))
                dve.wait_ge(set_v, n)
                dve.tensor_copy(pix_i[:], pix_f[:]).then_inc(pix_ready, 1)
                dve.wait_ge(patch_tr, 2)
                dve.wait_ge(set_p, 8)
                for t in range(2):
                    chain(dve.tensor_copy(patches_t[0:3 * B, t, :], bank_v[t][0:3 * B, 0:P]))
                dve.wait_ge(ups_loaded, 48)
                split_weights(1)

            @block.tensor
            def _(pe):
                pe.wait_ge(patch_in, 32)
                for t in range(2):
                    pe.transpose(bank_v[t][0:3 * B, 0:P], patches[:, t, :], ident[:]).then_inc(patch_tr, 1)

        rows_in = sem("rows_in")
        scattered = sem("scattered")
        emb_ready = sem("emb_ready")
        own_ready = sem("own_ready")
        carried = [sem(f"carried{s}") for s in range(3)]
        a_full, a_free = sem("a_full"), sem("a_free")
        v_full, v_free = sem("v_full"), sem("v_free")
        dve_step, pool_step = sem("dve_step"), sem("pool_step")
        var_ready = [sem(f"var_ready{k}") for k in range(4)]
        rstd_ready = [sem(f"rstd_ready{k}") for k in range(4)]
        xn_ready = [sem(f"xn_ready{k}") for k in range(4)]
        rope_ready = [sem(f"rope_ready{k}") for k in range(2)]
        high_ready = [sem(f"high_ready{k}") for k in range(2)]
        low_ready = [sem(f"low_ready{k}") for k in range(2)]
        split_high, split_low = sem("split_high"), sem("split_low")
        vcen_ready, vsq_ready = sem("vcen_ready"), sem("vsq_ready")
        vvar_ready, vrstd_ready, v0_ready = sem("vvar_ready"), sem("vrstd_ready"), sem("v0_ready")
        heads_done = [sem(f"heads_done{k}") for k in range(2)]
        o_free = sem("o_free")
        dl_ready = [sem(f"dl_ready{k}") for k in range(2)]
        th_ready = [sem(f"th_ready{k}") for k in range(2)]
        oh_ready = sem("oh_ready")
        slot_ready = sem("slot_ready")
        h_stored = sem("h_stored")
        per_body = range(emb_ready.num, h_stored.num + 1)

        def body(streams, image_x, image_y, image_z):
            order = schedule(streams)
            A, V = bank_plan(order)
            head_order = [(k, hd) for what, *at in order if what == "head" for k, hd in [at]]
            probs_of = {head: n for n, head in enumerate(head_order)}
            parts_order = [unit for unit in order if unit[0] in ("parts", "split")]
            parts_of = {unit: n for n, unit in enumerate(parts_order)}
            last_transposed = [("xt", 1, 2) if unit[0] == "split" else ("blocks", *unit[1:], 2)
                               for unit in parts_order]
            split = parts[parts_of["split",] % 2][:].rearrange("p s n -> p (s n)").rearrange(
                "p (t n) -> p t n", t=NT) if "x" in streams else None
            o_of = {group: n for n, group in enumerate(
                (k, hd // PER_BLOCK[k]) for k, hd in head_order if hd % PER_BLOCK[k] == 0)}

            def part(k, t, side):
                return parts[parts_of["parts", k, t] % 2][:, side, :].rearrange("p (h w) -> p h w", h=HEADS[k]
                                                                       )[:, :, 0:3 * DHS[k]].rearrange(
                    "p h (a d) -> p h a d", a=3)

            def rotated(k, t, side):
                return rope_a[:, t, side * D:(side + 1) * D].rearrange("p (h d) -> p h d", d=DHS[k])

            products = ((0, 0), (1, 0), (0, 1), (2, 2), (3, 2))

            def pairs(cols):
                return split[:, :, cols].rearrange("p t (a d) -> p t a d", a=2)

            def one(i, n=1):
                return slice(i * n, (i + 1) * n) if isinstance(i, int) else bass.ds(i * n, n)

            with nc.Block(no_gpsimd_drain=True) as block:

                @block.sync
                def _(sp):
                    if "z" in streams:
                        sp.wait_ge(v_free, V["out", 1, NT - 1] + 1)
                        sp.dma_start(h_dram.rearrange("(i t p) d -> p i t d", t=NT, p=P)[:, one(image_z)],
                                     h[2][:].unsqueeze(1)).then_inc(h_stored, 16)
                        sp.wait_ge(h_stored, 16)

                @block.gpsimd
                def _(pool):
                    steps = 0

                    def step(ins):
                        nonlocal steps
                        steps += 1
                        ins.then_inc(pool_step, 1)
                        pool.wait_ge(pool_step, steps)

                    for what, *at in order:
                        if what == "rows":
                            pool.tensor_tensor(own_proj[:], proj[:], cst[0:3 * B + 1, _COLS["own"]][:, one(image_x)]
                                               .to_broadcast([3 * B + 1, D]), ALU.mult).then_inc(own_ready, 1)
                            step(pool.tensor_copy(idx[:].unsqueeze(2), ids_i[:, :, one(image_x)]))
                            pool.indirect_dma_start(tokrow[:], None, tok_table,
                                                    bass.IndirectOffsetOnAxis(ap=idx[:, 0:1], axis=0)
                                                    ).then_inc(rows_in, 16)
                            pool.indirect_dma_start(segrow[:], None, seg_table,
                                                    bass.IndirectOffsetOnAxis(ap=idx[:, 1:2], axis=0)
                                                    ).then_inc(rows_in, 16)
                        elif what == "patches":
                            pool.wait_ge(rows_in, (image_x + 1) * 32)
                            step(pool.tensor_tensor(embsum[:], segrow[:], c("pos"), ALU.add))
                            if "y" in streams:
                                pool.wait_ge(carried[1], 1)
                            pool.tensor_tensor(h[0][:, 2, :], embsum[:], tokrow[:], ALU.add).then_inc(emb_ready, 1)
                        elif what == "stats":
                            k, = at
                            pool.wait_ge(var_ready[k], 1)
                            pool.tensor_tensor(rstd[k][:], ve[k][:], pow_half[:, 0:NT], ALU.pow
                                               ).then_inc(rstd_ready[k], 1)
                        elif what == "qk":
                            k, t = at
                            pool.wait_ge(v_free, V["qk", k, t] + 1)
                            pool.tensor_tensor(rope_a[:, t, :], rope_a[:, t, :], rope_b[:, t, :], ALU.add
                                               ).then_inc(rope_ready[k], 1)
                        elif what == "parts":
                            k, t = at
                            pool.wait_ge(rope_ready[k], t + 1)
                            pool.wait_ge(high_ready[k], 2 * (t + 1))
                            for side in range(2):
                                pool.tensor_tensor(part(k, t, side)[:, :, 2 - side, :], rotated(k, t, side),
                                                   part(k, t, side)[:, :, 0, :].bitcast(F32), ALU.subtract
                                                   ).then_inc(low_ready[k], 1)
                        elif what == "split":
                            pool.wait_ge(split_high, 2)
                            pool.tensor_tensor(split[:, :, P:2 * P], xn[1][:, :, 0:P],
                                               split[:, :, 0:P].bitcast(F32), ALU.subtract).then_inc(split_low, 1)
                            pool.tensor_tensor(pairs(slice(3 * P, 4 * P)),
                                               xn[1][:, :, P:D].unsqueeze(2).to_broadcast([P, NT, 2, D2]),
                                               pairs(slice(2 * P, 3 * P)).bitcast(F32), ALU.subtract
                                               ).then_inc(split_low, 1)
                        elif what == "values":
                            if at[0] == 0:
                                pool.wait_ge(vcen_ready, NT)
                                pool.tensor_tensor(vsq, vcen, vcen, ALU.mult).then_inc(vsq_ready, 1)
                            elif at[0] == 1:
                                pool.wait_ge(vvar_ready, 1)
                                pool.tensor_tensor(vrstd[:], vvar[:], pow_half[:], ALU.pow
                                                   ).then_inc(vrstd_ready, 1)
                        elif what == "places":
                            pool.wait_ge(zeroed, 16 * n_zero)
                            pool.wait_ge(xn_ready[3], NT)
                            pool.wait_ge(slot_ready, 1)
                            for t in range(NT):
                                for k in range(2):
                                    pool.indirect_dma_start(
                                        xs_dram,
                                        bass.IndirectOffsetOnAxis(ap=slot_i[:, 2 * t + k:2 * t + k + 1], axis=0),
                                        xn[3][:, t, :], None).then_inc(scattered, 16)
                    if "z" in streams:
                        pool.wait_ge(scattered, (image_z + 1) * (16 * 2 * NT))

                @block.scalar
                def _(act):
                    def empty(*what):
                        act.wait_ge(a_full, A[what] + 1)
                        return bank_a[A[what] % NA]

                    def buffer_free(*unit):
                        n = parts_of[unit]
                        if n >= 2:
                            act.wait_ge(a_full, A[last_transposed[n - 2]] + 1)

                    def maxima_transposed(k, g):
                        act.activation(max_t[k][0:PER_BLOCK[k], g % 2, :], empty("m_t", k, g)[0:PER_BLOCK[k], 0:T],
                                       ACT.Copy).then_inc(a_free, 1)

                    def group_summed(k, hd):
                        g = hd // PER_BLOCK[k]
                        act.wait_ge(heads_done[k], hd + 1)
                        act.activation(sums_t[k][:, g, :], bank_o[o_of[k, g] % 2][:, 0:T], ACT.Copy
                                       ).then_inc(o_free, 1)

                    for what, *at in order:
                        if what == "carry":
                            s, = at
                            if s == 1 and "z" in streams:
                                act.wait_ge(carried[2], 1)
                            act.activation(h[s][:], h[s - 1][:], ACT.Copy).then_inc(carried[s], 1)
                        elif what == "split":
                            act.wait_ge(xn_ready[1], NT)
                            buffer_free("split")
                            act.activation(split[:, :, 0:P], xn[1][:, :, 0:P], ACT.Copy).then_inc(split_high, 1)
                            act.activation(pairs(slice(2 * P, 3 * P)),
                                           xn[1][:, :, P:D].unsqueeze(2).to_broadcast([P, NT, 2, D2]), ACT.Copy
                                           ).then_inc(split_high, 1)
                        elif (what, *at) == ("xt", 1):
                            for t in (0, 2):
                                act.activation(ffn_x[:, :, t * P:(t + 1) * P],
                                               empty("xt", 1, t)[:].rearrange("p (b n) -> p b n", b=4), ACT.Copy
                                               ).then_inc(a_free, 1)
                        elif what in ("xt", "att_t"):
                            k, = at
                            dst = xt[k] if what == "xt" else att_t
                            act.activation(dst[0:KH, 0, :], empty(what, k)[0:KH, 0:T], ACT.Copy
                                           ).then_inc(a_free, 1)
                        elif what == "low_rank":
                            act.activation(r_qk, empty("r_qk")[0:64 + RANK, 0:T], ACT.Copy).then_inc(a_free, 1)
                        elif what == "qk" and at[0] == 1:
                            act.activation(v1[:, at[1], :, 0:DH1],
                                           empty("v1", at[1])[:, 0:D].rearrange("p (h d) -> p h d", d=DH1),
                                           ACT.Copy).then_inc(a_free, 1)
                        elif what == "parts":
                            k, t = at
                            act.wait_ge(rope_ready[k], t + 1)
                            buffer_free(what, k, t)
                            for side in range(2):
                                high = part(k, t, side)[:, :, 0:2, :] if side == 0 else part(k, t, side)[:, :, 0:3:2, :]
                                act.activation(high, rotated(k, t, side).unsqueeze(2).to_broadcast(
                                    [P, HEADS[k], 2, DHS[k]]), ACT.Copy).then_inc(high_ready[k], 1)
                        elif what == "blocks":
                            k, t = at
                            for g in (0, 2):
                                act.activation(heads_t[k][:, 4 * g:4 * g + 4, t * P:(t + 1) * P],
                                               empty("blocks", k, t, g)[:].rearrange("p (b n) -> p b n", b=4),
                                               ACT.Copy).then_inc(a_free, 1)
                        elif what == "head":
                            k, hd = at
                            n = probs_of[k, hd]
                            if n >= PTH:
                                k_old, hd_old = head_order[n - PTH]
                                act.wait_ge(heads_done[k_old], hd_old + 1)
                            for kt in range(NT):
                                lo = kt * P if k == 1 else 0
                                act.activation(probs[:, n % PTH, kt, lo:T],
                                               empty("score", k, hd, kt)[:, lo:T], ACT.Exp,
                                               scale=DHS[k] ** -0.5).then_inc(a_free, 1)
                            if (hd + 1) % PER_BLOCK[k] == 0 and hd + 1 < HEADS[k]:
                                maxima_transposed(k, (hd + 1) // PER_BLOCK[k])
                            if hd and hd % PER_BLOCK[k] == 0:
                                group_summed(k, hd - 1)
                        elif what == "maxima" and at[1] == AHEAD[at[0]] - 1:
                            maxima_transposed(at[0], 0)
                        elif what == "last":
                            group_summed(at[0], HEADS[at[0]] - 1)
                        elif what == "tanh":
                            k, = at
                            act.wait_ge(dl_ready[k], 1)
                            act.activation(th[k][:], dl[k][:], ACT.Tanh, scale=0.5).then_inc(th_ready[k], 1)
                        elif what == "ffn":
                            e, m = at
                            if e:
                                act.wait_ge(v_free, V["up", e - 1, m] + 1)
                            act.activation(silu[:, m, :], empty("gate", e, m)[:, 0:T], ACT.Silu).then_inc(a_free, 1)

                @block.tensor
                def _(pe):
                    def fill_a(*what):
                        if A[what] >= NA:
                            pe.wait_ge(a_free, A[what] - NA + 1)
                        return bank_a[A[what] % NA]

                    def fill_v(*what):
                        if V[what] >= NV:
                            pe.wait_ge(v_free, V[what] - NV + 1)
                        return bank_v[V[what] % NV]

                    def emptied_a(*what):
                        pe.wait_ge(a_free, A[what] + 1)

                    def emptied_v(*what):
                        pe.wait_ge(v_free, V[what] + 1)

                    def two_halves(name, k, src, ready):
                        for half, (bank, full) in enumerate(((fill_a(name, k), a_full), (None, v_full))):
                            if half:
                                bank = fill_v(name, k)
                            for t in range(NT):
                                if ready is not None:
                                    pe.wait_ge(ready, t + 1)
                                mm = pe.transpose(bank[0:KH, t * P:(t + 1) * P],
                                                  src[:, t, half * KH:(half + 1) * KH], ident[:])
                            mm.then_inc(full, 1)

                    def halves_ready(name, k):
                        emptied_a(name, k)
                        emptied_v(name, k)

                    def project(dst, x, tokens, w, cols, bias):
                        pe.matmul(dst, x[0:KH + bias, 0, tokens], w[0:KH + bias, 0, cols], start=True, stop=False)
                        return pe.matmul(dst, x[0:KH, 1, tokens], w[0:KH, 1, cols], start=False, stop=True)

                    tile = [slice(t * P, (t + 1) * P) for t in range(NT)]

                    def rows_of(k, hd):
                        return hd * HEAD_ROWS[k] // P, hd * HEAD_ROWS[k] % P

                    def maxima(k, hd):
                        (b, r), dh = rows_of(k, hd), DHS[k]
                        if hd == 0:
                            emptied_a("blocks", k, NT - 1, 2)
                            emptied_v("blocks", k, NT - 1, 1)
                        for t in range(NT):
                            bank = fill_v("max", k, hd, t)
                            keys = (t + 1) * P if k == 1 else CTX if t < NT - 1 else T
                            mm = pe.matmul(bank[:, 0:keys], heads_t[k][r:r + dh, b, tile[t]],
                                           heads_t[k][r:r + dh, 6 + b, 0:keys], start=True,
                                           stop=(k == 0 and t < NT - 1))
                            if k == 1:
                                mm = pe.matmul(bank[:, tile[t]], identb[:], maskq[:], start=False, stop=True)
                            elif t == NT - 1:
                                mm = pe.matmul(bank[:, CTX:T], identb[:], maskl[:], start=False, stop=True)
                            mm.then_inc(v_full, 1)

                    def transpose_maxima(k, g):
                        emptied_v("max", k, (g + 1) * PER_BLOCK[k] - 1, NT - 1)
                        bank = fill_a("m_t", k, g)
                        for t in range(NT):
                            mm = pe.transpose(bank[0:PER_BLOCK[k], tile[t]],
                                              neg_max[k][:, t, g * PER_BLOCK[k]:(g + 1) * PER_BLOCK[k]], ident[:])
                        mm.then_inc(a_full, 1)

                    def scores(k, hd):
                        (b, r), dh = rows_of(k, hd), DHS[k]
                        g, i = divmod(hd, PER_BLOCK[k])
                        if i == 0:
                            emptied_a("m_t", k, g)
                        for t in range(NT):
                            bank = fill_a("score", k, hd, t)
                            lo = t * P if k == 1 else 0
                            pe.matmul(bank[:, lo:T], heads_t[k][r:r + 3 * dh, 6 + b, tile[t]],
                                      heads_t[k][r:r + 3 * dh, b, lo:T], start=True, stop=False)
                            mm = pe.matmul(bank[:, lo:T], pick[:, i, :], max_t[k][:, g % 2, lo:T],
                                           start=False, stop=(k == 0))
                            if k == 1:
                                mm = pe.matmul(bank[:, tile[t]], identb[:], maskt[:], start=False, stop=True)
                            mm.then_inc(a_full, 1)

                    def apply(k, hd):
                        emptied_a("score", k, hd, NT - 1)
                        if hd == 0 and k == 0:
                            pe.wait_ge(v0_ready, 1)
                        pr, v, rows = probs[:, probs_of[k, hd] % PTH], (v0, v1)[k], P // PER_BLOCK[k]
                        n = o_of[k, hd // PER_BLOCK[k]]
                        if hd % PER_BLOCK[k] == 0 and n >= 2:
                            pe.wait_ge(o_free, n - 1)
                        r = rows * (hd % PER_BLOCK[k])
                        o = bank_o[n % 2][r:r + rows]
                        last = NT - 1
                        if k == 1:
                            for kt in range(NT):
                                mm = pe.matmul(o[:, kt * P:T], v[:, kt, hd, :], pr[:, kt, kt * P:T],
                                               start=(kt == 0), stop=(kt == last))
                        else:
                            for kt in range(last):
                                pe.matmul(o[:, 0:T], v[:, kt, hd, :], pr[:, kt, :], start=(kt == 0), stop=False)
                            pe.matmul(o[:, 0:CTX], v[0:P - LAT, last, hd, :], pr[0:P - LAT, last, 0:CTX],
                                      start=False, stop=False)
                            mm = pe.matmul(o[:, CTX:T], v[:, last, hd, :], pr[:, last, CTX:T],
                                           start=False, stop=True)
                        mm.then_inc(heads_done[k], 1)

                    for what, *at in order:
                        if what == "patches":
                            pe.wait_ge(own_ready, 1)
                            for t in range(2):
                                pe.matmul(fill_v("patch", t)[:, 0:D], patches_t[:, t, :], own_proj[:],
                                          start=True, stop=True).then_inc(v_full, 1)
                        elif (what, *at) == ("xt", 1):
                            pe.wait_ge(split_low, 2)
                            for t, fill, full in ((0, fill_a, a_full), (1, fill_v, v_full), (2, fill_a, a_full)):
                                bank = fill("xt", 1, t)
                                for b in range(4):
                                    mm = pe.transpose(bank[:, b * P:(b + 1) * P].bitcast(F32R),
                                                      split[:, t, b * P:(b + 1) * P], identr[:])
                                mm.then_inc(full, 1)
                        elif what == "xt":
                            two_halves("xt", at[0], xn[at[0]], xn_ready[at[0]])
                        elif what == "qk":
                            k, t = at
                            if k == 0:
                                halves_ready("xt", 0)
                                project(fill_v("qk", 0, t)[:, 0:2 * D], xt[0], tile[t], w_qkv, slice(0, 2 * D), 0
                                        ).then_inc(v_full, 1)
                            else:
                                emptied_a("r_qk")
                                emptied_v("r_v")
                                pe.matmul(fill_v("qk", 1, t)[:, 0:2 * D], r_qk[:, tile[t]], w_b[:], start=True,
                                          stop=True).then_inc(v_full, 1)
                                pe.matmul(fill_a("v1", t)[:, 0:D], r_v[:, tile[t]], w_vb[:], start=True, stop=True
                                          ).then_inc(a_full, 1)
                        elif what == "blocks":
                            k, t = at
                            pe.wait_ge(low_ready[k], 2 * (t + 1))
                            sides = parts[parts_of["parts", k, t] % 2][:].rearrange("p s n -> p (s n)")
                            for g, fill, full in ((0, fill_a, a_full), (1, fill_v, v_full), (2, fill_a, a_full)):
                                bank = fill("blocks", k, t, g)
                                for b in range(4):
                                    mm = pe.transpose(bank[:, b * P:(b + 1) * P].bitcast(F32R),
                                                      sides[:, (4 * g + b) * P:(4 * g + b + 1) * P], identr[:])
                                mm.then_inc(full, 1)
                        elif what == "maxima":
                            maxima(*at)
                            if at[1] == AHEAD[at[0]] - 1:
                                transpose_maxima(at[0], 0)
                        elif what == "head":
                            k, hd = at
                            scores(k, hd)
                            if (hd + 1) % PER_BLOCK[k] == 0 and hd + 1 < HEADS[k]:
                                transpose_maxima(k, (hd + 1) // PER_BLOCK[k])
                            if hd + AHEAD[k] < HEADS[k]:
                                maxima(k, hd + AHEAD[k])
                            if hd:
                                apply(k, hd - 1)
                        elif what == "last":
                            apply(at[0], HEADS[at[0]] - 1)
                        elif what == "sums":
                            k, t = at
                            pe.wait_ge(o_free, o_of[k, HEADS[k] // PER_BLOCK[k] - 1] + 1)
                            bank = fill_v("sums", k, t)
                            for g in range(3):
                                mm = pe.transpose(bank[:, g * P:(g + 1) * P], sums_t[k][:, g, tile[t]], ident[:])
                            mm.then_inc(v_full, 1)
                        elif what == "att_t":
                            if at[0] == 0:
                                emptied_v("sums", 0, NT - 1)
                            two_halves("att_t", at[0], att[at[0]], None)
                        elif what == "out":
                            k, = at
                            halves_ready("att_t", k)
                            for t in range(NT):
                                bank = fill_v("out", k, t)
                                if k == 1:
                                    mm = project(bank[:, 0:D], att_t, tile[t], w_o1, slice(0, D), 0)
                                elif t < NT - 1:
                                    mm = project(bank[:, 0:D], att_t, tile[t], w_octx, slice(0, D), 1)
                                else:
                                    project(bank[0:P - LAT, 0:D], att_t, slice(t * P, CTX), w_octx, slice(0, D), 1)
                                    mm = project(bank[P - LAT:P, 0:D], att_t, slice(CTX, T), w_olat, slice(0, D), 1)
                                mm.then_inc(v_full, 1)
                        elif what == "logits":
                            k, = at
                            if k == 1:
                                halves_ready("xt", 3)
                            bank = fill_v("logits", k)
                            for t in range(NT):
                                o = bank[:, 8 * t:8 * t + 8]
                                if k == 1:
                                    mm = project(o, xt[3], tile[t], w_g1, slice(0, E1), 0)
                                    continue
                                for n, (xb, wb) in enumerate(products):
                                    mm = pe.matmul(o, ffn_x[:, xb, tile[t]], w_ffn[:, wb, router_cols],
                                                   start=(n == 0), stop=(n == len(products) - 1))
                            mm.then_inc(v_full, 1)
                        elif what == "ffn":
                            e, m = at
                            for name, fill, full in (("gate", fill_a, a_full), ("up", fill_v, v_full)):
                                bank = fill(name, e, m)
                                first = ffn_cols[name == "up"].start + e * I0 + m * P
                                for n, (xb, wb) in enumerate(products):
                                    mm = pe.matmul(bank[:, 0:T], w_ffn[:, wb, first:first + P], ffn_x[:, xb, :],
                                                   start=(n == 0), stop=(n == len(products) - 1))
                                mm.then_inc(full, 1)
                        elif what == "down":
                            e, = at
                            emptied_v("up", e, 1)
                            for t in range(NT):
                                bank = fill_v("down", e, t)
                                for m in range(2):
                                    mm = pe.matmul(bank[:, 0:D], hid[:, e % 2, m, tile[t]], w_down[:, m, e, :],
                                                   start=(m == 0), stop=(m == 1))
                                mm.then_inc(v_full, 1)
                        elif what == "low_rank":
                            halves_ready("xt", 2)
                            for w, bank, rows, full in ((w_a, fill_a("r_qk"), 64 + RANK, a_full),
                                                        (w_va, fill_v("r_v"), RANK, v_full)):
                                for half in range(2):
                                    mm = pe.matmul(bank[0:rows, 0:T], w[:, half, :], xt[2][0:KH, half, :],
                                                   start=(half == 0), stop=(half == 1))
                                mm.then_inc(full, 1)
                        elif what == "rank":
                            pe.wait_ge(oh_ready, 1)
                            bank = fill_v("rank")
                            for t in range(NT):
                                o = bank[:, 16 * t:16 * t + 16]
                                pe.matmul(o, before[:], ohb[:, t, :], start=True, stop=False)
                                for u in range(t):
                                    pe.matmul(o, onesb[:], ohb[:, u, :], start=False, stop=False)
                                mm = pe.matmul(o, onesb[:], seenb[:], start=False, stop=True)
                            mm.then_inc(v_full, 1)

                @block.vector
                def _(dve):
                    steps = 0

                    def step(ins):
                        nonlocal steps
                        steps += 1
                        ins.then_inc(dve_step, 1)

                    def done():
                        dve.wait_ge(dve_step, steps)

                    def full(*what):
                        dve.wait_ge(v_full, V[what] + 1)
                        return bank_v[V[what] % NV]

                    def written(*what):
                        dve.wait_ge(v_free, V[what] + 1)

                    def statistics(k):
                        src = h[STREAM_OF_NORM[k]]
                        for t in range(NT):
                            step(dve.bn_stats(st6[k][:, t, :], src[:, t, :]))
                        done()
                        for t in range(NT):
                            step(dve.bn_aggr(mv[k][:, t, :], st6[k][:, t, :]))
                        done()
                        dve.tensor_scalar(ve[k][:], mv[k][:, :, 1], EPS, None, ALU.add).then_inc(var_ready[k], 1)

                    def rope_products(k, t):
                        dh = DHS[k]
                        g, half = 2 * D // dh, dh // 2
                        x = full("qk", k, t)[:, 0:2 * D].rearrange("p (g d) -> p g d", d=dh)
                        cos = c(f"cos{k}", dh)[:, t, :].unsqueeze(1)
                        sin = c(f"sin{k}", dh)[:, t, :].unsqueeze(1)
                        a = rope_a[:, t, :].rearrange("p (g d) -> p g d", d=dh)
                        b = rope_b[:, t, :].rearrange("p (g d) -> p g d", d=dh)
                        if k == 1 and "x" in streams:
                            dve.wait_ge(low_ready[0], 2 * (t + 1))
                            dve.wait_ge(vcen_ready, NT)
                        step(dve.tensor_tensor(a, x, cos.to_broadcast([P, g, dh]), ALU.mult))
                        step(dve.tensor_tensor(b[:, :, 0:half], x[:, :, half:dh],
                                               sin[:, :, 0:half].to_broadcast([P, g, half]), ALU.mult))
                        done()
                        dve.tensor_tensor(b[:, :, half:dh], x[:, :, 0:half],
                                          sin[:, :, half:dh].to_broadcast([P, g, half]), ALU.mult
                                          ).then_inc(v_free, 1)

                    def values(n):
                        keys = rope_a[:, :, D:2 * D].rearrange("p t (h d) -> p t h d", d=DH0)
                        tiled = vsum[:].rearrange("p (t h) -> p t h", h=H0)
                        vv = v0[:].rearrange("p t h d -> p (t h) d")[:, :, 0:DH0]
                        if n == 0:
                            dve.wait_ge(rope_ready[0], NT)
                            step(dve.tensor_reduce(tiled, keys, AX.X, ALU.add))
                            done()
                            for t in range(NT):
                                dve.scalar_tensor_tensor(
                                    vcen[:, t * H0:(t + 1) * H0, :],
                                    vsum[:, t * H0:(t + 1) * H0].unsqueeze(2).to_broadcast([P, H0, DH0]), -1.0 / DH0,
                                    keys[:, t], ALU.mult, ALU.add).then_inc(vcen_ready, 1)
                        elif n == 1:
                            dve.wait_ge(vsq_ready, 1)
                            step(dve.tensor_reduce(vms[:], vsq, AX.X, ALU.add))
                            done()
                            dve.tensor_scalar(vvar[:], vms[:], 1.0 / DH0, EPS, ALU.mult, ALU.add
                                              ).then_inc(vvar_ready, 1)
                        else:
                            dve.wait_ge(vrstd_ready, 1)
                            step(dve.tensor_tensor(
                                vv, vcen, vrstd[:].unsqueeze(2).to_broadcast([P, NT * H0, DH0]), ALU.mult))
                            done()
                            step(dve.tensor_tensor(
                                vv, vv, lng[:].unsqueeze(1).to_broadcast([P, NT * H0, DH0]), ALU.mult))
                            done()
                            dve.tensor_tensor(vv, vv, lnb[:].unsqueeze(1).to_broadcast([P, NT * H0, DH0]), ALU.add
                                              ).then_inc(v0_ready, 1)

                    def maxima(k, hd):
                        for t in range(NT):
                            bank = full("max", k, hd, t)
                            to = neg_max[k][:, t, hd:hd + 1]
                            keys = (t + 1) * P if k == 1 else CTX if t < NT - 1 else T
                            dve.tensor_reduce(to, bank[:, 0:keys], AX.X, ALU.max, negate=True).then_inc(v_free, 1)

                    def attention_out(k, t):
                        heads, dh = HEADS[k], DHS[k]
                        sums = full("sums", k, t)[:, 0:3 * P].rearrange("p (h d) -> p h d", h=heads)
                        step(dve.reciprocal(rsum[k][:, t, 0:heads], sums[:, :, dh]))
                        done()
                        dve.tensor_tensor(att[k][:, t, :].rearrange("p (h d) -> p h d", d=dh), sums[:, :, 0:dh],
                                          rsum[k][:, t, 0:heads].unsqueeze(2).to_broadcast([P, heads, dh]),
                                          ALU.mult).then_inc(v_free, 1)

                    def largest(k, experts):
                        got = full("logits", k)[:, 0:8 * NT].rearrange("p (t e) -> p t e", e=8)[:, :, 0:experts]
                        if k == 0:
                            dve.tensor_tensor(lg[k][:, :, 0:experts], got,
                                              router_bias[:].unsqueeze(1).to_broadcast([P, NT, E0]), ALU.add
                                              ).then_inc(v_free, 1)
                        else:
                            dve.tensor_copy(lg[k][:, :, 0:experts], got).then_inc(v_free, 1)
                        written("logits", k)
                        for t in range(NT):
                            step(dve.max(top[k][:, t, :], lg[k][:, t, :]))
                        done()
                        dve.tensor_tensor(dl[k][:], top[k][:, :, 1], top[k][:, :, 0], ALU.subtract
                                          ).then_inc(dl_ready[k], 1)
                        for t in range(NT):
                            step(dve.max_index(topi[k][:, t, :], top[k][:, t, :], lg[k][:, t, :]))
                        done()
                        step(dve.tensor_copy(topf[k][:], topi[k][:, :, 0:2]))
                        done()
                        step(dve.tensor_tensor(
                            oh[k][:].rearrange("p t k e -> p (t k) e"),
                            c("iota").unsqueeze(1).to_broadcast([P, 2 * NT, 8]),
                            topf[k][:].rearrange("p t k -> p (t k)").unsqueeze(2).to_broadcast([P, 2 * NT, 8]),
                            ALU.is_equal))

                    def softmax_of_two(k):
                        dve.wait_ge(th_ready[k], 1)
                        step(dve.tensor_scalar(wk[k][:, :, 0], th[k][:], -0.5, 0.5, ALU.mult, ALU.add))
                        step(dve.tensor_scalar(wk[k][:, :, 1], th[k][:], 0.5, 0.5, ALU.mult, ALU.add))
                        done()

                    def count_choices():
                        step(dve.tensor_copy(seenb[:], seen[:]))
                        done()
                        dve.tensor_copy(ohb[:], oh[1][:].rearrange("p t k e -> p t (k e)")).then_inc(oh_ready, 1)
                        for t in range(NT):
                            done()
                            step(dve.tensor_tensor(seen[:], seen[:], oh[1][:, t].rearrange("p k e -> p (k e)"),
                                                   ALU.add))
                        step(dve.tensor_tensor(
                            ohbase[:].rearrange("p t k e -> p t (k e)"), oh[1][:].rearrange("p t k e -> p t (k e)"),
                            c("base").unsqueeze(1).to_broadcast([P, NT, 16]), ALU.mult))
                        done()
                        step(dve.tensor_reduce(bases[:], ohbase[:], AX.X, ALU.add))

                    def places():
                        written("rank")
                        step(dve.tensor_reduce(rank[:], ohw[1][:], AX.X, ALU.add))
                        done()
                        step(dve.tensor_scalar(keep[:], rank[:], float(CAP), None, ALU.is_lt))
                        step(dve.tensor_tensor(place[:], rank[:], bases[:], ALU.add))
                        done()
                        step(dve.tensor_tensor(off[:], place[:], drop[:], ALU.subtract))
                        step(dve.tensor_tensor(kept[:], place[:], keep[:], ALU.mult))
                        step(dve.tensor_tensor(weights_all[:, one(image_z, 2 * NT)],
                                               wk[1][:].rearrange("p t k -> p (t k)"),
                                               keep[:].rearrange("p t k -> p (t k)"), ALU.mult))
                        done()
                        step(dve.tensor_copy(slots_all[:, one(image_z, 2 * NT)],
                                             kept[:].rearrange("p t k -> p (t k)")))
                        step(dve.tensor_tensor(place[:], off[:], keep[:], ALU.mult))
                        done()
                        dve.tensor_tensor(slot_i[:].rearrange("p (t k) -> p t k", k=2), place[:], drop[:], ALU.add
                                          ).then_inc(slot_ready, 1)
                        dve.wait_ge(slot_ready, 1)
                        step(dve.tensor_scalar(drop[:], drop[:], float(T), None, ALU.add))

                    for what, *at in order:
                        if what == "patches":
                            if "y" in streams:
                                dve.wait_ge(carried[1], 1)
                            for t in range(2):
                                dve.tensor_copy(h[0][:, t, :], full("patch", t)[:, 0:D]).then_inc(v_free, 1)
                        elif what == "stats":
                            if at[0] == 0:
                                written("patch", 1)
                                dve.wait_ge(emb_ready, 1)
                            elif at[0] == 2:
                                written("down", E0 - 1, NT - 1)
                            else:
                                written("out", at[0] // 2, NT - 1)
                            statistics(*at)
                        elif what == "xn":
                            k, = at
                            dve.wait_ge(rstd_ready[k], 1)
                            for t in range(NT):
                                dve.tensor_scalar(xn[k][:, t, :], h[STREAM_OF_NORM[k]][:, t, :], mv[k][:, t, 0:1],
                                                  rstd[k][:, t:t + 1], ALU.subtract, ALU.mult
                                                  ).then_inc(xn_ready[k], 1)
                        elif (what, *at) == ("xt", 1):
                            dve.tensor_copy(ffn_x[:, :, P:2 * P],
                                            full("xt", 1, 1)[:].rearrange("p (b n) -> p b n", b=4)
                                            ).then_inc(v_free, 1)
                        elif what in ("xt", "att_t"):
                            k, = at
                            dst = xt[k] if what == "xt" else att_t
                            dve.tensor_copy(dst[0:KH, 1, :], full(what, k)[0:KH, 0:T]).then_inc(v_free, 1)
                        elif what == "qk":
                            rope_products(*at)
                        elif what == "blocks":
                            k, t = at
                            dve.tensor_copy(heads_t[k][:, 4:8, t * P:(t + 1) * P],
                                            full("blocks", k, t, 1)[:].rearrange("p (b n) -> p b n", b=4)
                                            ).then_inc(v_free, 1)
                        elif what == "values":
                            values(*at)
                        elif what == "maxima":
                            maxima(*at)
                        elif what == "head":
                            k, hd = at
                            if hd + AHEAD[k] < HEADS[k]:
                                maxima(k, hd + AHEAD[k])
                        elif what == "sums":
                            attention_out(*at)
                        elif what == "out":
                            k, = at
                            s = (0, 2)[k]
                            if k == 1:
                                dve.wait_ge(carried[2], 1)
                            for t in range(NT):
                                dve.tensor_tensor(h[s][:, t, :], full("out", k, t)[:, 0:D], h[s][:, t, :], ALU.add
                                                  ).then_inc(v_free, 1)
                        elif what == "logits":
                            largest(at[0], (E0, E1)[at[0]])
                        elif what == "weights":
                            softmax_of_two(*at)
                            if at[0] == 0:
                                step(dve.tensor_tensor(ohw[0][:], oh[0][:],
                                                       wk[0][:].unsqueeze(3).to_broadcast([P, NT, 2, 8]), ALU.mult))
                                done()
                                step(dve.tensor_tensor(comb[:], ohw[0][:, :, 0, :], ohw[0][:, :, 1, :], ALU.add))
                            else:
                                count_choices()
                        elif what == "ffn":
                            e, m = at
                            bank = full("up", e, m)
                            dve.wait_ge(a_free, A["gate", e, m] + 1)
                            dve.tensor_tensor(hid[:, e % 2, m, :], bank[:, 0:T], silu[:, m, :], ALU.mult
                                              ).then_inc(v_free, 1)
                        elif what == "low_rank":
                            dve.tensor_copy(r_v, full("r_v")[0:RANK, 0:T]).then_inc(v_free, 1)
                        elif what == "down":
                            e, = at
                            if e == 0:
                                dve.wait_ge(carried[1], 1)
                                done()
                            for t in range(NT):
                                if e:
                                    written("down", e - 1, t)
                                dve.scalar_tensor_tensor(h[1][:, t, :], full("down", e, t)[:, 0:D],
                                                         comb[:, t, e:e + 1], h[1][:, t, :], ALU.mult, ALU.add
                                                         ).then_inc(v_free, 1)
                        elif what == "rank":
                            bank = full("rank")
                            dve.tensor_tensor(ohw[1][:].rearrange("p t k e -> p (t k e)"), bank[:, 0:16 * NT],
                                              oh[1][:].rearrange("p t k e -> p (t k e)"), ALU.mult
                                              ).then_inc(v_free, 1)
                        elif what == "places":
                            places()
                    done()
            nc.all_engine_barrier(sems_to_clear=per_body)

        body("x", 0, None, None)
        body("xy", 1, 0, None)
        with nc.Fori(0, B - 2) as image:
            body("xyz", image + 2, image + 1, image)
        body("yz", None, B - 1, B - 2)
        body("z", None, None, B - 1)


def expert_stage(nc, w1, w2, xs_dram, y_dram, ident):
    NX = 3
    NM = HF // P
    LOWER = slice(D2, P)
    with ExitStack() as ctx:
        def sb(name, shape, dt=F32):
            return ctx.enter_context(nc.sbuf_tensor(name, shape, dt))

        def sem(name):
            return ctx.enter_context(nc.semaphore(name))

        raw = sb("raw", [P, 2, 2 * HF])
        w_in = [sb(f"w_in{i}", [P, 3, 2 * HF], F32R) for i in range(2)]
        w_out = [sb(f"w_out{i}", [P, NM, D]) for i in range(2)]
        e_identr = sb("e_identr", [P, P], F32R)
        e_zeros = sb("e_zeros", [P, NT, D2])
        rows = sb("rows", [P, NX, NT, D])
        split = [sb(f"split{i}", [P, NT, 4 * P], F32R) for i in range(2)]
        split_t = [sb(f"split_t{i}", [P, 4, T], F32R) for i in range(2)]
        gated = sb("gated", [P, 2, T])
        hid = sb("e_hid", [P, 2, NM, T])
        res = sb("res", [P, 2, NT, D])
        bank_a = [ctx.enter_context(nc.psum_tensor(f"e_bank_a{i}", [P, 512], F32)) for i in range(4)]
        bank_v = [ctx.enter_context(nc.psum_tensor(f"e_bank_v{i}", [P, 512], F32)) for i in range(4)]

        stored = [sem(f"stored{i}") for i in range(2)]
        w_loaded = sem("w_loaded")
        rounded, rests = sem("rounded"), sem("rests")
        rows_in = [sem(f"rows_in{i}") for i in range(NX)]
        rows_high, rows_split = sem("rows_high"), sem("rows_split")
        ea_full, ea_free, ev_full, ev_free = sem("ea_full"), sem("ea_free"), sem("ev_full"), sem("ev_free")
        set_up = sem("set_up")
        per_body = range(w_loaded.num, set_up.num + 1)

        CH = 2 * NCHUNK
        READY = (1, NCHUNK + 1)
        a, v = [("x", 0, 0)], [("x", 0, 1), ("x", 0, 2)]
        for ch in range(CH):
            a += [("b", ch, m) for m in range(NM)]
            v += [("a", ch, m) for m in range(NM)]
            if ch + 1 < CH:
                a.append(("x", ch + 1, 0))
                v += [("x", ch + 1, 1), ("x", ch + 1, 2)]
            a += [("y", ch, t) for t in range(NT)]
        ea = {what: n for n, what in enumerate(a)}
        ev = {what: n for n, what in enumerate(v)}

        def load_weights(sp, i, e):
            sp.dma_start(raw[:, 0, :].unsqueeze(1), w1[:, 0:P, :].rearrange("e p n -> p e n")[:, e]
                         ).then_inc(w_loaded, 16)
            for half in (slice(0, D2), LOWER):
                sp.dma_start(raw[half, 1, :].unsqueeze(1), w1[:, P:D, :].rearrange("e p n -> p e n")[:, e]
                             ).then_inc(w_loaded, 16)
            sp.dma_start(w_out[i][:].unsqueeze(1), w2.rearrange("e (k p) n -> p e k n", p=P)[:, e]
                         ).then_inc(w_loaded, 16)

        def split_weights(dve, i, n):
            dve.tensor_copy(w_in[i][:, 0, :], raw[:, 0, :]).then_inc(rounded, 1)
            dve.tensor_copy(w_in[i][:, 2, :], raw[:, 1, :]).then_inc(rounded, 1)
            dve.wait_ge(rounded, 2 * (n + 1))
            dve.tensor_tensor(w_in[i][LOWER, 2, :], raw[LOWER, 1, :], w_in[i][LOWER, 2, :].bitcast(F32),
                              ALU.subtract).then_inc(rests, 1)

        def take_rests(pool, i, n):
            pool.wait_ge(rounded, 2 * n + 1)
            pool.tensor_tensor(w_in[i][:, 1, :], raw[:, 0, :], w_in[i][:, 0, :].bitcast(F32), ALU.subtract
                               ).then_inc(rests, 1)

        with nc.Block() as block:
            @block.sync
            def _(sp):
                load_weights(sp, 0, slice(0, 1))

            @block.vector
            def _(dve):
                dve.memset(e_zeros[:], 0.0).then_inc(set_up, 1)
                dve.tensor_copy(e_identr[:], ident[:]).then_inc(set_up, 1)
                dve.wait_ge(set_up, 2)
                for i in range(2):
                    dve.tensor_copy(split[i][:, :, 4 * P - D2:4 * P], e_zeros[:]).then_inc(set_up, 1)
                dve.wait_ge(w_loaded, 64)
                split_weights(dve, 0, 0)
                dve.wait_ge(set_up, 4)

            @block.gpsimd
            def _(pool):
                take_rests(pool, 0, 0)
                pool.wait_ge(rests, 2)
        nc.all_engine_barrier(sems_to_clear=per_body)

        def body(pair, last):
            loads = [slice(2 * pair + 1, 2 * pair + 2) if last else bass.ds(pair * 2 + 1, 1)]
            if not last:
                loads.append(bass.ds(pair * 2 + 2, 1))
            with nc.Block(no_gpsimd_drain=True) as block:

                @block.sync
                def _(sp):
                    xs = xs_dram[0:NROWS, :].rearrange("(j c t p) d -> p j c t d", j=E1 // 2, c=CH, p=P)
                    for ch in range(CH):
                        if ch >= NX:
                            sp.wait_ge(rows_split, 2 * (ch - NX + 1))
                        for t in range(NT):
                            sp.dma_start(rows[:, ch % NX, t, :].unsqueeze(1),
                                         xs[:, slice(pair, pair + 1) if last else bass.ds(pair, 1), ch, t]
                                         ).then_inc(rows_in[ch % NX], 16)
                        if ch == 1:
                            load_weights(sp, 1, loads[0])
                        if ch == READY[1] and not last:
                            sp.wait_ge(rests, 2)
                            sp.wait_ge(ea_full, ea["y", NCHUNK - 1, NT - 1] + 1)
                            load_weights(sp, 0, loads[1])

                @block.gpsimd
                def _(pool):
                    ys = y_dram.rearrange("(j c t p) d -> p j c t d", j=E1 // 2, c=CH, p=P)

                    def rest_of_rows(ch):
                        pool.wait_ge(rows_high, 2 * (ch + 1))
                        x, s = rows[:, ch % NX], split[ch % 2]
                        pool.tensor_tensor(s[:, :, P:2 * P], x[:, :, 0:P], s[:, :, 0:P].bitcast(F32), ALU.subtract
                                           ).then_inc(rows_split, 1)
                        pool.tensor_tensor(s[:, :, 3 * P:3 * P + D2], x[:, :, P:D],
                                           s[:, :, 2 * P:2 * P + D2].bitcast(F32), ALU.subtract
                                           ).then_inc(rows_split, 1)

                    rest_of_rows(0)
                    for ch in range(CH):
                        if ch + 1 < CH:
                            rest_of_rows(ch + 1)
                        for n in range(len(loads)):
                            if ch == min(READY[n] + 1, CH - 1):
                                take_rests(pool, 1 - n, n)
                        pool.wait_ge(ea_free, ea["y", ch, NT - 1] + 1)
                        pool.dma_start(ys[:, slice(pair, pair + 1) if last else bass.ds(pair, 1), ch],
                                       res[:, ch % 2].unsqueeze(1)).then_inc(stored[ch % 2], 16)
                    pool.wait_ge(rests, 2 * len(loads))
                    for i in range(2):
                        pool.wait_ge(stored[i], (pair + 1) * (16 * NCHUNK))

                @block.tensor
                def _(pe):
                    def fill_a(*what):
                        if ea[what] >= 4:
                            pe.wait_ge(ea_free, ea[what] - 4 + 1)
                        return bank_a[ea[what] % 4]

                    def fill_v(*what):
                        if ev[what] >= 4:
                            pe.wait_ge(ev_free, ev[what] - 4 + 1)
                        return bank_v[ev[what] % 4]

                    def down(ch):
                        pe.wait_ge(ev_free, ev["a", ch, NM - 1] + 1)
                        for t in range(NT):
                            bank = fill_a("y", ch, t)
                            for m in range(NM):
                                mm = pe.matmul(bank[:, 0:D], hid[:, ch % 2, m, t * P:(t + 1) * P],
                                               w_out[ch // NCHUNK][:, m, :], start=(m == 0), stop=(m == NM - 1))
                            mm.then_inc(ea_full, 1)

                    def transpose_rows(ch):
                        pe.wait_ge(rows_split, 2 * (ch + 1))
                        for t, fill, full in ((0, fill_a, ea_full), (1, fill_v, ev_full), (2, fill_v, ev_full)):
                            bank = fill("x", ch, t)
                            for b in range(4):
                                mm = pe.transpose(bank[:, b * P:(b + 1) * P].bitcast(F32R),
                                                  split[ch % 2][:, t, b * P:(b + 1) * P], e_identr[:])
                            mm.then_inc(full, 1)

                    transpose_rows(0)
                    for ch in range(CH):
                        w, x = w_in[ch // NCHUNK], split_t[ch % 2]
                        pe.wait_ge(ea_free, ea["x", ch, 0] + 1)
                        pe.wait_ge(ev_free, ev["x", ch, 2] + 1)
                        if ch == NCHUNK:
                            pe.wait_ge(rests, 2)
                            pe.wait_ge(w_loaded, 64)
                        for m in range(NM):
                            for at, bank, full in ((HF + m * P, fill_a("b", ch, m), ea_full), (m * P, None, ev_full)):
                                if bank is None:
                                    bank = fill_v("a", ch, m)
                                for n, (xb, wb) in enumerate(((0, 0), (1, 0), (0, 1), (2, 2), (3, 2))):
                                    mm = pe.matmul(bank[:, 0:T], w[:, wb, at:at + P], x[:, xb, :],
                                                   start=(n == 0), stop=(n == 4))
                                mm.then_inc(full, 1)
                        if ch + 1 < CH:
                            transpose_rows(ch + 1)
                        down(ch)

                @block.scalar
                def _(act):
                    def full(*what):
                        act.wait_ge(ea_full, ea[what] + 1)
                        return bank_a[ea[what] % 4]

                    def results(ch):
                        if ch >= 2:
                            act.wait_ge(stored[ch % 2], pair * (16 * NCHUNK) + 16 * (ch // 2))
                        for t in range(NT):
                            act.activation(res[:, ch % 2, t, :], full("y", ch, t)[:, 0:D], ACT.Copy
                                           ).then_inc(ea_free, 1)

                    def round_rows(ch):
                        act.wait_ge(rows_in[ch % NX], 16 * NT * (ch // NX + 1))
                        if ch >= 2:
                            act.wait_ge(ev_full, ev["x", ch - 2, 2] + 1)
                        x, s = rows[:, ch % NX], split[ch % 2]
                        act.activation(s[:, :, 0:P], x[:, :, 0:P], ACT.Copy).then_inc(rows_high, 1)
                        act.activation(s[:, :, 2 * P:3 * P].rearrange("p t (a d) -> p t a d", a=2),
                                       x[:, :, P:D].unsqueeze(2).to_broadcast([P, NT, 2, D2]), ACT.Copy
                                       ).then_inc(rows_high, 1)

                    def tile_transposed(ch):
                        act.activation(split_t[ch % 2][:, :, 0:P],
                                       full("x", ch, 0)[:].rearrange("p (b n) -> p b n", b=4), ACT.Copy
                                       ).then_inc(ea_free, 1)

                    round_rows(0)
                    round_rows(1)
                    tile_transposed(0)
                    for ch in range(CH):
                        for m in range(NM):
                            if m >= 2:
                                act.wait_ge(ev_free, ev["a", ch, m - 2] + 1)
                            elif ch:
                                act.wait_ge(ev_free, ev["a", ch - 1, m + NM - 2] + 1)
                            act.activation(gated[:, m % 2, :], full("b", ch, m)[:, 0:T], ACT.Silu
                                           ).then_inc(ea_free, 1)
                        if ch + 1 < CH:
                            tile_transposed(ch + 1)
                        if ch + 2 < CH:
                            round_rows(ch + 2)
                        results(ch)

                @block.vector
                def _(dve):
                    def full(*what):
                        dve.wait_ge(ev_full, ev[what] + 1)
                        return bank_v[ev[what] % 4]

                    def tiles_transposed(ch):
                        for t in (1, 2):
                            dve.tensor_copy(split_t[ch % 2][:, :, t * P:(t + 1) * P],
                                            full("x", ch, t)[:].rearrange("p (b n) -> p b n", b=4)
                                            ).then_inc(ev_free, 1)

                    tiles_transposed(0)
                    for ch in range(CH):
                        for m in range(NM):
                            bank = full("a", ch, m)
                            dve.wait_ge(ea_free, ea["b", ch, m] + 1)
                            dve.tensor_tensor(hid[:, ch % 2, m, :], bank[:, 0:T], gated[:, m % 2, :], ALU.mult
                                              ).then_inc(ev_free, 1)
                        if ch + 1 < CH:
                            tiles_transposed(ch + 1)
                        for n in range(len(loads)):
                            if ch == READY[n]:
                                dve.wait_ge(w_loaded, 64 * (n + 1))
                                split_weights(dve, 1 - n, n)
            nc.all_engine_barrier(sems_to_clear=per_body)

        with nc.Fori(0, E1 // 2 - 1) as pair:
            body(pair, False)
        body(E1 // 2 - 1, True)


def combine_stage(nc, y_dram, h_dram, out, slots_all, weights_all):
    TI = CIMG * NT
    with ExitStack() as ctx:
        def sb(name, shape, dt=F32):
            return ctx.enter_context(nc.sbuf_tensor(name, shape, dt))

        def sem(name):
            return ctx.enter_context(nc.semaphore(name))

        idx = sb("c_idx", [P, 2 * TI], I32)
        wts = sb("c_wts", [P, 2 * TI])
        hrow = sb("hrow", [P, TI, D])
        y = sb("y", [P, TI, 2, D])
        part = sb("part", [P, TI, D])
        y_in = [sem(f"y_in{t}") for t in range(TI)]
        idx_copied, wts_copied, h_in = sem("idx_copied"), sem("wts_copied"), sem("h_in")
        first_added, both_added, out_stored = sem("first_added"), sem("both_added"), sem("out_stored")
        per_step = range(idx_copied.num, out_stored.num + 1)
        tiles = lambda ap: ap.rearrange("(s t p) d -> p s t d", t=TI, p=P)

        with nc.Fori(0, B // CIMG) as group:
            with nc.Block(no_gpsimd_drain=True) as block:

                @block.gpsimd
                def _(pool):
                    pool.tensor_copy(idx[:], slots_all[:, bass.ds(group * (2 * TI), 2 * TI)]).then_inc(idx_copied, 1)
                    pool.wait_ge(idx_copied, 1)
                    for t in range(TI):
                        for k in range(2):
                            pool.indirect_dma_start(
                                y[:, t, k, :], None, y_dram,
                                bass.IndirectOffsetOnAxis(ap=idx[:, 2 * t + k:2 * t + k + 1], axis=0)
                            ).then_inc(y_in[t], 16)

                @block.sync
                def _(sp):
                    sp.dma_start(hrow[:].unsqueeze(1), tiles(h_dram)[:, bass.ds(group, 1)]).then_inc(h_in, 16)
                    sp.wait_ge(both_added, TI)
                    sp.dma_start(tiles(out)[:, bass.ds(group, 1)], hrow[:].unsqueeze(1)).then_inc(out_stored, 16)
                    sp.wait_ge(out_stored, 16)

                @block.vector
                def _(dve):
                    dve.tensor_copy(wts[:], weights_all[:, bass.ds(group * (2 * TI), 2 * TI)]
                                    ).then_inc(wts_copied, 1)
                    dve.wait_ge(wts_copied, 1)
                    dve.wait_ge(h_in, 16)
                    for t in range(TI):
                        dve.wait_ge(y_in[t], (group + 1) * 32)
                        dve.scalar_tensor_tensor(part[:, t, :], y[:, t, 0, :], wts[:, 2 * t:2 * t + 1], hrow[:, t, :],
                                                 ALU.mult, ALU.add).then_inc(first_added, 1)
                        dve.wait_ge(first_added, t + 1)
                        dve.scalar_tensor_tensor(hrow[:, t, :], y[:, t, 1, :], wts[:, 2 * t + 1:2 * t + 2],
                                                 part[:, t, :], ALU.mult, ALU.add).then_inc(both_added, 1)
            nc.all_engine_barrier(sems_to_clear=per_step)


def kernel(x, x_txt, mask_BS_i2_0, L0_tok_curve, L0_tok_proj_w, L0_tok_proj_b, L0_txt_token_table,
           L0_txt_segm_table, L0_attn_Wq, L0_attn_Wkv, L0_attn_Wo_ctx, L0_attn_bo_ctx, L0_attn_Wo_lat,
           L0_attn_bo_lat, L0_attn_ln_g, L0_attn_ln_b, L0_ffn_router_w, L0_ffn_router_b, L0_ffn_gate_w,
           L0_ffn_up_w, L0_ffn_down_w, L1_attn_qA, L1_attn_qB, L1_attn_kA, L1_attn_kB, L1_attn_vA,
           L1_attn_vB, L1_attn_o_w, L1_ffn_Wg, L1_ffn_W1, L1_ffn_W2):
    import numpy as np
    import concourse.bacc as bacc
    from concourse.bass_utils import run_bass_kernel_spmd

    a = np.asarray
    arrays = {
        "consts": constants(),
        "img": a(x).transpose(2, 3, 1, 0).reshape(IMG * IMG, 3 * B),
        "txt": a(x_txt).T, "seg": a(mask_BS_i2_0).T, "curve": a(L0_tok_curve),
        "projw": a(L0_tok_proj_w).T, "projb": a(L0_tok_proj_b),
        "tok_table": a(L0_txt_token_table), "seg_table": a(L0_txt_segm_table),
        "wqkv": np.concatenate([a(L0_attn_Wq), a(L0_attn_Wkv)], axis=1),
        "wo_ctx": a(L0_attn_Wo_ctx), "bo_ctx": a(L0_attn_bo_ctx),
        "wo_lat": a(L0_attn_Wo_lat), "bo_lat": a(L0_attn_bo_lat),
        "ln_g": a(L0_attn_ln_g), "ln_b": a(L0_attn_ln_b),
        "router_w": a(L0_ffn_router_w).T, "router_b": a(L0_ffn_router_b),
        "gate_w": a(L0_ffn_gate_w), "up_w": a(L0_ffn_up_w), "down_w": a(L0_ffn_down_w),
        "qa": a(L1_attn_qA), "qb": a(L1_attn_qB), "ka": a(L1_attn_kA), "kb": a(L1_attn_kB),
        "va": a(L1_attn_vA), "vb": a(L1_attn_vB), "ow": a(L1_attn_o_w),
        "wg": a(L1_ffn_Wg), "w1": a(L1_ffn_W1), "w2": a(L1_ffn_W2),
    }
    arrays = {name: np.ascontiguousarray(value) for name, value in arrays.items()}
    nc = bacc.Bacc("TRN2", target_bir_lowering=False, num_devices=1)
    args = [nc.dram_tensor(f"in_{name}", value.shape, mybir.dt.from_np(value.dtype), kind="ExternalInput").ap()
            for name, value in arrays.items()]
    out = nc.dram_tensor("out_tokens", (N, D), F32, kind="ExternalOutput").ap()
    early_fusion_kernel(nc, *args, out)
    got = run_bass_kernel_spmd(nc, [{f"in_{name}": value for name, value in arrays.items()}], core_ids=[0])
    return np.asarray(got.results[0]["out_tokens"]).reshape(B, T, D)
```
